# Optimizing a Trainium2 kernel written in Bass

```python
import numpy as np
import jax
import jax.numpy as jnp

def _softmax(x, axis=-1):
    return jax.nn.softmax(x, axis=axis)

def _gelu(x):
    return jax.nn.gelu(x, approximate=True)

def _silu(x):
    return jax.nn.silu(x)

def _sigmoid(x):
    return jax.nn.sigmoid(x)

def _layernorm(x, axis=-1, eps=1e-05):
    m = jnp.mean(x, axis=axis, keepdims=True)
    v = jnp.var(x, axis=axis, keepdims=True)
    return (x - m) / jnp.sqrt(v + eps)

def _scatter_add(tgt, idx, src, axis=0):
    return tgt.at[idx].add(src)

def _segment_sum(src, seg, n):
    return jax.ops.segment_sum(src, seg, n)
kernel_name = 'mk_gnn_resnorm_d4_gnn_r32_dddd61'

def setup_inputs(seed: int=0):
    np.random.seed(seed)
    _w = jnp.asarray

    def _rec_inputs():
        import jax
        import jax.numpy as jnp
        _gk = jax.random.key(seed)
        x = -0.0002117 + 1 * jax.random.normal(jax.random.fold_in(_gk, 1), (3125, 256), jnp.float32)
        src = jax.random.randint(jax.random.fold_in(_gk, 2), (50000,), 0, 3125, jnp.int32)
        dst = jnp.minimum((3125 * jax.random.uniform(jax.random.fold_in(_gk, 3), (50000,)) ** 2.0).astype(jnp.int32), 99999)
        _o = jnp.argsort(dst, stable=True)
        src = src[_o]
        dst = dst[_o]
        edge_attr_3 = -1.09012e-05 + 0.99985 * jax.random.normal(jax.random.fold_in(_gk, 12), (50000, 3), jnp.float32)
        edge_weight = jax.random.uniform(jax.random.fold_in(_gk, 14), (50000,), jnp.float32, 0.0, 1)
        return (x, src, dst, edge_attr_3, edge_weight)
    x, src, dst, edge_attr_3, edge_weight = _rec_inputs()

    def _L0_gnn_setup():
        import jax, jax.numpy as jnp
        import numpy as np
        N_NODES = 3125
        N_EDGES = 100000
        D_IN = 256
        D_OUT = 256
        key = jax.random.key(seed)
        k1, k2, k3, k4, k5, k6 = jax.random.split(key, 6)
        x = jax.random.normal(k1, (N_NODES, D_IN), dtype=jnp.float32)
        edge_row = jax.random.randint(k2, (N_EDGES,), 0, N_NODES, dtype=jnp.int32)
        edge_col = jax.random.randint(k3, (N_EDGES,), 0, N_NODES, dtype=jnp.int32)
        edge_val = jax.random.uniform(k4, (N_EDGES,), dtype=jnp.float32)
        bound = 1.0 / np.sqrt(D_IN)
        W = jax.random.uniform(k5, (D_OUT, D_IN), minval=-bound, maxval=bound, dtype=jnp.float32)
        b = jax.random.uniform(k6, (D_OUT,), minval=-bound, maxval=bound, dtype=jnp.float32)
        return {'x': x, 'edge_row': edge_row, 'edge_col': edge_col, 'edge_val': edge_val, 'W': W, 'b': b}
    _L0_gnn_all = _L0_gnn_setup()
    _L0_gnn_in = {k: v for k, v in _L0_gnn_all.items() if k in ('W', 'b')}
    del _L0_gnn_all

    def _L1_gnn_setup():
        import jax, jax.numpy as jnp
        import numpy as np
        N = 625
        E = 10000
        D_IN = 256
        HID = 64
        HEADS = 4
        D_OUT = 256
        EPS = 1e-05
        SLOPE = 0.2

        def _gat(x, src, dst, W, a_src, a_dst, b, heads, ch, concat):
            n = x.shape[0]
            h = (x @ W).reshape(n, heads, ch)
            es = (h * a_src).sum(-1)
            ed = (h * a_dst).sum(-1)
            e = jax.nn.leaky_relu(es[src] + ed[dst], SLOPE)
            m = jax.ops.segment_max(e, dst, num_segments=n)
            w = jnp.exp(e - m[dst])
            den = jax.ops.segment_sum(w, dst, num_segments=n)
            alpha = w / den[dst]
            msg = h[src] * alpha[:, :, None]
            out = jax.ops.segment_sum(msg, dst, num_segments=n)
            out = out.reshape(n, heads * ch) if concat else out.mean(axis=1)
            return out + b

        def _layernorm(x, g, b):
            mu = x.mean(-1, keepdims=True)
            v = ((x - mu) ** 2).mean(-1, keepdims=True)
            return (x - mu) * jax.lax.rsqrt(v + EPS) * g + b
        key = jax.random.key(seed)
        ks = jax.random.split(key, 10)

        def glorot(k, shape):
            fan_in, fan_out = (shape[0], int(np.prod(shape[1:])))
            s = np.sqrt(2.0 / (fan_in + fan_out)).astype(np.float32)
            return jax.random.normal(k, shape, dtype=jnp.float32) * s
        x = jax.random.normal(ks[0], (N, D_IN), dtype=jnp.float32)
        edge_index = jax.random.randint(ks[1], (2, E), 0, N, dtype=jnp.int64)
        return {'x': x, 'edge_index': edge_index, 'W1': glorot(ks[2], (D_IN, HEADS * HID)), 'a1_src': glorot(ks[3], (HEADS, HID)), 'a1_dst': glorot(ks[4], (HEADS, HID)), 'b1': jnp.zeros((HEADS * HID,), jnp.float32), 'ln_g': jnp.ones((HEADS * HID,), jnp.float32), 'ln_b': jnp.zeros((HEADS * HID,), jnp.float32), 'W2': glorot(ks[5], (HEADS * HID, D_OUT)), 'a2_src': glorot(ks[6], (1, D_OUT)), 'a2_dst': glorot(ks[7], (1, D_OUT)), 'b2': jnp.zeros((D_OUT,), jnp.float32)}
    _L1_gnn_all = _L1_gnn_setup()
    _L1_gnn_in = {k: v for k, v in _L1_gnn_all.items() if k in ('W1', 'a1_src', 'a1_dst', 'b1', 'ln_g', 'ln_b', 'W2', 'a2_src', 'a2_dst', 'b2')}
    del _L1_gnn_all

    def _L2_gnn_setup():
        import jax, jax.numpy as jnp
        import numpy as np
        N_NODES = 50000
        N_EDGES = 12500
        IN_DIM = 256
        HID = 64
        HEADS = 8
        OUT_DIM = 256
        NEG_SLOPE = 0.2

        def _gat_forward(x, edge_index, W, a, Wo, bo):
            n = x.shape[0]
            src, tgt = (edge_index[0], edge_index[1])
            h = jnp.einsum('ni,hio->nho', x, W)
            a_src, a_tgt = (a[:, :HID], a[:, HID:])
            s_src = jnp.einsum('nho,ho->nh', h, a_src)
            s_tgt = jnp.einsum('nho,ho->nh', h, a_tgt)
            e = s_src[src] + s_tgt[tgt]
            e = jnp.where(e >= 0, e, NEG_SLOPE * e)
            m = jax.ops.segment_max(e, tgt, num_segments=n)
            ex = jnp.exp(e - m[tgt])
            denom = jax.ops.segment_sum(ex, tgt, num_segments=n)
            alpha = ex / (denom[tgt] + 1e-16)
            msgs = h[src] * alpha[:, :, None]
            out = jax.ops.segment_sum(msgs, tgt, num_segments=n)
            out = out.reshape(n, HEADS * HID)
            out = out @ Wo + bo
            return jax.nn.elu(out)
        key = jax.random.key(seed)
        ks = jax.random.split(key, 6)
        x = jax.random.normal(ks[0], (N_NODES, IN_DIM), dtype=jnp.float32)
        edge_index = jax.random.randint(ks[1], (2, N_EDGES), 0, N_NODES, dtype=jnp.int64)
        W = jax.random.normal(ks[2], (HEADS, IN_DIM, HID), dtype=jnp.float32) * (1.0 / np.sqrt(IN_DIM))
        a = jax.random.normal(ks[3], (HEADS, 2 * HID), dtype=jnp.float32) * (1.0 / np.sqrt(2 * HID))
        Wo = jax.random.normal(ks[4], (HEADS * HID, OUT_DIM), dtype=jnp.float32) * (1.0 / np.sqrt(HEADS * HID))
        bo = jnp.zeros((OUT_DIM,), dtype=jnp.float32)
        return {'x': x, 'edge_index': edge_index, 'W': W, 'a': a, 'Wo': Wo, 'bo': bo}
    _L2_gnn_all = _L2_gnn_setup()
    _L2_gnn_in = {k: v for k, v in _L2_gnn_all.items() if k in ('W', 'a', 'Wo', 'bo')}
    del _L2_gnn_all

    def _L3_gnn_setup():
        import jax, jax.numpy as jnp
        import numpy as np
        N = 50000
        E = 12500
        IN = 256
        H = 8
        D = 32
        EF = 3
        key = jax.random.key(seed)
        ks = jax.random.split(key, 8)
        x = jax.random.normal(ks[0], (N, IN), dtype=jnp.float32)
        edge_index = jax.random.randint(ks[1], (2, E), 0, N, dtype=jnp.int64)
        edge_attr = jax.random.normal(ks[2], (E, EF), dtype=jnp.float32)
        W = jax.random.normal(ks[3], (H * D, IN), dtype=jnp.float32) * np.float32(np.sqrt(2.0 / (IN + H * D)))
        a_src = jax.random.normal(ks[4], (H, D), dtype=jnp.float32) * np.float32(np.sqrt(2.0 / (H + D)))
        a_dst = jax.random.normal(ks[5], (H, D), dtype=jnp.float32) * np.float32(np.sqrt(2.0 / (H + D)))
        edge_W = jax.random.normal(ks[6], (H * D, EF), dtype=jnp.float32) * np.float32(np.sqrt(2.0 / (EF + H * D)))
        edge_b = jnp.zeros((H * D,), dtype=jnp.float32)
        bias = jnp.zeros((H * D,), dtype=jnp.float32)
        return {'x': x, 'W': W, 'a_src': a_src, 'a_dst': a_dst, 'edge_W': edge_W, 'edge_b': edge_b, 'bias': bias, 'edge_attr': edge_attr, 'edge_index': edge_index}
    _L3_gnn_all = _L3_gnn_setup()
    _L3_gnn_in = {k: v for k, v in _L3_gnn_all.items() if k in ('W', 'a_src', 'a_dst', 'edge_W', 'edge_b', 'bias')}
    del _L3_gnn_all
    return {'x': x, 'src': src, 'dst': dst, 'edge_attr_3': edge_attr_3, 'edge_weight': edge_weight, 'L0_gnn_W': _L0_gnn_in['W'], 'L0_gnn_b': _L0_gnn_in['b'], 'L1_gnn_W1': _L1_gnn_in['W1'], 'L1_gnn_a1_src': _L1_gnn_in['a1_src'], 'L1_gnn_a1_dst': _L1_gnn_in['a1_dst'], 'L1_gnn_b1': _L1_gnn_in['b1'], 'L1_gnn_ln_g': _L1_gnn_in['ln_g'], 'L1_gnn_ln_b': _L1_gnn_in['ln_b'], 'L1_gnn_W2': _L1_gnn_in['W2'], 'L1_gnn_a2_src': _L1_gnn_in['a2_src'], 'L1_gnn_a2_dst': _L1_gnn_in['a2_dst'], 'L1_gnn_b2': _L1_gnn_in['b2'], 'L2_gnn_W': _L2_gnn_in['W'], 'L2_gnn_a': _L2_gnn_in['a'], 'L2_gnn_Wo': _L2_gnn_in['Wo'], 'L2_gnn_bo': _L2_gnn_in['bo'], 'L3_gnn_W': _L3_gnn_in['W'], 'L3_gnn_a_src': _L3_gnn_in['a_src'], 'L3_gnn_a_dst': _L3_gnn_in['a_dst'], 'L3_gnn_edge_W': _L3_gnn_in['edge_W'], 'L3_gnn_edge_b': _L3_gnn_in['edge_b'], 'L3_gnn_bias': _L3_gnn_in['bias']}

def reference(x, src, dst, edge_attr_3, edge_weight, L0_gnn_W, L0_gnn_b, L1_gnn_W1, L1_gnn_a1_src, L1_gnn_a1_dst, L1_gnn_b1, L1_gnn_ln_g, L1_gnn_ln_b, L1_gnn_W2, L1_gnn_a2_src, L1_gnn_a2_dst, L1_gnn_b2, L2_gnn_W, L2_gnn_a, L2_gnn_Wo, L2_gnn_bo, L3_gnn_W, L3_gnn_a_src, L3_gnn_a_dst, L3_gnn_edge_W, L3_gnn_edge_b, L3_gnn_bias):
    import jax
    import jax.numpy as jnp

    def _L0_gnn_ref(x, edge_row, edge_col, edge_val, W, b):
        import jax, jax.numpy as jnp
        import numpy as np
        N_NODES = 3125
        N_EDGES = 100000
        D_IN = 256
        D_OUT = 256
        gathered = edge_val[:, None] * x[edge_col]
        agg = jax.ops.segment_sum(gathered, edge_row, num_segments=N_NODES)
        return jnp.einsum('nd,od->no', agg, W) + b

    def _L1_gnn_ref(x, edge_index, W1, a1_src, a1_dst, b1, ln_g, ln_b, W2, a2_src, a2_dst, b2):
        import jax, jax.numpy as jnp
        import numpy as np
        N = 625
        E = 10000
        D_IN = 256
        HID = 64
        HEADS = 4
        D_OUT = 256
        EPS = 1e-05
        SLOPE = 0.2

        def _gat(x, src, dst, W, a_src, a_dst, b, heads, ch, concat):
            n = x.shape[0]
            h = (x @ W).reshape(n, heads, ch)
            es = (h * a_src).sum(-1)
            ed = (h * a_dst).sum(-1)
            e = jax.nn.leaky_relu(es[src] + ed[dst], SLOPE)
            m = jax.ops.segment_max(e, dst, num_segments=n)
            w = jnp.exp(e - m[dst])
            den = jax.ops.segment_sum(w, dst, num_segments=n)
            alpha = w / den[dst]
            msg = h[src] * alpha[:, :, None]
            out = jax.ops.segment_sum(msg, dst, num_segments=n)
            out = out.reshape(n, heads * ch) if concat else out.mean(axis=1)
            return out + b

        def _layernorm(x, g, b):
            mu = x.mean(-1, keepdims=True)
            v = ((x - mu) ** 2).mean(-1, keepdims=True)
            return (x - mu) * jax.lax.rsqrt(v + EPS) * g + b
        loops = jnp.arange(N, dtype=edge_index.dtype)
        src = jnp.concatenate([edge_index[0], loops])
        dst = jnp.concatenate([edge_index[1], loops])
        h = _gat(x, src, dst, W1, a1_src, a1_dst, b1, HEADS, HID, True)
        h = jax.nn.relu(_layernorm(h, ln_g, ln_b))
        out = _gat(h, src, dst, W2, a2_src, a2_dst, b2, 1, D_OUT, False)
        return out

    def _L2_gnn_ref(x, edge_index, W, a, Wo, bo):
        import jax, jax.numpy as jnp
        import numpy as np
        N_NODES = 50000
        N_EDGES = 12500
        IN_DIM = 256
        HID = 64
        HEADS = 8
        OUT_DIM = 256
        NEG_SLOPE = 0.2

        def _gat_forward(x, edge_index, W, a, Wo, bo):
            n = x.shape[0]
            src, tgt = (edge_index[0], edge_index[1])
            h = jnp.einsum('ni,hio->nho', x, W)
            a_src, a_tgt = (a[:, :HID], a[:, HID:])
            s_src = jnp.einsum('nho,ho->nh', h, a_src)
            s_tgt = jnp.einsum('nho,ho->nh', h, a_tgt)
            e = s_src[src] + s_tgt[tgt]
            e = jnp.where(e >= 0, e, NEG_SLOPE * e)
            m = jax.ops.segment_max(e, tgt, num_segments=n)
            ex = jnp.exp(e - m[tgt])
            denom = jax.ops.segment_sum(ex, tgt, num_segments=n)
            alpha = ex / (denom[tgt] + 1e-16)
            msgs = h[src] * alpha[:, :, None]
            out = jax.ops.segment_sum(msgs, tgt, num_segments=n)
            out = out.reshape(n, HEADS * HID)
            out = out @ Wo + bo
            return jax.nn.elu(out)
        return _gat_forward(x, edge_index, W, a, Wo, bo)

    def _L3_gnn_ref(x, W, a_src, a_dst, edge_W, edge_b, bias, edge_attr, edge_index):
        import jax, jax.numpy as jnp
        import numpy as np
        N = 50000
        E = 12500
        IN = 256
        H = 8
        D = 32
        EF = 3
        n = x.shape[0]
        h = (x @ W.T).reshape(n, H, D)
        src, dst = (edge_index[0], edge_index[1])
        h_src = h[src]
        h_dst = h[dst]
        alpha = jnp.einsum('ehd,hd->eh', h_src, a_src) + jnp.einsum('ehd,hd->eh', h_dst, a_dst)
        enc = jax.nn.relu(edge_attr @ edge_W.T + edge_b).reshape(-1, H, D)
        alpha = alpha + jnp.sum(enc * h_dst, axis=-1)
        alpha = jnp.where(alpha >= 0, alpha, 0.2 * alpha)
        amax = jax.ops.segment_max(alpha, dst, num_segments=n)
        ex = jnp.exp(alpha - amax[dst])
        denom = jax.ops.segment_sum(ex, dst, num_segments=n)
        attn = ex / jnp.maximum(denom[dst], 1e-10)
        out = jax.ops.segment_sum(h_src * attn[..., None], dst, num_segments=n)
        return out.reshape(n, H * D) + bias
    edge_index = jnp.stack([src, dst])
    x = _layernorm(x + _L0_gnn_ref(x, src, dst, edge_weight, L0_gnn_W, L0_gnn_b), axis=-1)
    x = _layernorm(x + _L1_gnn_ref(x, edge_index, L1_gnn_W1, L1_gnn_a1_src, L1_gnn_a1_dst, L1_gnn_b1, L1_gnn_ln_g, L1_gnn_ln_b, L1_gnn_W2, L1_gnn_a2_src, L1_gnn_a2_dst, L1_gnn_b2), axis=-1)
    x = _layernorm(x + _L2_gnn_ref(x, edge_index, L2_gnn_W, L2_gnn_a, L2_gnn_Wo, L2_gnn_bo), axis=-1)
    x = _layernorm(x + _L3_gnn_ref(x, L3_gnn_W, L3_gnn_a_src, L3_gnn_a_dst, L3_gnn_edge_W, L3_gnn_edge_b, L3_gnn_bias, edge_attr_3, edge_index), axis=-1)
    return x

_drawn_inputs = setup_inputs


def setup_inputs(seed=0):
    import zlib

    import numpy as np

    out = dict(_drawn_inputs(seed))
    spreads = {'L1_gnn_b1': (0.0, 0.1),
     'L1_gnn_ln_g': (1.0, 0.2),
     'L1_gnn_ln_b': (0.0, 0.1),
     'L1_gnn_b2': (0.0, 0.1),
     'L2_gnn_bo': (0.0, 0.1),
     'L3_gnn_edge_b': (0.0, 0.1),
     'L3_gnn_bias': (0.0, 0.1)}
    factors = {}
    for name, (base, spread) in spreads.items():
        noise = np.random.default_rng([zlib.crc32(name.encode()), seed]).standard_normal(out[name].shape)
        drawn = base * np.exp(spread * noise) if base else spread * noise
        out[name] = jnp.asarray(drawn.astype(out[name].dtype))
    for name, factor in factors.items():
        out[name] = (out[name] * factor).astype(out[name].dtype)
    return out
```

```python
from contextlib import ExitStack

import concourse.bass as bass
import numpy as np
from concourse import mybir

F32 = mybir.dt.float32
BF16 = mybir.dt.bfloat16
I32 = mybir.dt.int32
U32 = mybir.dt.uint32
U8 = mybir.dt.uint8
ALU = mybir.AluOpType
ACT = mybir.ActivationFunctionType
AX = mybir.AxisListType.X
DVE_ENGINE = mybir.EngineType.DVE
PE_ENGINE = mybir.EngineType.PE
ACT_ENGINE = mybir.EngineType.Activation

P = 128
N_NODES = 3125
D = 256
KC = D // P
NB = -(-N_NODES // P)
FEAT_ROWS = 96
LAST = N_NODES - (NB - 1) * P
N_LOOPS = 625
N_EDGES = 50000
COLS = -(-N_EDGES // P)
E_PAD = COLS * P
ROWS = E_PAD + P
U = 8
T = -(-(N_EDGES // P + NB) // U) * U
TURNS = T // U
CH = 4
TP = CH * P
NO_NODE = NB * P
BANK = 512
BIG = 1e30
EPS = 1e-5
HW = 8
ACCS = 4
DUMP = NB * P
assert T <= TP and ROWS >= N_EDGES + P


class Signal:

    def __init__(self, sem):
        self.sem = sem
        self.base = 0

    def at(self, count):
        return count + self.base

    def phase_ends(self, counted):
        self.base += counted


def chain(engine, sig):
    count = [0]

    def step(ins):
        count[0] += 1
        ins.then_inc(sig.sem, 1)
        engine.wait_ge(sig.sem, sig.at(count[0]))
        return count[0]

    step.count = count
    return step


def stand_alone(engine, passed):
    engine.sem_inc(passed.sem, 1)


class Steps:

    def __init__(self, engine, sig, per):
        self.engine, self.sig, self.per = engine, sig, per

    def turn(self, n):
        self.n, self.c = n, 0

    def __call__(self, ins, apart=None):
        self.c += 1
        assert self.c <= self.per
        ins.then_inc(self.sig.sem, 1)
        self.engine.wait_ge(self.sig.sem, self.sig.at(self.n * self.per + self.c))
        if apart is not None:
            stand_alone(self.engine, apart)


def over_tiles(engine, turn):
    turn(0, True)
    with engine.Fori(1, TURNS) as i:
        turn(i, False)


def slot_turn(n, slot):
    return n // 2 + 1 if isinstance(n, int) else (n + 2 - slot) // 2


def over_blocks(engine, one):
    one(0, 0, True)
    one(1, 1, True)
    with engine.Fori(1, NB // 2) as i:
        one(2 * i, 0, False)
        one(2 * i + 1, 1, False)
    one(NB - 1, 0, False)


class Layer:
    def __init__(self, name, heads, cols, w, a, b=None, loops=False, edge_feats=False):
        self.name, self.heads, self.cols, self.w, self.a, self.b = name, heads, cols, w, a, b
        self.loops, self.edge_feats = loops, edge_feats
        self.wcols = 2 * heads if loops else heads


def gnn_kernel(nc, t, out, debug=None, stop=None):
    ctx = ExitStack()
    with ctx:
        def dram(name, shape, dt):
            return nc.dram_tensor(name, shape, dt, kind="Internal").ap()

        def sb(name, shape, dt=F32):
            return ctx.enter_context(nc.sbuf_tensor(name, shape, dt))

        def signal(name):
            return Signal(ctx.enter_context(nc.semaphore(name)))

        edge_ids = dram("edge_ids", [ROWS, 2], I32)
        edge_vals = dram("edge_vals", [ROWS, 4], F32)
        table = {w: dram(f"table{w}", [NB * P, w], F32) for w in (D, 2 * D)}
        sums = [dram(f"sums{k}", [DUMP + P, D], F32) for k in range(ACCS)]
        dst_rows = dram("dst_rows", [1, TP * P], BF16)
        src_rows = dram("src_rows", [1, TP * P], BF16)
        src_ids = dram("src_ids", [1, TP * P], F32)
        feat_rows = dram("feat_rows", [9, TP * P], BF16)
        key_list = dram("key_list", [1, E_PAD], F32)
        block_row = dram("block_row", [1, TP], I32)
        ends = dram("ends", [2, TP + 2], F32)

        x = sb("x", [P, NB, D])
        acc = sb("acc", [P, NB, 2 * D + HW])
        node_rows = acc[:, :, D + HW:2 * D + HW]
        node_parts = acc[:, :, 0:3 * D // 2].bitcast(BF16)
        logits = sb("logits", [P, 8, TP])
        weights = sb("weights", [P, T, HW])
        ones_row = sb("ones_row", [1, P])
        stats = sb("stats", [P, NB, 2])
        rstd = sb("rstd", [P, NB])
        root_t = sb("root_t", [P, NB])
        att = sb("att", [P, NB, 2 * HW])
        src_hot = sb("src_hot", [P, T, NB], U8)
        src_u = sb("src_u", [P, T], U32)
        dst_in = sb("dst_in", [P, TP])
        src_f = sb("src_f", [P, TP])
        edge_w = sb("edge_w", [P, TP])
        keep = sb("keep", [P, T])
        block_of = sb("block_of", [1, TP], I32)
        loop_mask = sb("loop_mask", [P, NB])
        loop_pen = sb("loop_pen", [P, NB])
        ident = sb("ident", [P, P])
        iota_row = sb("iota_row", [P, P])
        iota_col = sb("iota_col", [P, 1])
        left_pen = sb("left_pen", [P, TP])
        right_pen = sb("right_pen", [P, TP])
        left_in = sb("left_in", [P, TP])
        right_in = sb("right_in", [P, TP])
        first = sb("first", [P, TP])
        tile_left_pen = sb("tile_left_pen", [8, TP])
        tile_right_pen = sb("tile_right_pen", [8, TP])

        psum = ctx.enter_context(nc.psum_tensor("psum", [P, 8, 512], F32))

        ds = [signal(f"sw_dma_{i}") for i in range(8)]
        hs = [signal(f"sp_dma_{i}") for i in range(8)]
        hload = signal("load_landed")
        hstore = signal("store_landed")
        hload2 = signal("load2_landed")
        dve_done = signal("dve_done")
        act_done = signal("act_done")
        pe_done = signal("pe_done")
        pool_done = signal("pool_done")
        dve_b = signal("dve_b_done")
        act_b = signal("act_b_done")
        pe_b = signal("pe_b_done")
        flags = [signal(f"flag_{i}") for i in range(16)]
        begun2 = signal("feats_ready")
        passed = signal("waits_passed")
        order_rows = signal("order_rows_loaded")
        order_keyed = signal("order_keys_made")
        order_key = signal("order_keys_stored")
        order_in = signal("order_chunk_landed")
        order_ranked = signal("order_chunk_counted")
        order_step = signal("order_step_done")
        order_staged = signal("order_column_staged")
        order_out = signal("order_column_scattered")
        every = [*flags, *ds, *hs, hload, hstore, hload2, dve_done, act_done, pe_done, pool_done, dve_b, act_b, pe_b]


        V, A, PE, POOL, SP = nc.vector, nc.scalar, nc.tensor, nc.gpsimd, nc.sync

        def tiles_first(ap):
            return ap.rearrange("o (c p i) -> p (o c) i", c=CH, p=P)

        def row(ap, n):
            return ap[:, bass.ds(n, 1), :].rearrange("p o d -> p (o d)")

        def order_phase():
            (loaded, copied, keyed, key_stored, chunk_in, scattered) = (hload, hstore, flags[0], hs[0], order_in, ds[0])
            (counted, flagged, ones_set, staged, ranked) = (flags[1], flags[2], flags[3], order_staged, order_ranked)
            CHUNK = E_PAD // 8
            with ExitStack() as scope:
                def tmp(name, shape, dt=F32):
                    return scope.enter_context(nc.sbuf_tensor(name, shape, dt))

                dst_i = tmp("order_dst", [P, 2, COLS], I32)
                dst_f = tmp("order_dst_f", [P, 2, COLS])
                falls = tmp("order_falls", [P, COLS])
                n_falls = tmp("order_n_falls", [P, 1])
                ones = tmp("order_ones", [P, P])
                flag_f = tmp("order_flag_f", [P, 1])
                flag_i = tmp("order_flag_i", [P, 1], I32)
                key = tmp("order_key", [P, COLS])
                rank = tmp("order_rank", [P, COLS])
                column_i = tmp("order_column_i", [P, COLS], I32)
                column = tmp("order_column", [P, COLS])
                less = tmp("order_less", [P, COLS])
                count = tmp("order_count", [P, 2])
                lane_i = tmp("order_lane_i", [P, 1], I32)
                lane = tmp("order_lane", [P, 1])
                ids = tmp("order_ids", [P, COLS, 2], I32)
                vals = tmp("order_vals", [P, COLS, 4])
                one_rank = tmp("order_one_rank", [P, 1], U32)
                one_ids = tmp("order_one_ids", [P, 2], I32)
                one_vals = tmp("order_one_vals", [P, 4])
                room = acc[:, :, :].rearrange("p n d -> p (n d)")
                chunk, junk = room[:, 0:CHUNK], room[:, CHUNK:2 * CHUNK]

                def flat(ap, rows, per):
                    return ap[0:rows, :].rearrange("(p r) f -> p r f", p=P)

                def unsorted(engine):
                    return engine.If(engine.value_load(flag_i[0:1, 0:1], min_val=0, max_val=1) > 0)

                with nc.Block() as block:
                    @block.sync
                    def _(sp):
                        sp.dma_start(dst_i[:, 0, :], t["dst_list"][0:1, 0:E_PAD].rearrange("o (p c) -> (o p) c", p=P),
                                     ).then_inc(loaded.sem, 16)
                        sp.dma_start(dst_i[:, 1, :], t["dst_list"][0:1, 1:E_PAD + 1].rearrange("o (p c) -> (o p) c", p=P),
                                     ).then_inc(loaded.sem, 16)
                        for to, of in ((edge_ids, t["edge_ids"]), (edge_vals, t["edge_vals"])):
                            sp.dma_start(flat(to, ROWS, 0).rearrange("p r f -> p (r f)"),
                                         flat(of, ROWS, 0).rearrange("p r f -> p (r f)")).then_inc(copied.sem, 16)
                        sp.wait_ge(copied.sem, copied.at(32))
                        sp.wait_ge(flagged.sem, flagged.at(1))
                        with unsorted(sp):
                            sp.dma_start(ids[:, :, :], flat(t["edge_ids"], E_PAD, 0)).then_inc(order_rows.sem, 16)
                            sp.dma_start(vals[:, :, :], flat(t["edge_vals"], E_PAD, 0)).then_inc(order_rows.sem, 16)
                            sp.wait_ge(order_keyed.sem, order_keyed.at(1))
                            sp.dma_start(key_list.rearrange("o (p c) -> (o p) c", p=P), key[:, :]).then_inc(order_key.sem, 16)
                            sp.wait_ge(order_key.sem, order_key.at(16))
                            with sp.Fori(0, E_PAD // CHUNK) as c:
                                sp.wait_ge(ranked.sem, ranked.at(c + 1))
                                sp.dma_start(chunk, key_list[0:1, bass.ds(c * CHUNK, CHUNK)].broadcast_to([P, CHUNK]),
                                             ).then_inc(chunk_in.sem, 16)
                            sp.wait_ge(order_rows.sem, order_rows.at(32))

                    @block.gpsimd
                    def _(pool):
                        step = chain(pool, pool_done)
                        step(POOL.iota(column_i[:, :], [[1, COLS]], base=0, channel_multiplier=0))
                        step(POOL.tensor_copy(column[:, :], column_i[:, :]))
                        step(POOL.iota(lane_i[:, :], [[1, 1]], base=0, channel_multiplier=1))
                        step(POOL.tensor_copy(lane[:, :], lane_i[:, :]))
                        POOL.memset(ones[:, :], 1.0).then_inc(ones_set.sem, 1)
                        pool.wait_ge(flagged.sem, flagged.at(1))
                        with unsorted(pool):
                            with pool.Fori(0, COLS) as j:
                                pool.wait_ge(staged.sem, staged.at(j + 1))
                                stand_alone(pool, passed)
                                pool.indirect_dma_start(
                                    edge_ids, bass.IndirectOffsetOnAxis(ap=one_rank[:, :], axis=0), one_ids[:, :], None,
                                ).then_inc(order_out.sem, 16)
                                pool.indirect_dma_start(
                                    edge_vals, bass.IndirectOffsetOnAxis(ap=one_rank[:, :], axis=0), one_vals[:, :], None,
                                ).then_inc(order_out.sem, 16)
                                pool.wait_ge(order_out.sem, order_out.at(32 * (j + 1)))
                                stand_alone(pool, passed)

                    @block.tensor
                    def _(pe):
                        pe.wait_ge(ones_set.sem, ones_set.at(1))
                        pe.wait_ge(counted.sem, counted.at(1))
                        PE.matmul(psum[:, 0, 0:1], ones[:, :], n_falls[:, :], start=True, stop=True).then_inc(keyed.sem, 1)

                    @block.vector
                    def _(dve):
                        step = chain(dve, dve_done)
                        dve.wait_ge(loaded.sem, loaded.at(32))
                        step(V.tensor_copy(dst_f[:, :, :], dst_i[:, :, :]))
                        step(V.tensor_tensor(falls[:, :], dst_f[:, 0, :], dst_f[:, 1, :], ALU.is_gt))
                        V.reduce_sum(n_falls[:, :], falls[:, :], AX).then_inc(counted.sem, 1)
                        dve.wait_ge(keyed.sem, keyed.at(1))
                        step(V.tensor_scalar_min(flag_f[:, :], psum[:, 0, 0:1], 1.0))
                        V.tensor_copy(flag_i[:, :], flag_f[:, :]).then_inc(flagged.sem, 1)
                        dve_done.phase_ends(step.count[0])
                        dve.wait_ge(flagged.sem, flagged.at(1))
                        with unsorted(dve):
                            V.tensor_scalar(key[:, :], dst_f[:, 0, :], float(P), lane[:, :], ALU.mult, ALU.add,
                                            ).then_inc(order_keyed.sem, 1)
                            V.memset(rank[:, :], 0.0).then_inc(ranked.sem, 1)
                            dve.wait_ge(order_keyed.sem, order_keyed.at(1))
                            with dve.Fori(0, E_PAD // CHUNK) as c:
                                dve.wait_ge(chunk_in.sem, chunk_in.at(16 * (c + 1)))
                                stand_alone(dve, passed)
                                with dve.Fori(0, COLS) as j:
                                    V.tensor_scalar(junk, chunk, key[:, bass.ds(j, 1)], 0.0, ALU.is_lt, ALU.add,
                                                    accum_out=count[:, 0:1]).then_inc(order_step.sem, 1)
                                    dve.wait_ge(order_step.sem, order_step.at(c * (2 * COLS) + j * 2 + 1))
                                    V.tensor_tensor(rank[:, bass.ds(j, 1)], rank[:, bass.ds(j, 1)], count[:, 0:1], ALU.add,
                                                    ).then_inc(order_step.sem, 1)
                                    dve.wait_ge(order_step.sem, order_step.at(c * (2 * COLS) + j * 2 + 2))
                                V.memset(count[:, 0:1], 0.0).then_inc(ranked.sem, 1)
                            dve.wait_ge(order_rows.sem, order_rows.at(32))
                            done = E_PAD // CHUNK * 2 * COLS
                            with dve.Fori(0, COLS) as j:
                                V.tensor_scalar(less[:, :], column[:, :], column[:, bass.ds(j, 1)], None, ALU.is_lt,
                                                ).then_inc(order_step.sem, 1)
                                dve.wait_ge(order_step.sem, order_step.at(done + j * 2 + 1))
                                V.scalar_tensor_tensor(junk[:, 0:COLS], dst_f[:, 0, :], dst_f[:, 0, bass.ds(j, 1)], less[:, :],
                                                       ALU.is_equal, ALU.mult, accum_out=count[:, 1:2]).then_inc(order_step.sem, 1)
                                dve.wait_ge(order_step.sem, order_step.at(done + j * 2 + 2))
                                V.tensor_tensor(one_rank[:, :], rank[:, bass.ds(j, 1)], count[:, 1:2], ALU.add)
                                V.tensor_copy(one_ids[:, :], row(ids, j))
                                V.tensor_copy(one_vals[:, :], row(vals, j)).then_inc(staged.sem, 1)
                                dve.wait_ge(staged.sem, staged.at(j + 1))
                                dve.wait_ge(order_out.sem, order_out.at(32 * (j + 1)))
                                stand_alone(dve, passed)
            for sig, n in ((loaded, 32), (copied, 32), (keyed, 1), (counted, 1), (flagged, 1), (ones_set, 1), (pool_done, 4)):
                sig.phase_ends(n)

        def edge_phase():
            (loaded, gathered, rows_out, rows_in, feats_out) = (hload, ds[0], hs[0], hs[1], hs[2])
            (consts, counted, totalled, placed, tiled, ends_ready, t_ready, feats_split, int_consts) = flags[:9]
            with ExitStack() as scope:
                def tmp(name, shape, dt=F32):
                    return scope.enter_context(nc.sbuf_tensor(name, shape, dt))

                dst_cols = tmp("dst_cols", [P, COLS], I32)
                dst_f = tmp("dst_f", [P, COLS])
                below = tmp("below", [P, COLS])
                cnt = tmp("cnt", [P, NB])
                ones = tmp("ones", [P, P])
                start = tmp("start", [P, NB + 1])
                size = tmp("size", [P, NB])
                size_i = tmp("size_i", [P, NB], I32)
                n_tiles = tmp("n_tiles", [P, NB])
                tile0 = tmp("tile0", [P, NB + 1])
                shift = tmp("shift", [P, NB])
                dshift = tmp("dshift", [P, NB - 1])
                tile_i = tmp("tile_i", [P, CH], I32)
                tile_no = tmp("tile_no", [P, CH])
                past = tmp("past", [P, CH, NB - 1])
                prod = tmp("prod", [P, CH, NB - 1])
                block_t = tmp("block_t", [P, CH])
                block_i = tmp("block_i", [P, CH], I32)
                edge0 = tmp("edge0", [P, CH])
                valid = tmp("valid", [P, CH])
                clamped = tmp("clamped", [P, CH])
                edge0_u = tmp("edge0_u", [P, CH], U32)
                ids_t = tmp("ids_t", [P, CH, 2 * P], I32)
                vals_t = tmp("vals_t", [P, CH, 4 * P])
                iota_i = tmp("iota_i", [P, P], I32)
                dst_g = tmp("dst_g", [P, CH, P])
                dst_l = tmp("dst_l", [P, CH, P])
                inside = tmp("inside", [P, CH, P])
                src_i = tmp("src_i", [P, CH, P], I32)
                src_t = tmp("src_t", [P, CH, P])
                src_lo = tmp("src_lo", [P, CH, P])
                src_hi = tmp("src_hi", [P, CH, P])
                src_hi_e = tmp("src_hi_e", [P, TP])
                w_t = tmp("w_t", [P, CH, P])
                feat_t = tmp("feat_t", [P, 3, CH, P])
                room = acc[:, :, :].rearrange("p n d -> p (n d)")
                feat_b = room[:, 0:9 * TP // 2].bitcast(BF16).rearrange("p (a k c i) -> p a k c i", a=3, k=3, c=CH)
                src_lo_b = tmp("src_lo_b", [P, CH, P], BF16)
                dst_l_b = tmp("dst_l_b", [P, CH, P], BF16)
                same = tmp("same", [P, CH, P])
                prev_last = tmp("prev_last", [P, CH])
                next_first = tmp("next_first", [P, CH])
                none = tmp("none", [1, 2])
                firsts = tmp("firsts", [8, TP + 1])
                lasts = tmp("lasts", [8, TP + 1])
                first_c = tmp("first_c", [P, CH])
                last_c = tmp("last_c", [P, CH])
                prev_block = tmp("prev_block", [P, CH])
                keep_row = tmp("keep_row", [1, TP])
                block_f = tmp("block_f", [1, TP + 1])

                lp3 = left_pen[:, :].rearrange("p (c i) -> p c i", c=CH)
                rp3 = right_pen[:, :].rearrange("p (c i) -> p c i", c=CH)
                li3 = left_in[:, :].rearrange("p (c i) -> p c i", c=CH)
                ri3 = right_in[:, :].rearrange("p (c i) -> p c i", c=CH)
                fi3 = first[:, :].rearrange("p (c i) -> p c i", c=CH)
                turned = [src_t, dst_l, w_t, src_hi]

                with nc.Block() as block:
                    @block.sync
                    def _(sp):
                        sp.dma_start(dst_cols[:, :], t["dst_list"][0:1, 0:E_PAD].rearrange("o (p c) -> (o p) c", p=P)).then_inc(loaded.sem, 16)
                        sp.wait_ge(tiled.sem, tiled.at(1))
                        sp.dma_start(tiles_first(dst_rows), dst_l_b[:, :, :]).then_inc(rows_out.sem, 16)
                        sp.dma_start(tiles_first(src_rows), src_lo_b[:, :, :]).then_inc(rows_out.sem, 16)
                        sp.dma_start(tiles_first(src_ids), src_t[:, :, :]).then_inc(rows_out.sem, 16)
                        sp.dma_start(block_row.rearrange("o (c p) -> p (o c)", p=P), block_i[:, :], allow_slow_non_contiguous=True).then_inc(rows_out.sem, 16)
                        sp.dma_start(ends[0:1, 1:TP + 1].rearrange("o (c p) -> p (o c)", p=P), first_c[:, :], allow_slow_non_contiguous=True).then_inc(rows_out.sem, 16)
                        sp.dma_start(ends[1:2, 1:TP + 1].rearrange("o (c p) -> p (o c)", p=P), last_c[:, :], allow_slow_non_contiguous=True).then_inc(rows_out.sem, 16)
                        sp.dma_start(ends[0:1, TP + 1:TP + 2], none[:, 0:1]).then_inc(rows_out.sem, 16)
                        sp.dma_start(ends[1:2, 0:1], none[:, 1:2]).then_inc(rows_out.sem, 16)
                        sp.wait_ge(rows_out.sem, rows_out.at(16 * 8))
                        sp.dma_start(prev_last[:, :], ends[1:2, 0:TP].rearrange("o (c p) -> p (o c)", p=P),
                                     allow_slow_non_contiguous=True).then_inc(rows_in.sem, 16)
                        sp.dma_start(next_first[:, :], ends[0:1, 2:TP + 2].rearrange("o (c p) -> p (o c)", p=P),
                                     allow_slow_non_contiguous=True).then_inc(rows_in.sem, 16)
                        sp.dma_start(firsts[:, :], ends[0:1, 1:TP + 2].broadcast_to([8, TP + 1])).then_inc(rows_in.sem, 16)
                        sp.dma_start(lasts[:, :], ends[1:2, 0:TP + 1].broadcast_to([8, TP + 1])).then_inc(rows_in.sem, 16)
                        sp.dma_start(block_of[:, :], block_row).then_inc(rows_in.sem, 16)
                        sp.wait_ge(feats_split.sem, feats_split.at(1))
                        for k in range(9):
                            sp.dma_start(tiles_first(feat_rows[k:k + 1, :]), feat_b[:, k // 3, k % 3, :, :]).then_inc(feats_out.sem, 16)
                        sp.wait_ge(rows_in.sem, rows_in.at(16 * 5))
                        sp.wait_ge(feats_out.sem, feats_out.at(16 * 9))

                    @block.gpsimd
                    def _(pool):
                        step = chain(pool, pool_done)
                        step(POOL.iota(tile_i[:, :], [[P, CH]], base=0, channel_multiplier=1))
                        step(POOL.iota(iota_i[:, :], [[1, P]], base=0, channel_multiplier=0))
                        step(POOL.tensor_copy(tile_no[:, :], tile_i[:, :]))
                        step(POOL.tensor_copy(iota_col[:, :], tile_i[:, 0:1]))
                        step(POOL.memset(ones[:, :], 1.0))
                        POOL.tensor_copy(iota_row[:, :], iota_i[:, :]).then_inc(consts.sem, 1)
                        pool.wait_ge(consts.sem, consts.at(1))
                        POOL.tensor_scalar(ident[:, :], iota_row[:, :], iota_col[:, :], None, ALU.is_equal,
                                           ).then_inc(int_consts.sem, 1)
                        pool.wait_ge(placed.sem, placed.at(1))
                        for c in range(CH):
                            pool.indirect_dma_start(
                                ids_t[:, c, :], None, edge_ids,
                                bass.IndirectOffsetOnAxis(ap=edge0_u[:, c:c + 1], axis=0)).then_inc(gathered.sem, 16)
                            pool.indirect_dma_start(
                                vals_t[:, c, :], None, edge_vals,
                                bass.IndirectOffsetOnAxis(ap=edge0_u[:, c:c + 1], axis=0)).then_inc(gathered.sem, 16)
                        pool.wait_ge(gathered.sem, gathered.at(16 * 2 * CH))

                    @block.vector
                    def _(dve):
                        step = chain(dve, dve_done)
                        dve.wait_ge(loaded.sem, loaded.at(16))
                        step(V.tensor_copy(dst_f[:, :], dst_cols[:, :]))
                        for n in range(NB):
                            step(V.tensor_scalar(below[:, :], dst_f[:, :], float((n + 1) * P), 0.0, ALU.is_lt, ALU.add,
                                                 accum_out=cnt[:, n:n + 1]))
                        V.memset(start[:, 0:1], 0.0).then_inc(counted.sem, 1)
                        dve.wait_ge(totalled.sem, totalled.at(1))
                        step(V.tensor_copy(start[:, 1:NB + 1], psum[:, 0, 0:NB]))
                        step(V.tensor_tensor(size[:, :], start[:, 1:NB + 1], start[:, 0:NB], ALU.subtract))
                        step(V.tensor_scalar_add(size_i[:, :], size[:, :], float(P - 1)))
                        step(V.tensor_single_scalar(size_i[:, :], size_i[:, :], P.bit_length() - 1, ALU.arith_shift_right))
                        step(V.tensor_copy(n_tiles[:, :], size_i[:, :]))
                        step(V.memset(tile0[:, 0:1], 0.0))
                        dve.wait_ge(consts.sem, consts.at(1))
                        step(V.tensor_tensor_scan(tile0[:, 1:NB + 1], ones[:, 0:NB], n_tiles[:, :], 0.0, ALU.mult, ALU.add))
                        step(V.scalar_tensor_tensor(shift[:, :], tile0[:, 0:NB], float(-P), start[:, 0:NB], ALU.mult, ALU.add))
                        step(V.tensor_tensor(dshift[:, :], shift[:, 1:NB], shift[:, 0:NB - 1], ALU.subtract))
                        for c in range(CH):
                            step(V.tensor_scalar(past[:, c, :], tile0[:, 1:NB], tile_no[:, c:c + 1], None, ALU.is_le))
                        step(V.reduce_sum(block_t[:, :], past[:, :, :], AX))
                        step(V.tensor_tensor(prod[:, :, :], past[:, :, :],
                                             dshift[:, :].unsqueeze(1).broadcast_to([P, CH, NB - 1]), ALU.mult))
                        step(V.reduce_sum(edge0[:, :], prod[:, :, :], AX))
                        step(V.tensor_tensor(prod[:, :, :], past[:, :, :],
                                             size[:, 1:NB].unsqueeze(1).broadcast_to([P, CH, NB - 1]), ALU.mult))
                        step(V.reduce_sum(valid[:, :], prod[:, :, :], AX))
                        step(V.scalar_tensor_tensor(edge0[:, :], tile_no[:, :], float(P), edge0[:, :], ALU.mult, ALU.add))
                        step(V.scalar_tensor_tensor(valid[:, :], valid[:, :], start[:, 1:2], edge0[:, :], ALU.add, ALU.subtract))
                        step(V.tensor_scalar_min(clamped[:, :], edge0[:, :], float(ROWS - P)))
                        V.tensor_copy(edge0_u[:, :], clamped[:, :]).then_inc(placed.sem, 1)
                        step(V.tensor_copy(block_i[:, :], block_t[:, :]))
                        for c in range(CH):
                            step(V.tensor_scalar(inside[:, c, :], iota_row[:, :], valid[:, c:c + 1], None, ALU.is_lt))
                        dve.wait_ge(gathered.sem, gathered.at(16 * 2 * CH))
                        ids = ids_t[:, :, :].rearrange("p c (i f) -> p c i f", f=2)
                        vals = vals_t[:, :, :].rearrange("p c (i f) -> p c i f", f=4)
                        step(V.tensor_copy(src_i[:, :, :], ids[:, :, :, 0]))
                        step(V.tensor_copy(dst_g[:, :, :], ids[:, :, :, 1]))
                        step(V.tensor_copy(src_t[:, :, :], src_i[:, :, :]))
                        step(V.tensor_single_scalar(src_i[:, :, :], src_i[:, :, :], P - 1, ALU.bitwise_and))
                        step(V.tensor_copy(src_lo[:, :, :], src_i[:, :, :]))
                        step(V.tensor_copy(src_lo_b[:, :, :], src_lo[:, :, :]))
                        step(V.tensor_tensor(src_hi[:, :, :], src_t[:, :, :], src_lo[:, :, :], ALU.subtract))
                        step(V.tensor_scalar(src_hi[:, :, :], src_hi[:, :, :], 1.0 / P, None, ALU.mult))
                        step(V.tensor_scalar(block_t[:, :], block_t[:, :], float(P), None, ALU.mult))
                        for c in range(CH):
                            step(V.tensor_scalar(dst_l[:, c, :], dst_g[:, c, :], block_t[:, c:c + 1], None, ALU.subtract))
                        for d in (dst_g, dst_l):
                            step(V.scalar_tensor_tensor(d[:, :, :], d[:, :, :], 1.0, inside[:, :, :], ALU.add, ALU.mult))
                            step(V.tensor_scalar_add(d[:, :, :], d[:, :, :], -1.0))
                        step(V.tensor_copy(dst_l_b[:, :, :], dst_l[:, :, :]))
                        step(V.tensor_copy(w_t[:, :, :], vals[:, :, :, 0]))
                        step(V.tensor_copy(first_c[:, :], dst_g[:, :, 0]))
                        step(V.tensor_copy(last_c[:, :], dst_g[:, :, P - 1]))
                        V.memset(none[:, :], -5.0).then_inc(tiled.sem, 1)
                        step(V.tensor_tensor(same[:, :, 0:P - 1], dst_g[:, :, 0:P - 1], dst_g[:, :, 1:P], ALU.is_equal))
                        step(V.memset(lp3[:, :, 0:1], -BIG))
                        step(V.memset(rp3[:, :, P - 1:P], -BIG))
                        step(V.tensor_scalar(lp3[:, :, 1:P], same[:, :, 0:P - 1], -1.0, BIG, ALU.add, ALU.mult))
                        step(V.tensor_scalar(rp3[:, :, 0:P - 1], same[:, :, 0:P - 1], -1.0, BIG, ALU.add, ALU.mult))
                        step(V.tensor_scalar(fi3[:, :, 1:P], same[:, :, 0:P - 1], -1.0, 1.0, ALU.mult, ALU.add))
                        for k in range(3):
                            step(V.tensor_copy(feat_t[:, k, :, :], vals[:, :, :, k + 1]))
                        for part in range(3):
                            step(V.tensor_copy(feat_b[:, part, :, :, :], feat_t[:, :, :, :]))
                            if part < 2:
                                step(V.tensor_tensor(feat_t[:, :, :, :], feat_t[:, :, :, :], feat_b[:, part, :, :, :],
                                                     ALU.subtract))
                        V.memset(block_f[:, 0:1], -1.0).then_inc(feats_split.sem, 1)
                        dve.wait_ge(rows_in.sem, rows_in.at(16 * 5))
                        for c in range(CH):
                            step(V.tensor_scalar(li3[:, c, :], dst_g[:, c, :], prev_last[:, c:c + 1], None, ALU.is_equal))
                            step(V.tensor_scalar(ri3[:, c, :], dst_g[:, c, :], next_first[:, c:c + 1], None, ALU.is_equal))
                        step(V.tensor_scalar(fi3[:, :, 0:1], li3[:, :, 0:1], -1.0, 1.0, ALU.mult, ALU.add))
                        step(V.tensor_scalar(left_in[:, :], left_in[:, :], -1.0, BIG, ALU.add, ALU.mult))
                        step(V.tensor_scalar(right_in[:, :], right_in[:, :], -1.0, BIG, ALU.add, ALU.mult))
                        step(V.tensor_tensor(tile_left_pen[:, :], lasts[:, 0:TP], lasts[:, 1:TP + 1], ALU.is_equal))
                        step(V.tensor_tensor(tile_right_pen[:, :], firsts[:, 0:TP], firsts[:, 1:TP + 1], ALU.is_equal))
                        step(V.tensor_scalar(tile_left_pen[:, :], tile_left_pen[:, :], -1.0, BIG, ALU.add, ALU.mult))
                        step(V.tensor_scalar(tile_right_pen[:, :], tile_right_pen[:, :], -1.0, BIG, ALU.add, ALU.mult))
                        step(V.memset(block_f[:, 0:1], -1.0))
                        step(V.tensor_copy(block_f[:, 1:TP + 1], block_of[:, :]))
                        V.tensor_tensor(keep_row[:, :], block_f[:, 0:TP], block_f[:, 1:TP + 1], ALU.is_equal,
                                        ).then_inc(ends_ready.sem, 1)
                        for k, to in enumerate([src_f, dst_in, edge_w, src_hi_e]):
                            dve.wait_ge(t_ready.sem, t_ready.at(k + 1))
                            step(V.tensor_copy(to[:, :], psum[:, 1 + k, :]))
                        step(V.tensor_copy(src_u[:, :], src_f[:, 0:T]))
                        dve.wait_ge(t_ready.sem, t_ready.at(5))
                        step(V.tensor_copy(keep[:, :], psum[:, 5, 0:T]))
                        step(V.tensor_tensor(src_hot[:, :, :],
                                             src_hi_e[:, 0:T].unsqueeze(2).broadcast_to([P, T, NB]),
                                             iota_row[:, 0:NB].unsqueeze(1).broadcast_to([P, T, NB]), ALU.is_equal))
                        dve_done.phase_ends(step.count[0])

                    @block.tensor
                    def _(pe):
                        pe.wait_ge(consts.sem, consts.at(1))
                        pe.wait_ge(counted.sem, counted.at(1))
                        PE.matmul(psum[:, 0, 0:NB], ones[:, :], cnt[:, :], start=True, stop=True).then_inc(totalled.sem, 1)
                        pe.wait_ge(int_consts.sem, int_consts.at(1))
                        pe.wait_ge(tiled.sem, tiled.at(1))
                        for k, array in enumerate(turned):
                            for c in range(CH):
                                last = PE.transpose(psum[:, 1 + k, c * P:(c + 1) * P], array[:, c, :], ident[:, :])
                            last.then_inc(t_ready.sem, 1)
                        pe.wait_ge(ends_ready.sem, ends_ready.at(1))
                        PE.matmul(psum[:, 5, :], ones[0:1, :], keep_row[:, :], start=True, stop=True).then_inc(t_ready.sem, 1)

                    @block.scalar
                    def _(act):
                        act.wait_ge(consts.sem, consts.at(1))
                        act.wait_ge(counted.sem, counted.at(1))
            for sig, n in ((loaded, 16), (gathered, 32 * CH), (rows_out, 16 * 8), (feats_out, 16 * 9), (feats_split, 1), (rows_in, 16 * 5), (consts, 1),
                           (counted, 1), (totalled, 1), (placed, 1), (tiled, 1), (ends_ready, 1), (t_ready, 5),
                           (int_consts, 1), (pool_done, 5)):
                sig.phase_ends(n)


        def refine_root(step):
            step(V.reciprocal(rstd[:, :], rstd[:, :]))
            step(V.tensor_tensor(root_t[:, :], rstd[:, :], rstd[:, :], ALU.mult))
            step(V.scalar_tensor_tensor(root_t[:, :], stats[:, :, 1], EPS, root_t[:, :], ALU.add, ALU.mult))
            step(V.tensor_scalar(root_t[:, :], root_t[:, :], -0.5, 1.5, ALU.mult, ALU.add))
            step(V.tensor_tensor(rstd[:, :], rstd[:, :], root_t[:, :], ALU.mult))

        def row_stats(dve, step, rows, n, bn, mv):
            step(V.bn_stats(bn[:, :], rows), apart=passed)
            step(V.bn_aggr(mv[:, :], bn[:, :]))
            step(V.tensor_copy(row(stats, n), mv[:, :]))

        def scatter_phase():
            (rows_in, hot_ready, index_ready, m_ready, m_copied, out_ready, out_copied, consts, zeroed) = (
                hs[:2], flags[0], flags[1], flags[2], flags[3], flags[4], flags[5], flags[6], hstore)
            with ExitStack() as scope:
                def tmp(name, shape, dt=F32):
                    return scope.enter_context(nc.sbuf_tensor(name, shape, dt))

                ids = tmp("ids_rows", [P, 2, 4 * P])
                equal = tmp("equal", [P, 2, 4 * P])
                hot_w = tmp("hot_w", [P, 2, 4 * P])
                tril = tmp("tril", [P, P])
                junk = tmp("junk", [P, P])
                dup = tmp("dup", [P, 2, 4])
                move = tmp("move", [P, 2, 4])
                index = tmp("index", [P, 2, 4], U32)
                m_sb = tmp("m_sb", [P, 2, 4 * P])
                val = tmp("val", [P, 2, 4 * D])
                dump = tmp("dump", [P, 1])
                zero = tmp("zero", [P, (DUMP + P) // P * D // 2])
                SD = 2 * 7

                with nc.Block() as block:
                    @block.sync
                    def _(sp):
                        sp.dma_start(x[:, 0:NB - 1, :], t["x"][0:(NB - 1) * P, :].rearrange("(n p) d -> p n d", p=P),
                                     ).then_inc(hload.sem, 16)
                        sp.wait_ge(consts.sem, consts.at(1))
                        sp.dma_start(x[0:LAST, NB - 1, :], t["x"][(NB - 1) * P:N_NODES, :]).then_inc(hload.sem, 16)
                        for k in range(ACCS):
                            for half in sums[k].rearrange("(h p r) d -> h p (r d)", h=2, p=P):
                                sp.dma_start(half, zero[:, :]).then_inc(zeroed.sem, 16)

                        def turn(i, first):
                            for h in range(2):
                                if not first:
                                    sp.wait_ge(hot_ready.sem, hot_ready.at(2 * i + h - 1))
                                at = (i * U + 4 * h) * P
                                sp.dma_start(ids[:, h, :], src_ids[0:1, bass.ds(at, 4 * P)].broadcast_to([P, 4 * P]),
                                             ).then_inc(rows_in[h].sem, 16)
                        over_tiles(sp, turn)
                        for h in range(2):
                            sp.wait_ge(rows_in[h].sem, rows_in[h].at(16 * TURNS))
                        sp.wait_ge(zeroed.sem, zeroed.at(16 * 2 * ACCS))

                    @block.gpsimd
                    def _(pool):
                        step = chain(pool, pool_done)
                        step(POOL.memset(zero[:, :], 0.0))
                        step(POOL.memset(x[:, NB - 1, :], 0.0))
                        step(POOL.memset(ones_row[:, :], 1.0))
                        step(POOL.memset(tril[:, :], 1.0))
                        whole, part = divmod(N_LOOPS, P)
                        step(POOL.memset(loop_mask[:, :], 0.0))
                        step(POOL.memset(loop_mask[:, 0:whole], 1.0))
                        step(POOL.tensor_scalar(loop_mask[:, whole:whole + 1], iota_col[:, :], float(part), None, ALU.is_lt))
                        step(POOL.tensor_scalar(loop_pen[:, :], loop_mask[:, :], -1.0, BIG, ALU.add, ALU.mult))
                        step(POOL.tensor_scalar(dump[:, :], iota_col[:, :], float(DUMP), None, ALU.add))
                        POOL.tensor_scalar(tril[:, :], iota_row[:, :], iota_col[:, :], None, ALU.is_lt).then_inc(consts.sem, 1)
                        pool.wait_ge(zeroed.sem, zeroed.at(16 * 2 * ACCS))

                        def turn(i, first):
                            for h in range(2):
                                pool.wait_ge(index_ready.sem, index_ready.at(2 * i + h + 1))
                                pool.wait_ge(out_copied.sem, out_copied.at(2 * i + h + 1))
                                for j in range(4):
                                    if not (first and h == 0):
                                        pool.wait_ge(ds[j].sem, ds[j].at(16 * (2 * i + h)))
                                        stand_alone(pool, passed)
                                    pool.indirect_dma_start(
                                        sums[j], bass.IndirectOffsetOnAxis(ap=index[:, h, j:j + 1], axis=0),
                                        val[:, h, j * D:(j + 1) * D], None, compute_op=ALU.add,
                                    ).then_inc(ds[j].sem, 16)
                        over_tiles(pool, turn)
                        for j in range(4):
                            pool.wait_ge(ds[j].sem, ds[j].at(16 * 2 * TURNS))

                    @block.vector
                    def _(dve):
                        step = Steps(dve, dve_done, SD)
                        dve.wait_ge(consts.sem, consts.at(1))

                        def turn(i, first):
                            step.turn(i)
                            for h in range(2):
                                k = 2 * i + h
                                tile = i * U + 4 * h
                                dve.wait_ge(rows_in[h].sem, rows_in[h].at(16 * (i + 1)))
                                if not first:
                                    dve.wait_ge(m_ready.sem, m_ready.at(k - 1))
                                for j in range(4):
                                    V.tensor_scalar(equal[:, h, j * P:(j + 1) * P], ids[:, h, j * P:(j + 1) * P],
                                                    src_f[:, bass.ds(tile + j, 1)], None, ALU.is_equal)
                                    ins = V.tensor_scalar(hot_w[:, h, j * P:(j + 1) * P], iota_row[:, :],
                                                          dst_in[:, bass.ds(tile + j, 1)], edge_w[:, bass.ds(tile + j, 1)],
                                                          ALU.is_equal, ALU.mult)
                                ins.then_inc(hot_ready.sem, 1)
                                dve.wait_ge(hot_ready.sem, hot_ready.at(k + 1))
                                for j in range(4):
                                    step(V.scalar_tensor_tensor(junk[:, :], equal[:, h, j * P:(j + 1) * P], 1.0, tril[:, :],
                                                                ALU.mult, ALU.mult, accum_out=dup[:, h, j:j + 1]))
                                step(V.tensor_scalar(move[:, h, :], src_f[:, bass.ds(tile, 4)], -1.0, dump[:, :],
                                                     ALU.mult, ALU.add))
                                step(V.scalar_tensor_tensor(dup[:, h, :], dup[:, h, :], 1.0, move[:, h, :], ALU.min, ALU.mult))
                                if not first:
                                    for j in range(4):
                                        dve.wait_ge(ds[j].sem, ds[j].at(16 * (k - 1)))
                                V.tensor_tensor(index[:, h, :], dup[:, h, :], src_f[:, bass.ds(tile, 4)],
                                                ALU.add).then_inc(index_ready.sem, 1)
                                step(V.memset(junk[:, 0:1], 0.0))
                        over_tiles(dve, turn)

                    @block.tensor
                    def _(pe):
                        pe.wait_ge(hload.sem, hload.at(32))

                        def turn(i, first):
                            _, blk = nc.values_load_multi_w_load_instructions(
                                block_of[0:1, bass.ds(i * U, U)], engines=[PE_ENGINE], min_val=0, max_val=NB - 1,
                                skip_runtime_bounds_check_because="blocks are counted on the chip, below NB")
                            for h in range(2):
                                k = 2 * i + h
                                pe.wait_ge(hot_ready.sem, hot_ready.at(k + 1))
                                if not first:
                                    pe.wait_ge(m_copied.sem, m_copied.at(k - 1))
                                for j in range(4):
                                    cut = slice(j * P, (j + 1) * P)
                                    ins = PE.matmul(psum[:, h, cut], hot_w[:, h, cut], equal[:, h, cut], start=True, stop=True)
                                ins.then_inc(m_ready.sem, 1)
                                pe.wait_ge(m_copied.sem, m_copied.at(k + 1))
                                if not first:
                                    pe.wait_ge(out_copied.sem, out_copied.at(k - 1))
                                for j in range(4):
                                    ins = PE.matmul(psum[:, 2 + 2 * h + j // 2, (j % 2) * D:(j % 2 + 1) * D],
                                                    m_sb[:, h, j * P:(j + 1) * P],
                                                    x[:, bass.ds(blk[4 * h + j], 1), :].rearrange("p o d -> p (o d)"),
                                                    start=True, stop=True)
                                ins.then_inc(out_ready.sem, 1)
                        over_tiles(pe, turn)

                    @block.scalar
                    def _(act):
                        def turn(i, first):
                            for h in range(2):
                                k = 2 * i + h
                                act.wait_ge(m_ready.sem, m_ready.at(k + 1))
                                if not first:
                                    act.wait_ge(out_ready.sem, out_ready.at(k - 1))
                                A.copy(m_sb[:, h, :], psum[:, h, :]).then_inc(m_copied.sem, 1)
                                act.wait_ge(out_ready.sem, out_ready.at(k + 1))
                                if not first:
                                    for j in range(4):
                                        act.wait_ge(ds[j].sem, ds[j].at(16 * (k - 1)))
                                A.copy(val[:, h, :], psum[:, 2 + 2 * h:4 + 2 * h, :].rearrange("p b f -> p (b f)"),
                                       ).then_inc(out_copied.sem, 1)
                        over_tiles(act, turn)
            for sig in (hot_ready, index_ready, m_ready, m_copied, out_ready, out_copied):
                sig.phase_ends(2 * TURNS)
            for sig, n in ((hload, 32), (zeroed, 32 * ACCS), (consts, 1), (pool_done, 9), (dve_done, SD * TURNS),
                           *((d, 32 * TURNS) for d in ds[:4]), *((d, 16 * TURNS) for d in rows_in)):
                sig.phase_ends(n)

        def first_layer_nodes():
            (turned, copied, produced, summed, stat, loaded_w) = flags[:5] + [hload]
            slot_in = hs[:2]
            with ExitStack() as scope:
                def tmp(name, shape, dt=F32):
                    return scope.enter_context(nc.sbuf_tensor(name, shape, dt))

                w_sb = tmp("w0_sb", [P, KC, D])
                b_sb = tmp("b0_sb", [1, D])
                part = tmp("part", [P, 2, ACCS, D])
                sum_t = tmp("sum_t", [P, 2, KC * P])
                bn = tmp("bn", [P, 6])
                mv = tmp("mv", [P, 2])
                SD = 3

                with nc.Block() as block:
                    @block.sync
                    def _(sp):
                        sp.dma_start(w_sb[:, :, :], t["w0"].rearrange("(k p) o -> p k o", p=P)).then_inc(loaded_w.sem, 16)
                        sp.dma_start(b_sb[:, :], t["b0"]).then_inc(loaded_w.sem, 16)

                        def one(n, s, first):
                            if not first:
                                sp.wait_ge(turned.sem, turned.at(n - 1))
                            for k in range(ACCS):
                                sp.dma_start(part[:, s, k, :], sums[k][bass.ds(n * P, P), :]).then_inc(slot_in[s].sem, 16)
                        over_blocks(sp, one)

                    @block.tensor
                    def _(pe):
                        pe.wait_ge(loaded_w.sem, loaded_w.at(32))

                        def one(n, s, first):
                            pe.wait_ge(slot_in[s].sem, slot_in[s].at(16 * ACCS * slot_turn(n, s)))
                            if not first:
                                pe.wait_ge(copied.sem, copied.at(n - 1))
                            for c in range(KC):
                                for k in range(ACCS):
                                    ins = PE.matmul(psum[:, s, c * P:(c + 1) * P], part[:, s, k, c * P:(c + 1) * P],
                                                    ident[:, :], start=k == 0, stop=k == ACCS - 1)
                            ins.then_inc(turned.sem, 1)
                            pe.wait_ge(copied.sem, copied.at(n + 1))
                            if not first:
                                pe.wait_ge(summed.sem, summed.at(n - 1))
                            for c in range(KC):
                                PE.matmul(psum[:, 2 + s, 0:D], sum_t[:, s, c * P:(c + 1) * P], w_sb[:, c, :],
                                          start=c == 0, stop=False)
                            PE.matmul(psum[:, 2 + s, 0:D], ones_row[:, :], b_sb[:, :], start=False, stop=True,
                                      ).then_inc(produced.sem, 1)
                        over_blocks(pe, one)

                    @block.scalar
                    def _(act):
                        def one(n, s, first):
                            act.wait_ge(turned.sem, turned.at(n + 1))
                            if not first:
                                act.wait_ge(produced.sem, produced.at(n - 1))
                            A.copy(sum_t[:, s, :], psum[:, s, 0:KC * P]).then_inc(copied.sem, 1)
                        over_blocks(act, one)

                    @block.vector
                    def _(dve):
                        step = Steps(dve, dve_done, SD)

                        def one(n, s, first):
                            step.turn(n)
                            xn = x[:, bass.ds(n, 1), :].rearrange("p o d -> p (o d)")
                            dve.wait_ge(produced.sem, produced.at(n + 1))
                            V.tensor_tensor(xn, xn, psum[:, 2 + s, 0:D], ALU.add).then_inc(summed.sem, 1)
                            dve.wait_ge(summed.sem, summed.at(n + 1))
                            stand_alone(dve, passed)
                            row_stats(dve, step, xn, n, bn, mv)
                        over_blocks(dve, one)
            for sig in (turned, copied, produced, summed):
                sig.phase_ends(NB)
            for sig, n in ((loaded_w, 32), (dve_done, SD * NB), (slot_in[0], 16 * ACCS * (NB // 2 + 1)),
                           (slot_in[1], 16 * ACCS * (NB // 2))):
                sig.phase_ends(n)


        def project(L, rows_of, affine, es_tab, ed_tab):
            (normed, turned, copied, produced, rows_ready, att_ready, varied, rooted, attended, kept, parted) = flags[:11]
            staged = L.cols > D or L.edge_feats
            stored = hs[:2]
            H, C = L.heads, L.cols
            with ExitStack() as scope:
                def tmp(name, shape, dt=F32):
                    return scope.enter_context(nc.sbuf_tensor(f"{L.name}_{name}", shape, dt))

                w_sb = tmp("w", [P, KC, C])
                a_sb = tmp("a", [P, 2, C])
                prod = tmp("prod", [P, C])
                w_x = tmp("wx", [P, KC, 2 * H])
                g_sb = tmp("g", [P, 2, D]) if affine else None
                y_sb = tmp("y", [P, 2, D])
                x_t = tmp("xt", [P, 2, KC * P])
                wide = tmp("wide", [P, 2, C]) if staged else None
                left = tmp("left", [P, 2, C]) if L.edge_feats else None
                rest = tmp("rest", [P, NB * 2 * H])
                rest2 = tmp("rest2", [P, NB * 2 * H])
                own = tmp("own", [P, NB, 2 * H])
                n_loads = 3 + 2 * affine
                SD = 5

                with nc.Block() as block:
                    @block.sync
                    def _(sp):
                        sp.dma_start(w_sb[:, :, :], t[L.w].rearrange("(k p) o -> p k o", p=P)).then_inc(hload.sem, 16)
                        for k in range(2):
                            sp.dma_start(a_sb[:, k, :], t[L.a[k]].broadcast_to([P, C])).then_inc(hload.sem, 16)
                        if affine:
                            sp.dma_start(g_sb[:, 0, :], t["ln_g"].broadcast_to([P, D])).then_inc(hload.sem, 16)
                            sp.dma_start(g_sb[:, 1, :], t["ln_b"].broadcast_to([P, D])).then_inc(hload.sem, 16)

                        def one(n, s, first):
                            sp.wait_ge(rows_ready.sem, rows_ready.at(n + 1))
                            sp.dma_start(table[C][bass.ds(n * P, P), :], wide[:, s, :] if staged else row(node_rows, n),
                                         ).then_inc(stored[s].sem, 16)
                        over_blocks(sp, one)
                        sp.wait_ge(stored[0].sem, stored[0].at(16 * (NB // 2 + 1)))
                        sp.wait_ge(stored[1].sem, stored[1].at(16 * (NB // 2)))

                    @block.vector
                    def _(dve):
                        step = Steps(dve, dve_done, 4 * KC + 5)
                        step.turn(0)
                        V.tensor_scalar_add(rstd[:, :], stats[:, :, 1], EPS).then_inc(varied.sem, 1)
                        dve.wait_ge(hload.sem, hload.at(16 * n_loads))
                        for k in range(KC):
                            for side in range(2):
                                step(V.tensor_tensor(prod[:, :], w_sb[:, k, :], a_sb[:, side, :], ALU.mult))
                                step(V.reduce_sum(w_x[:, k, side * H:(side + 1) * H],
                                                  prod[:, :].rearrange("p (h d) -> p h d", h=H), AX))
                        V.memset(prod[:, 0:1], 0.0).then_inc(attended.sem, 1)
                        dve.wait_ge(rooted.sem, rooted.at(1))
                        refine_root(step)
                        assert step.c == step.per
                        dve_done.phase_ends(step.per)
                        step = Steps(dve, dve_done, 3 if affine or L.edge_feats else 0)

                        def one(n, s, first):
                            step.turn(n)
                            y = y_sb[:, s, :]
                            if not first:
                                dve.wait_ge(turned.sem, turned.at(n - 1))
                                if not affine:
                                    dve.wait_ge(kept.sem, kept.at(n - 1))
                            norm = V.tensor_scalar(y, rows_of(n), stats[:, bass.ds(n, 1), 0], rstd[:, bass.ds(n, 1)],
                                                   ALU.subtract, ALU.mult)
                            if affine:
                                step(norm)
                                step(V.tensor_tensor(y, y, g_sb[:, 0, :], ALU.mult))
                                step(V.tensor_tensor(y, y, g_sb[:, 1, :], ALU.add))
                                norm = V.tensor_scalar_max(y, y, 0.0)
                            norm.then_inc(normed.sem, 1)

                        def late(n, s, first):
                            dve.wait_ge(produced.sem, produced.at(n + 1))
                            V.tensor_copy(row(att, n)[:, 0:2 * H], psum[:, 3 + 2 * s, 0:2 * H]).then_inc(att_ready.sem, 1)
                            if L.edge_feats:
                                step.turn(n)
                                dve.wait_ge(rows_ready.sem, rows_ready.at(n + 1))
                                parts = [row(node_parts, n)[:, k * D:(k + 1) * D] for k in range(3)]
                                step(V.tensor_copy(parts[0], wide[:, s, :]))
                                step(V.tensor_tensor(left[:, s, :], wide[:, s, :], parts[0], ALU.subtract))
                                step(V.tensor_copy(parts[1], left[:, s, :]))
                                V.tensor_tensor(parts[2], left[:, s, :], parts[1], ALU.subtract).then_inc(parted.sem, 1)

                        def both(n, s, first):
                            one(n, s, first)
                            if not (first and s == 0):
                                late(n - 1, 1 - s, first)
                        over_blocks(dve, both)
                        late(NB - 1, 0, False)
                        dve_done.phase_ends(step.per * NB)
                        dve.wait_ge(att_ready.sem, att_ready.at(NB))
                        step = chain(dve, dve_done)
                        rest_s = rest[:, 0:NB * H]
                        step(V.tensor_copy(rest_s.rearrange("p (n h) -> p n h", h=H), att[:, :, 0:H]))
                        for part in range(3):
                            step(V.tensor_copy(es_tab[:, part, :], rest_s))
                            step(V.tensor_tensor(rest_s, rest_s, es_tab[:, part, :], ALU.subtract))
                        M = L.wcols
                        step(V.tensor_copy(own[:, :, 0:H], att[:, :, H:2 * H]))
                        if L.loops:
                            z = own[:, :, H:2 * H]
                            step(V.tensor_tensor(z, att[:, :, 0:H], att[:, :, H:2 * H], ALU.add))
                            step(V.scalar_tensor_tensor(z, z, 0.2, z, ALU.mult, ALU.max))
                            step(V.tensor_tensor(z, z, loop_mask[:, :].unsqueeze(2).broadcast_to([P, NB, H]), ALU.mult))
                            step(V.tensor_tensor(z, z, loop_pen[:, :].unsqueeze(2).broadcast_to([P, NB, H]), ALU.add))
                        for part in range(3):
                            step(V.tensor_copy(ed_tab[:, :, part, :], own[:, :, 0:M]))
                            step(V.tensor_tensor(own[:, :, 0:M], own[:, :, 0:M], ed_tab[:, :, part, :], ALU.subtract))
                        dve_done.phase_ends(step.count[0])

                    @block.tensor
                    def _(pe):
                        pe.wait_ge(hload.sem, hload.at(16 * n_loads))
                        pe.wait_ge(attended.sem, attended.at(1))

                        def one(n, s, first):
                            pe.wait_ge(normed.sem, normed.at(n + 1))
                            if not first:
                                pe.wait_ge(copied.sem, copied.at(n - 1))
                            for c in range(KC):
                                ins = PE.transpose(psum[:, s, c * P:(c + 1) * P], y_sb[:, s, c * P:(c + 1) * P], ident[:, :])
                            ins.then_inc(turned.sem, 1)
                            pe.wait_ge(copied.sem, copied.at(n + 1))
                            if not first:
                                pe.wait_ge(rows_ready.sem, rows_ready.at(n - 1))
                                pe.wait_ge(att_ready.sem, att_ready.at(n - 1))
                            for c in range(KC):
                                PE.matmul(psum[:, 2 + 2 * s, 0:C], x_t[:, s, c * P:(c + 1) * P], w_sb[:, c, :],
                                          start=c == 0, stop=c == KC - 1)
                            for c in range(KC):
                                ins = PE.matmul(psum[:, 3 + 2 * s, 0:2 * H], x_t[:, s, c * P:(c + 1) * P], w_x[:, c, :],
                                                start=c == 0, stop=c == KC - 1)
                            ins.then_inc(produced.sem, 1)
                        over_blocks(pe, one)

                    if not affine:
                        @block.gpsimd
                        def _(pool):
                            def one(n, s, first):
                                pool.wait_ge(normed.sem, normed.at(n + 1))
                                stand_alone(pool, passed)
                                POOL.tensor_copy(rows_of(n), y_sb[:, s, :]).then_inc(kept.sem, 1)
                            over_blocks(pool, one)

                    @block.scalar
                    def _(act):
                        act.wait_ge(varied.sem, varied.at(1))
                        A.activation(rstd[:, :], rstd[:, :], ACT.Sqrt).then_inc(rooted.sem, 1)

                        def one(n, s, first):
                            act.wait_ge(turned.sem, turned.at(n + 1))
                            if not first:
                                act.wait_ge(produced.sem, produced.at(n - 1))
                            A.copy(x_t[:, s, :], psum[:, s, 0:KC * P]).then_inc(copied.sem, 1)
                            act.wait_ge(produced.sem, produced.at(n + 1))
                            if staged:
                                if L.edge_feats and not first:
                                    act.wait_ge(parted.sem, parted.at(n - 1))
                                if not first:
                                    act.wait_ge(stored[s].sem, stored[s].at(16 * (slot_turn(n, s) - 1)))
                                A.copy(wide[:, s, :], psum[:, 2 + 2 * s, 0:C]).then_inc(rows_ready.sem, 1)
                            else:
                                A.copy(row(node_rows, n), psum[:, 2 + 2 * s, 0:C]).then_inc(rows_ready.sem, 1)
                        over_blocks(act, one)
            for sig in (normed, turned, copied, produced, rows_ready, att_ready):
                sig.phase_ends(NB)
            if not affine:
                kept.phase_ends(NB)
            if L.edge_feats:
                parted.phase_ends(NB)
            for sig, n in ((varied, 1), (rooted, 1), (attended, 1), (hload, 16 * n_loads),
                           (stored[0], 16 * (NB // 2 + 1)), (stored[1], 16 * (NB // 2))):
                sig.phase_ends(n)

        def logit_phase(L, es_tab, ed_tab):
            (hot, found, looked_up, selected, summed, pair_found, rectified, multiplied, q_summed, q_added, split) = flags[:11]
            rows_in = hs[:2]
            feats_in = hs[2:4]
            H, M, FE = L.heads, L.wcols, L.edge_feats
            with ExitStack() as scope:
                def tmp(name, shape, dt=F32):
                    return scope.enter_context(nc.sbuf_tensor(f"{L.name}_{name}", shape, dt))

                s_rows = tmp("s_rows", [P, 2, 4 * P], BF16)
                d_rows = tmp("d_rows", [P, 2, 4 * P], BF16)
                hot_s = tmp("hot_s", [P, 2, 4 * P], BF16)
                hot_d = tmp("hot_d", [P, 2, 4 * P], BF16)
                sel = tmp("sel", [P, 4, NB * H])
                es = tmp("es", [P, 4, H])
                z = tmp("z", [P, 2, 4, H])
                if FE:
                    feats = tmp("feats", [FEAT_ROWS, 2, 4 * P], BF16)
                    we_sb = tmp("we", [FEAT_ROWS, D])
                    we_part = tmp("we_part", [FEAT_ROWS, D], BF16)
                    we_tab = tmp("we_tab", [FEAT_ROWS, D], BF16)
                    enc = tmp("enc", [P, 2, 4 * D])
                    q = tmp("q", [P, 4, H])
                ED0 = 2 * NB * H

                with nc.Block() as block:
                    @block.sync
                    def _(sp):
                        if FE:
                            sp.dma_start(we_sb[:, :], t["we"]).then_inc(hload.sem, 16)
                            sp.wait_ge(begun2.sem, begun2.at(1))

                        def turn(i, first):
                            for h in range(2):
                                k = 2 * i + h
                                at = (i * U + 4 * h) * P
                                if not first:
                                    sp.wait_ge(hot.sem, hot.at(k - 1))
                                    stand_alone(sp, passed)
                                for rows, to in ((src_rows, s_rows), (dst_rows, d_rows)):
                                    sp.dma_start(to[:, h, :], rows[0:1, bass.ds(at, 4 * P)].broadcast_to([P, 4 * P]),
                                                 ).then_inc(rows_in[h].sem, 16)
                                if FE:
                                    if not first:
                                        sp.wait_ge(pair_found.sem, pair_found.at(2 * k - 2))
                                        stand_alone(sp, passed)
                                    for b in range(3):
                                        sp.dma_start(feats[32 * b:32 * b + 9, h, :], feat_rows[:, bass.ds(at, 4 * P)],
                                                     ).then_inc(feats_in[h].sem, 16)
                        over_tiles(sp, turn)

                    @block.gpsimd
                    def _(pool):
                        if FE:
                            POOL.memset(feats[:, :, :], 1.0).then_inc(begun2.sem, 1)
                        POOL.memset(logits[:, :, T:TP], 0.0).then_inc(pool_done.sem, 1)

                    @block.vector
                    def _(dve):
                        if FE:
                            step = chain(dve, dve_done)
                            dve.wait_ge(hload.sem, hload.at(16))
                            for b in range(3):
                                step(V.tensor_copy(we_part[:, :], we_sb[:, :]))
                                step(V.tensor_copy(we_tab[32 * b:32 * b + 32, :], we_part[32 * b:32 * b + 32, :]))
                                step(V.tensor_tensor(we_sb[:, :], we_sb[:, :], we_part[:, :], ALU.subtract))
                            V.memset(q[:, :, :], 0.0).then_inc(split.sem, 1)
                            dve_done.phase_ends(step.count[0])

                        def rows_of_ones(i, h, side):
                            if side == 0:
                                dve.wait_ge(rows_in[h].sem, rows_in[h].at(32 * (i + 1)))
                                V.tensor_scalar(hot_s[:, h, :], s_rows[:, h, :], iota_col[:, :], None, ALU.is_equal)
                            else:
                                V.tensor_scalar(hot_d[:, h, :], d_rows[:, h, :], iota_col[:, :], None, ALU.is_equal,
                                                ).then_inc(hot.sem, 1)

                        def leaky(k, h, tile):
                            if FE:
                                dve.wait_ge(q_added.sem, q_added.at(k + 1))
                            else:
                                dve.wait_ge(looked_up.sem, looked_up.at(k + 1))
                            V.scalar_tensor_tensor(logits[:, 0:H, bass.ds(tile, 4)].rearrange("p h t -> p t h"),
                                                   z[:, h, :, :], 0.2, z[:, h, :, :], ALU.mult, ALU.max)

                        def add_q(k, h):
                            dve.wait_ge(looked_up.sem, looked_up.at(k + 1))
                            dve.wait_ge(q_summed.sem, q_summed.at(k + 1))
                            V.tensor_tensor(z[:, h, :, :], z[:, h, :, :], q[:, :, :], ALU.add).then_inc(q_added.sem, 1)

                        def turn(i, first, last):
                            for h in range(2):
                                k = 2 * i + h
                                tile = i * U + 4 * h
                                begun = not (first and h == 0)
                                dve.wait_ge(found.sem, found.at(k + 1))
                                for b in range(2):
                                    ins = V.tensor_tensor(
                                        sel[:, 2 * b:2 * b + 2, :].rearrange("p t (n h) -> p t n h", h=H),
                                        psum[:, 2 * h + b, 0:ED0].rearrange("p (t n h) -> p t n h", t=2, h=H),
                                        src_hot[:, bass.ds(tile + 2 * b, 2), :].unsqueeze(3).broadcast_to([P, 2, NB, H]),
                                        ALU.mult)
                                ins.then_inc(selected.sem, 1)
                                if FE:
                                    if begun:
                                        add_q(k - 1, 1 - h)
                                    for p in range(2):
                                        cut = slice(2 * p * D, (2 * p + 2) * D)
                                        dve.wait_ge(rectified.sem, rectified.at(2 * k + p + 1))
                                        V.tensor_tensor(enc[:, h, cut], enc[:, h, cut], psum[:, 4 + p, :], ALU.mult,
                                                        ).then_inc(multiplied.sem, 1)
                                if begun:
                                    leaky(k - 1, 1 - h, tile - 4)
                                if not last:
                                    rows_of_ones(i + 1, h, 0)
                                dve.wait_ge(selected.sem, selected.at(k + 1))
                                V.reduce_sum(es[:, :, :], sel[:, :, :].rearrange("p t (n h) -> p t h n", h=H), AX,
                                             ).then_inc(summed.sem, 1)
                                if not last:
                                    rows_of_ones(i + 1, h, 1)
                                ed = psum[:, 2 * h:2 * h + 2, ED0:ED0 + 32].rearrange("p b (t m) -> p b t m", t=2)
                                if L.loops:
                                    V.tensor_copy(logits[:, H:2 * H, bass.ds(tile, 4)].rearrange("p h (b t) -> p b t h", b=2),
                                                  ed[:, :, :, H:2 * H])
                                if FE:
                                    dve.wait_ge(multiplied.sem, multiplied.at(2 * k + 2))
                                    V.reduce_sum(q[:, :, :].rearrange("p t h -> p (t h)"),
                                                 enc[:, h, :].rearrange("p (t d) -> p t d", d=D // H), AX).then_inc(q_summed.sem, 1)
                                dve.wait_ge(summed.sem, summed.at(k + 1))
                                V.tensor_tensor(z[:, h, :, :].rearrange("p (b t) h -> p b t h", b=2),
                                                es[:, :, :].rearrange("p (b t) h -> p b t h", b=2),
                                                ed[:, :, :, 0:H], ALU.add).then_inc(looked_up.sem, 1)
                        for h in range(2):
                            for side in range(2):
                                rows_of_ones(0, h, side)
                        turn(0, True, False)
                        with dve.Fori(1, TURNS - 1) as i:
                            turn(i, False, False)
                        turn(TURNS - 1, False, True)
                        if FE:
                            add_q(2 * TURNS - 1, 1)
                        leaky(2 * TURNS - 1, 1, T - 4)

                    @block.tensor
                    def _(pe):
                        if FE:
                            pe.wait_ge(split.sem, split.at(1))

                        def turn(i, first):
                            _, blk = nc.values_load_multi_w_load_instructions(
                                block_of[0:1, bass.ds(i * U, U)], engines=[PE_ENGINE], min_val=0, max_val=NB - 1,
                                skip_runtime_bounds_check_because="blocks are counted on the chip, below NB")
                            for h in range(2):
                                k = 2 * i + h
                                pe.wait_ge(hot.sem, hot.at(k + 1))
                                if not first:
                                    pe.wait_ge(looked_up.sem, looked_up.at(k - 1))
                                for j in range(4):
                                    cut = slice(j * P, (j + 1) * P)
                                    bank = psum[:, 2 * h + j // 2, :]
                                    at = (j % 2) * NB * H
                                    for part in range(3):
                                        PE.matmul(bank[:, at:at + NB * H], hot_s[:, h, cut], es_tab[:, part, :],
                                                  start=part == 0, stop=part == 2)
                                    at = ED0 + (j % 2) * 16
                                    for part in range(3):
                                        ins = PE.matmul(bank[:, at:at + M], hot_d[:, h, cut],
                                                        ed_tab[:, bass.ds(blk[4 * h + j], 1), part, :].rearrange("p o m -> p (o m)"),
                                                        start=part == 0, stop=part == 2)
                                ins.then_inc(found.sem, 1)
                                if not FE:
                                    continue
                                pe.wait_ge(feats_in[h].sem, feats_in[h].at(48 * (i + 1)))
                                for p in range(2):
                                    if not (first and h == 0):
                                        pe.wait_ge(multiplied.sem, multiplied.at(2 * k + p - 1))
                                    for j in (2 * p, 2 * p + 1):
                                        cut, to = slice(j * P, (j + 1) * P), slice((j % 2) * D, (j % 2 + 1) * D)
                                        for part in range(3):
                                            PE.matmul(psum[:, 4 + p, to], hot_d[:, h, cut],
                                                      row(node_parts, blk[4 * h + j])[:, part * D:(part + 1) * D],
                                                      start=part == 0, stop=part == 2)
                                        ins = PE.matmul(psum[:, 6 + p, to], feats[:, h, cut], we_tab[:, :],
                                                        start=True, stop=True)
                                    ins.then_inc(pair_found.sem, 1)
                        over_tiles(pe, turn)

                    if FE:
                        @block.scalar
                        def _(act):
                            def turn(i, first):
                                for h in range(2):
                                    k = 2 * i + h
                                    if not first:
                                        act.wait_ge(q_summed.sem, q_summed.at(k - 1))
                                    for p in range(2):
                                        act.wait_ge(pair_found.sem, pair_found.at(2 * k + p + 1))
                                        A.activation(enc[:, h, 2 * p * D:(2 * p + 2) * D], psum[:, 6 + p, :], ACT.Relu,
                                                     ).then_inc(rectified.sem, 1)
                            over_tiles(act, turn)
            for sig in (hot, found, looked_up, selected, summed):
                sig.phase_ends(2 * TURNS)
            if FE:
                for sig in (pair_found, rectified, multiplied):
                    sig.phase_ends(4 * TURNS)
                for sig in (q_summed, q_added):
                    sig.phase_ends(2 * TURNS)
                for sig in feats_in:
                    sig.phase_ends(48 * TURNS)
                hload.phase_ends(16)
                begun2.phase_ends(1)
                split.phase_ends(1)
            pool_done.phase_ends(1)
            for sig in rows_in:
                sig.phase_ends(32 * TURNS)

        def softmax_phase(L):
            (turned, scanned, all_scanned, gathered, tiles_scanned, spread, spread_in, turned2, shifted, exped, wturned,
             stored, max_done) = flags[:13]
            H, LO = L.heads, L.loops
            with ExitStack() as scope:
                def tmp(name, shape, dt=F32):
                    return scope.enter_context(nc.sbuf_tensor(f"{L.name}_{name}", shape, dt))

                fwd = tmp("fwd", [P, TP])
                bwd = tmp("bwd", [P, TP])
                top = tmp("top", [P, H, TP])
                last_top = tmp("last_top", [P, CH, H])
                first_top = tmp("first_top", [P, CH, H])
                from_left = tmp("from_left", [H, TP + 1])
                from_right = tmp("from_right", [H, TP + 1])
                left_top = tmp("left_top", [P, CH, H])
                right_top = tmp("right_top", [P, CH, H])
                delta = tmp("delta", [P, 2, TP])
                delta_l = tmp("delta_l", [P, 2, TP]) if LO else None

                def turn_edges(pe_ap, bank):
                    for c in range(CH):
                        ins = PE.transpose(psum[:, bank, c * P:(c + 1) * P], pe_ap(c), ident[:, :])
                    return ins

                with nc.Block() as block:
                    @block.gpsimd
                    def _(pool):
                        POOL.memset(acc[:, :, 0:L.cols + HW], 0.0).then_inc(pool_done.sem, 1)

                    @block.tensor
                    def _(pe):
                        for h in range(H):
                            if h >= 2:
                                pe.wait_ge(scanned.sem, scanned.at(h - 1))
                            turn_edges(lambda c: logits[:, h, c * P:(c + 1) * P], h % 2).then_inc(turned.sem, 1)
                        pe.wait_ge(all_scanned.sem, all_scanned.at(1))
                        for k, part in enumerate((last_top, first_top)):
                            for c in range(CH):
                                ins = PE.transpose(psum[0:H, 2 + k, c * P:(c + 1) * P], part[:, c, :], ident[:, :])
                            ins.then_inc(gathered.sem, 1)
                        pe.wait_ge(tiles_scanned.sem, tiles_scanned.at(1))
                        for k, part in enumerate((from_left, from_right)):
                            for c in range(CH):
                                ins = PE.transpose(psum[:, 2 + k, c * H:(c + 1) * H], part[:, c * P + k:(c + 1) * P + k],
                                                   ident[0:H, 0:H])
                        ins.then_inc(spread.sem, 1)

                        def bring(h):
                            if h >= 2:
                                pe.wait_ge(shifted.sem, shifted.at(h - 1))
                            if h == 0:
                                pe.wait_ge(scanned.sem, scanned.at(H))
                            ins = turn_edges(lambda c: logits[:, h, c * P:(c + 1) * P], h % 2)
                            if LO:
                                if h == 0:
                                    pe.wait_ge(spread_in.sem, spread_in.at(1))
                                ins = turn_edges(lambda c: logits[:, H + h, c * P:(c + 1) * P], 2 + h % 2)
                            ins.then_inc(turned2.sem, 1)

                        def take(h):
                            pe.wait_ge(exped.sem, exped.at(h + 1))
                            if h >= 2:
                                pe.wait_ge(stored.sem, stored.at(h - 1))
                            ins = turn_edges(lambda c: delta[:, h % 2, c * P:(c + 1) * P], 4 + h % 2)
                            if LO:
                                ins = turn_edges(lambda c: delta_l[:, h % 2, c * P:(c + 1) * P], 6 + h % 2)
                            ins.then_inc(wturned.sem, 1)
                        bring(0)
                        for h in range(H):
                            if h + 1 < H:
                                bring(h + 1)
                            take(h)

                    @block.vector
                    def _(dve):
                        step = chain(dve, dve_done)
                        for h in range(H):
                            dve.wait_ge(turned.sem, turned.at(h + 1))
                            step(V.tensor_tensor_scan(fwd[:, :], left_pen[:, :], psum[:, h % 2, :], -BIG, ALU.add, ALU.max))
                            V.tensor_tensor_scan(bwd[:, ::-1], right_pen[:, ::-1], psum[:, h % 2, ::-1], -BIG, ALU.add, ALU.max,
                                                 ).then_inc(scanned.sem, 1)
                            dve.wait_ge(scanned.sem, scanned.at(h + 1))
                            step(V.tensor_tensor(top[:, h, :], fwd[:, :], bwd[:, :], ALU.max))
                            step(V.tensor_copy(last_top[:, :, h], fwd[:, P - 1:TP:P]))
                            step(V.tensor_copy(first_top[:, :, h], bwd[:, 0:TP:P]))
                        V.memset(from_left[:, 0:1], -BIG)
                        V.memset(from_right[:, TP:TP + 1], -BIG).then_inc(all_scanned.sem, 1)
                        dve.wait_ge(gathered.sem, gathered.at(2))
                        V.tensor_tensor_scan(from_left[:, 1:TP + 1], tile_left_pen[0:H, :], psum[0:H, 2, :], -BIG,
                                             ALU.add, ALU.max)
                        V.tensor_tensor_scan(from_right[:, TP - 1::-1], tile_right_pen[0:H, ::-1], psum[0:H, 3, ::-1], -BIG,
                                             ALU.add, ALU.max).then_inc(tiles_scanned.sem, 1)
                        dve.wait_ge(spread.sem, spread.at(1))
                        step(V.tensor_copy(left_top[:, :, :].rearrange("p c h -> p (c h)"), psum[:, 2, 0:CH * H]))
                        V.tensor_copy(right_top[:, :, :].rearrange("p c h -> p (c h)"), psum[:, 3, 0:CH * H],
                                      ).then_inc(spread_in.sem, 1)
                        dve.wait_ge(spread_in.sem, spread_in.at(1))
                        for h in range(H):
                            for c in range(CH):
                                cut = slice(c * P, (c + 1) * P)
                                V.scalar_tensor_tensor(top[:, h, cut], left_in[:, cut], left_top[:, c, h:h + 1],
                                                       top[:, h, cut], ALU.add, ALU.max)
                            step(V.memset(fwd[:, 0:1], 0.0))
                            for c in range(CH):
                                cut = slice(c * P, (c + 1) * P)
                                V.scalar_tensor_tensor(top[:, h, cut], right_in[:, cut], right_top[:, c, h:h + 1],
                                                       top[:, h, cut], ALU.add, ALU.max)
                            step(V.memset(fwd[:, 0:1], 0.0))
                            dve.wait_ge(turned2.sem, turned2.at(h + 1))
                            if LO:
                                step(V.tensor_tensor(top[:, h, :], top[:, h, :], psum[:, 2 + h % 2, :], ALU.max))
                            if h >= 2:
                                dve.wait_ge(wturned.sem, wturned.at(h - 1))
                            if LO:
                                V.tensor_tensor(delta_l[:, h % 2, :], psum[:, 2 + h % 2, :], top[:, h, :], ALU.subtract)
                            V.tensor_tensor(delta[:, h % 2, :], psum[:, h % 2, :], top[:, h, :], ALU.subtract,
                                            ).then_inc(shifted.sem, 1)
                            if LO:
                                dve.wait_ge(max_done.sem, max_done.at(h + 1))
                                V.scalar_tensor_tensor(delta_l[:, h % 2, :], delta_l[:, h % 2, :], -1.0, first[:, :],
                                                       ALU.add, ALU.mult).then_inc(exped.sem, 1)
                        dve_done.phase_ends(step.count[0])

                    @block.scalar
                    def _(act):
                        for h in range(H):
                            act.wait_ge(shifted.sem, shifted.at(h + 1))
                            ins = A.activation(delta[:, h % 2, :], delta[:, h % 2, :], ACT.Exp)
                            if LO:
                                A.activation(delta_l[:, h % 2, :], delta_l[:, h % 2, :], ACT.Exp).then_inc(max_done.sem, 1)
                            else:
                                ins.then_inc(exped.sem, 1)
                            act.wait_ge(wturned.sem, wturned.at(h + 1))
                            ins = A.copy(weights[:, :, h], psum[:, 4 + h % 2, 0:T])
                            if LO:
                                ins = A.copy(weights[:, :, H + h], psum[:, 6 + h % 2, 0:T])
                            ins.then_inc(stored.sem, 1)
            for sig in (turned, scanned, turned2, shifted, exped, wturned, stored):
                sig.phase_ends(H)
            if LO:
                max_done.phase_ends(H)
            for sig, n in ((pool_done, 1), (all_scanned, 1), (gathered, 2), (tiles_scanned, 1), (spread, 1), (spread_in, 1)):
                sig.phase_ends(n)

        def gather_phase(L):
            (staged, ready, summed, ran, kept, weighted) = flags[:6]
            H, C, M = L.heads, L.cols, L.wcols
            R = C + M
            with ExitStack() as scope:
                def tmp(name, shape, dt=F32):
                    return scope.enter_context(nc.sbuf_tensor(f"{L.name}_{name}", shape, dt))

                index = tmp("index", [P, 2, 4], U32)
                got = tmp("got", [P, U, R])
                hot = tmp("hot", [P, 4, P])
                running = tmp("running", [P, 4, R])

                def sums_of(s):
                    return psum[:, 2 * s:2 * s + 2, :].rearrange("p b f -> p (b f)")

                with nc.Block() as block:
                    @block.gpsimd
                    def _(pool):
                        def turn(i, first):
                            for h in range(2):
                                pool.wait_ge(staged.sem, staged.at(2 * i + h + 1))
                                stand_alone(pool, passed)
                                for j in range(4):
                                    tile = i * U + 4 * h + j
                                    if not first:
                                        pool.wait_ge(summed.sem, summed.at(tile - U + 1))
                                        stand_alone(pool, passed)
                                    pool.indirect_dma_start(
                                        got[:, 4 * h + j, 0:C], None, table[C],
                                        bass.IndirectOffsetOnAxis(ap=index[:, h, j:j + 1], axis=0),
                                    ).then_inc(ds[4 * h + j].sem, 16)
                        over_tiles(pool, turn)

                    @block.scalar
                    def _(act):
                        for h in range(2):
                            A.copy(index[:, h, :], src_u[:, 4 * h:4 * h + 4]).then_inc(staged.sem, 1)
                        A.copy(got[:, 0:4, C:R], weights[:, 0:4, 0:M]).then_inc(weighted.sem, 1)

                        def turn(i, first, last=False):
                            _, blk = nc.values_load_multi_w_load_instructions(
                                block_of[0:1, bass.ds(i * U, U)], engines=[ACT_ENGINE], min_val=0, max_val=NB - 1,
                                skip_runtime_bounds_check_because="blocks are counted on the chip, below NB")
                            for h in range(2):
                                if not last:
                                    for j in range(4):
                                        act.wait_ge(ds[4 * h + j].sem, ds[4 * h + j].at(16 * (i + 1)))
                                    A.copy(index[:, h, :], src_u[:, bass.ds((i + 1) * U + 4 * h, 4)]).then_inc(staged.sem, 1)
                                if not (last and h == 1):
                                    if not (first and h == 0):
                                        act.wait_ge(summed.sem, summed.at(i * U + 4 * h))
                                    A.copy(got[:, 4 - 4 * h:8 - 4 * h, C:R],
                                           weights[:, bass.ds(i * U + 4 * h + 4, 4), 0:M]).then_inc(weighted.sem, 1)
                                for j in range(4):
                                    act.wait_ge(ran.sem, ran.at(i * U + 4 * h + j + 1))
                                    if not (first and h == 0 and j == 0):
                                        act.wait_ge(kept.sem, kept.at(i * U + 4 * h + j))
                                    A.copy(row(acc, blk[4 * h + j])[:, 0:R], running[:, j, :]).then_inc(kept.sem, 1)
                        turn(0, True)
                        with act.Fori(1, TURNS - 1) as i:
                            turn(i, False)
                        turn(TURNS - 1, False, last=True)

                    @block.vector
                    def _(dve):
                        V.memset(running[:, 3, :], 0.0).then_inc(pool_done.sem, 1)
                        dve.wait_ge(pool_done.sem, pool_done.at(1))

                        def run_on(tile, s, first):
                            dve.wait_ge(summed.sem, summed.at(tile + 1))
                            if not first:
                                dve.wait_ge(ran.sem, ran.at(tile))
                                dve.wait_ge(kept.sem, kept.at(tile - 3))
                            V.scalar_tensor_tensor(running[:, s, :], running[:, (s + 3) % 4, :], keep[:, bass.ds(tile, 1)],
                                                   sums_of(s)[:, 0:R], ALU.mult, ALU.add).then_inc(ran.sem, 1)

                        def turn(i, first):
                            for j in range(U):
                                tile = i * U + j
                                s = j % 4
                                dve.wait_ge(ds[j].sem, ds[j].at(16 * (i + 1)))
                                view = got[:, j, 0:C].rearrange("p (h d) -> p h d", h=H)
                                V.tensor_tensor(view, view, weights[:, bass.ds(tile, 1), 0:H].rearrange(
                                    "p o h -> p (o h)").unsqueeze(2).broadcast_to([P, H, C // H]), ALU.mult)
                                if not (first and j < 4):
                                    dve.wait_ge(summed.sem, summed.at(tile - 3))
                                V.tensor_scalar(hot[:, s, :], iota_row[:, :], dst_in[:, bass.ds(tile, 1)], None,
                                                ALU.is_equal).then_inc(ready.sem, 1)
                                if first and j < 2:
                                    continue
                                if first and j < 6:
                                    if j > 2:
                                        dve.wait_ge(ran.sem, ran.at(tile - 2))
                                    run_on(tile - 2, (s + 2) % 4, True)
                                else:
                                    run_on(tile - 2, (s + 2) % 4, False)
                        over_tiles(dve, turn)
                        run_on(T - 2, 2, False)
                        run_on(T - 1, 3, False)

                    @block.tensor
                    def _(pe):
                        def turn(i, first):
                            for j in range(U):
                                tile = i * U + j
                                s = j % 4
                                if j % 4 == 0:
                                    pe.wait_ge(weighted.sem, weighted.at(2 * i + j // 4 + 1))
                                    stand_alone(pe, passed)
                                pe.wait_ge(ready.sem, ready.at(tile + 1))
                                if not (first and j < 4):
                                    pe.wait_ge(ran.sem, ran.at(tile - 3))
                                for c in range(0, R, BANK):
                                    cut = slice(c, min(c + BANK, R))
                                    ins = PE.matmul(sums_of(s)[:, cut], hot[:, s, :], got[:, j, cut], start=True, stop=True)
                                ins.then_inc(summed.sem, 1)
                        over_tiles(pe, turn)
            for sig in (ready, summed, ran, kept):
                sig.phase_ends(T)
            staged.phase_ends(2 * TURNS)
            weighted.phase_ends(2 * TURNS)
            pool_done.phase_ends(1)
            for sig in ds:
                sig.phase_ends(16 * TURNS)

        def loop_layer_nodes(L, residual):
            H = L.heads
            with ExitStack() as scope:
                def tmp(name, shape, dt=F32):
                    return scope.enter_context(nc.sbuf_tensor(f"{L.name}_{name}", shape, dt))

                b_sb = tmp("b", [P, D])
                inv = tmp("inv", [P, NB, H])
                own = tmp("own_w", [P, NB, H])
                bn = tmp("bn", [P, 6])
                mv = tmp("mv", [P, 2])
                with nc.Block() as block:
                    @block.sync
                    def _(sp):
                        sp.dma_start(b_sb[:, :], t[L.b].broadcast_to([P, D])).then_inc(hload.sem, 16)

                    @block.vector
                    def _(dve):
                        step = chain(dve, dve_done)
                        step(V.scalar_tensor_tensor(own[:, :, :], acc[:, :, D + H:D + 2 * H], 1.0,
                                                    loop_mask[:, :].unsqueeze(2).broadcast_to([P, NB, H]), ALU.add, ALU.mult))
                        step(V.tensor_tensor(inv[:, :, :], own[:, :, :], acc[:, :, D:D + H], ALU.add))
                        step(V.tensor_scalar_max(inv[:, :, :], inv[:, :, :], 1e-30))
                        step(V.reciprocal(inv[:, :, :], inv[:, :, :]))
                        step(V.tensor_tensor(own[:, :, :], own[:, :, :], inv[:, :, :], ALU.mult))
                        dve.wait_ge(hload.sem, hload.at(16))
                        dve_done.phase_ends(5)
                        step = Steps(dve, dve_done, 8 if residual else 7)

                        def heads(ap):
                            return ap.rearrange("p (h d) -> p h d", h=H)

                        def wide(ap, n):
                            return row(ap, n).unsqueeze(2).broadcast_to([P, H, D // H])

                        def one(n, s, first):
                            step.turn(n)
                            sums_n, own_n = row(acc, n)[:, 0:D], row(node_rows, n)
                            step(V.tensor_tensor(heads(sums_n), heads(sums_n), wide(inv, n), ALU.mult))
                            step(V.tensor_tensor(heads(own_n), heads(own_n), wide(own, n), ALU.mult))
                            step(V.tensor_tensor(own_n, own_n, sums_n, ALU.add))
                            step(V.tensor_tensor(own_n, own_n, b_sb[:, :], ALU.add), apart=passed)
                            y = own_n
                            if residual:
                                y = row(x, n)
                                step(V.tensor_tensor(y, y, own_n, ALU.add), apart=passed)
                            row_stats(dve, step, y, n, bn, mv)
                        over_blocks(dve, one)
                        dve_done.phase_ends(step.per * NB)
            hload.phase_ends(16)

        def out_project_nodes(L):
            (scaled, turned, copied, produced, exped, taken) = flags[:6]
            H, C, KO = L.heads, L.cols, L.cols // P
            with ExitStack() as scope:
                def tmp(name, shape, dt=F32):
                    return scope.enter_context(nc.sbuf_tensor(f"{L.name}_{name}", shape, dt))

                w_sb = tmp("wo", [P, KO, D])
                b_sb = tmp("bo", [1, D])
                inv = tmp("inv", [P, NB, H])
                m_sb = tmp("m_sb", [P, 2, C])
                m_t = tmp("m_t", [P, 2, C])
                neg = tmp("neg", [P, 2, D])
                bn = tmp("bn", [P, 6])
                mv = tmp("mv", [P, 2])
                with nc.Block() as block:
                    @block.sync
                    def _(sp):
                        sp.dma_start(w_sb[:, :, :], t["wo"].rearrange("(k p) o -> p k o", p=P)).then_inc(hload.sem, 16)
                        sp.dma_start(b_sb[:, :], t["bo"]).then_inc(hload.sem, 16)

                    @block.vector
                    def _(dve):
                        step = chain(dve, dve_done)
                        step(V.tensor_scalar_add(inv[:, :, :], acc[:, :, C:C + H], 1e-16))
                        step(V.reciprocal(inv[:, :, :], inv[:, :, :]))
                        dve_done.phase_ends(2)
                        step = Steps(dve, dve_done, 6)

                        def early(n, s, first):
                            if not first:
                                dve.wait_ge(turned.sem, turned.at(n - 1))
                            V.tensor_tensor(m_sb[:, s, :].rearrange("p (h d) -> p h d", h=H),
                                            row(acc, n)[:, 0:C].rearrange("p (h d) -> p h d", h=H), row(inv, n).unsqueeze(2).broadcast_to([P, H, C // H]), ALU.mult,
                                            ).then_inc(scaled.sem, 1)

                        def late(n, s, first):
                            step.turn(n)
                            xn = row(x, n)
                            z = psum[:, 2 + s, 0:D]
                            dve.wait_ge(produced.sem, produced.at(n + 1))
                            step(V.tensor_scalar_min(neg[:, s, :], z, 0.0))
                            V.scalar_tensor_tensor(xn, z, 0.0, xn, ALU.max, ALU.add).then_inc(taken.sem, 1)
                            dve.wait_ge(exped.sem, exped.at(n + 1))
                            dve.wait_ge(taken.sem, taken.at(n + 1))
                            step(V.scalar_tensor_tensor(xn, neg[:, s, :], -1.0, xn, ALU.add, ALU.add), apart=passed)
                            row_stats(dve, step, xn, n, bn, mv)

                        def one(n, s, first):
                            early(n, s, first)
                            if not (first and s == 0):
                                late(n - 1, 1 - s, first)
                        step.per = 5
                        over_blocks(dve, one)
                        late(NB - 1, 0, False)
                        dve_done.phase_ends(step.per * NB)

                    @block.tensor
                    def _(pe):
                        pe.wait_ge(hload.sem, hload.at(32))

                        def one(n, s, first):
                            pe.wait_ge(scaled.sem, scaled.at(n + 1))
                            if not first:
                                pe.wait_ge(copied.sem, copied.at(n - 1))
                            for c in range(KO):
                                ins = PE.transpose(psum[:, s, c * P:(c + 1) * P], m_sb[:, s, c * P:(c + 1) * P], ident[:, :])
                            ins.then_inc(turned.sem, 1)
                            pe.wait_ge(copied.sem, copied.at(n + 1))
                            if not first:
                                pe.wait_ge(taken.sem, taken.at(n - 1))
                            for c in range(KO):
                                PE.matmul(psum[:, 2 + s, 0:D], m_t[:, s, c * P:(c + 1) * P], w_sb[:, c, :], start=c == 0, stop=False)
                            PE.matmul(psum[:, 2 + s, 0:D], ones_row[:, :], b_sb[:, :], start=False, stop=True,
                                      ).then_inc(produced.sem, 1)
                        over_blocks(pe, one)

                    @block.scalar
                    def _(act):
                        def copy_in(n, s, first):
                            act.wait_ge(turned.sem, turned.at(n + 1))
                            if not first:
                                act.wait_ge(produced.sem, produced.at(n - 1))
                            A.copy(m_t[:, s, :], psum[:, s, 0:C]).then_inc(copied.sem, 1)

                        def exp_of(n, s):
                            act.wait_ge(taken.sem, taken.at(n + 1))
                            A.activation(neg[:, s, :], neg[:, s, :], ACT.Exp).then_inc(exped.sem, 1)

                        def one(n, s, first):
                            copy_in(n, s, first)
                            if not (first and s == 0):
                                exp_of(n - 1, 1 - s)
                        over_blocks(act, one)
                        exp_of(NB - 1, 0)
            for sig in (scaled, turned, copied, produced, exped, taken):
                sig.phase_ends(NB)
            hload.phase_ends(32)

        def last_layer_nodes(L):
            (stats_in, rooted, normed) = flags[:3]
            H = L.heads
            stored = hs[:2]
            with ExitStack() as scope:
                def tmp(name, shape, dt=F32):
                    return scope.enter_context(nc.sbuf_tensor(f"{L.name}_{name}", shape, dt))

                b_sb = tmp("b", [P, D])
                inv = tmp("inv", [P, NB, H])
                bn = tmp("bn", [P, 6])
                mv = tmp("mv", [P, 2])
                with nc.Block() as block:
                    @block.sync
                    def _(sp):
                        sp.dma_start(b_sb[:, :], t[L.b].broadcast_to([P, D])).then_inc(hload.sem, 16)
                        sp.wait_ge(normed.sem, normed.at(1))
                        sp.dma_start(out[0:(NB - 1) * P, :].rearrange("(n p) d -> p n d", p=P), x[:, 0:NB - 1, :],
                                     ).then_inc(hstore.sem, 16)
                        sp.dma_start(out[(NB - 1) * P:N_NODES, :], x[0:LAST, NB - 1, :]).then_inc(hstore.sem, 16)
                        sp.wait_ge(hstore.sem, hstore.at(32))

                    @block.vector
                    def _(dve):
                        step = chain(dve, dve_done)
                        step(V.tensor_scalar_max(inv[:, :, :], acc[:, :, D:D + H], 1e-10))
                        step(V.reciprocal(inv[:, :, :], inv[:, :, :]))
                        dve.wait_ge(hload.sem, hload.at(16))
                        dve_done.phase_ends(2)
                        step = Steps(dve, dve_done, 6)

                        def one(n, s, first):
                            step.turn(n)
                            sums_n, xn = row(acc, n)[:, 0:D], row(x, n)
                            h3 = sums_n.rearrange("p (h d) -> p h d", h=H)
                            step(V.tensor_tensor(h3, h3, row(inv, n).unsqueeze(2).broadcast_to([P, H, D // H]), ALU.mult))
                            step(V.tensor_tensor(sums_n, sums_n, b_sb[:, :], ALU.add))
                            step(V.tensor_tensor(xn, xn, sums_n, ALU.add), apart=passed)
                            row_stats(dve, step, xn, n, bn, mv)
                        over_blocks(dve, one)
                        dve_done.phase_ends(6 * NB)
                        V.tensor_scalar_add(rstd[:, :], stats[:, :, 1], EPS).then_inc(stats_in.sem, 1)
                        dve.wait_ge(rooted.sem, rooted.at(1))
                        step = chain(dve, dve_done)
                        refine_root(step)
                        dve_done.phase_ends(5)

                        def norm(n, s, first):
                            xn = row(x, n)
                            V.tensor_scalar(xn, xn, stats[:, bass.ds(n, 1), 0], rstd[:, bass.ds(n, 1)], ALU.subtract,
                                            ALU.mult)
                        over_blocks(dve, norm)
                        V.memset(mv[:, :], 0.0).then_inc(normed.sem, 1)

                    @block.scalar
                    def _(act):
                        act.wait_ge(stats_in.sem, stats_in.at(1))
                        A.activation(rstd[:, :], rstd[:, :], ACT.Sqrt).then_inc(rooted.sem, 1)
            for sig, n in ((hload, 16), (hstore, 32), (stats_in, 1), (rooted, 1), (normed, 1)):
                sig.phase_ends(n)

        def attention_layer(L, rows_of, affine):
            with ExitStack() as scope:
                es_tab = scope.enter_context(nc.sbuf_tensor(f"{L.name}_es_tab", [P, 3, NB * L.heads], BF16))
                ed_tab = scope.enter_context(nc.sbuf_tensor(f"{L.name}_ed_tab", [P, NB, 3, L.wcols], BF16))
                project(L, rows_of, affine, es_tab, ed_tab)
                logit_phase(L, es_tab, ed_tab)
                softmax_phase(L)
                gather_phase(L)

        gat_a = Layer("gat_a", 4, D, loops=True, w="w1", a=("a1s", "a1d"), b="b1")
        gat_b = Layer("gat_b", 1, D, loops=True, w="w2", a=("a2s", "a2d"), b="b2")
        gat_8 = Layer("gat_8", 8, 2 * D, w="w3", a=("a3s", "a3d"))
        gat_e = Layer("gat_e", 8, D, edge_feats=True, w="w4", a=("a4s", "a4d"), b="b4")

        order_phase()
        edge_phase()
        scatter_phase()
        first_layer_nodes()
        if stop == 0:
            return debug(nc, dict(locals()), out)
        attention_layer(gat_a, lambda n: row(x, n), False)
        loop_layer_nodes(gat_a, residual=False)
        if stop == 1:
            return debug(nc, dict(locals()), out)
        attention_layer(gat_b, lambda n: row(node_rows, n), True)
        loop_layer_nodes(gat_b, residual=True)
        if stop == 2:
            return debug(nc, dict(locals()), out)
        attention_layer(gat_8, lambda n: row(x, n), False)
        out_project_nodes(gat_8)
        if stop == 3:
            return debug(nc, dict(locals()), out)
        attention_layer(gat_e, lambda n: row(x, n), False)
        last_layer_nodes(gat_e)


_OUT = "out_dram"


def _layout(i):
    def a(n):
        return np.asarray(i[n])

    def row(n):
        return np.ascontiguousarray(a(n).reshape(1, -1))

    pad = ROWS - N_EDGES
    ids = np.stack([np.pad(a("src"), (0, pad)), np.pad(a("dst"), (0, pad), constant_values=NO_NODE)], axis=1)
    vals = np.concatenate([np.pad(a("edge_weight"), (0, pad))[:, None], np.pad(a("edge_attr_3"), ((0, pad), (0, 0)))], axis=1)
    H3 = a("L2_gnn_a").shape[1] // 2
    chunk = np.concatenate([a("L3_gnn_edge_W").T] * 3 + [row("L3_gnn_edge_b"), np.zeros((FEAT_ROWS // 3 - 10, D), np.float32)])
    we = np.ascontiguousarray(np.concatenate([chunk] * 3))
    return {
        "x": a("x"),
        "edge_ids": np.ascontiguousarray(ids),
        "edge_vals": np.ascontiguousarray(vals),
        "dst_list": np.pad(a("dst"), (0, pad), constant_values=NO_NODE).reshape(1, ROWS),
        "w0": np.ascontiguousarray(a("L0_gnn_W").T), "b0": row("L0_gnn_b"),
        "w1": a("L1_gnn_W1"), "a1s": row("L1_gnn_a1_src"), "a1d": row("L1_gnn_a1_dst"), "b1": row("L1_gnn_b1"),
        "ln_g": row("L1_gnn_ln_g"), "ln_b": row("L1_gnn_ln_b"),
        "w2": a("L1_gnn_W2"), "a2s": row("L1_gnn_a2_src"), "a2d": row("L1_gnn_a2_dst"), "b2": row("L1_gnn_b2"),
        "w3": np.ascontiguousarray(a("L2_gnn_W").transpose(1, 0, 2).reshape(D, -1)),
        "a3s": np.ascontiguousarray(a("L2_gnn_a")[:, :H3].reshape(1, -1)),
        "a3d": np.ascontiguousarray(a("L2_gnn_a")[:, H3:].reshape(1, -1)),
        "wo": a("L2_gnn_Wo"), "bo": row("L2_gnn_bo"),
        "w4": np.ascontiguousarray(a("L3_gnn_W").T), "a4s": row("L3_gnn_a_src"), "a4d": row("L3_gnn_a_dst"),
        "we": we, "b4": row("L3_gnn_bias"),
    }


def kernel(**inputs):
    import concourse.bacc as bacc
    from concourse.bass_utils import run_bass_kernel_spmd

    nc = bacc.Bacc("TRN2", target_bir_lowering=False, num_devices=1)
    arrays = _layout(inputs)
    given = {n: nc.dram_tensor(f"in_{n}", a.shape, mybir.dt.from_np(a.dtype), kind="ExternalInput").ap()
             for n, a in arrays.items()}
    out = nc.dram_tensor(_OUT, (N_NODES, D), F32, kind="ExternalOutput").ap()
    gnn_kernel(nc, given, out)
    r = run_bass_kernel_spmd(nc, [{f"in_{n}": a for n, a in arrays.items()}], core_ids=[0])
    return r.results[0][_OUT]
```

```python
from contextlib import ExitStack

import concourse.bass as bass
import numpy as np
from concourse import mybir

F32 = mybir.dt.float32
BF16 = mybir.dt.bfloat16
I32 = mybir.dt.int32
U32 = mybir.dt.uint32
U8 = mybir.dt.uint8
ALU = mybir.AluOpType
ACT = mybir.ActivationFunctionType
AX = mybir.AxisListType.X
DVE_ENGINE = mybir.EngineType.DVE
PE_ENGINE = mybir.EngineType.PE
ACT_ENGINE = mybir.EngineType.Activation

P = 128
N_NODES = 3125
D = 256
KC = D // P
NB = -(-N_NODES // P)
FEAT_ROWS = 96
LAST = N_NODES - (NB - 1) * P
N_LOOPS = 625
N_EDGES = 50000
COLS = -(-N_EDGES // P)
E_PAD = COLS * P
ROWS = E_PAD + P
U = 8
T = -(-(N_EDGES // P + NB) // U) * U
TURNS = T // U
assert TURNS % 2 == 0
CH = 4
TP = CH * P
NO_NODE = NB * P
G = 5
assert NB % G == 0
BANK = 512
BIG = 1e30
EPS = 1e-5
HW = 8
ACCS = 4
DUMP = NB * P
assert T <= TP and ROWS >= N_EDGES + P


class Signal:

    def __init__(self, sem):
        self.sem = sem
        self.base = 0

    def at(self, count):
        return count + self.base

    def phase_ends(self, counted):
        self.base += counted


def chain(engine, sig):
    count = [0]

    def step(ins):
        count[0] += 1
        ins.then_inc(sig.sem, 1)
        engine.wait_ge(sig.sem, sig.at(count[0]))
        return count[0]

    step.count = count
    return step


def stand_alone(engine, passed):
    engine.sem_inc(passed.sem, 1)


class Steps:

    def __init__(self, engine, sig, per):
        self.engine, self.sig, self.per = engine, sig, per

    def turn(self, n):
        self.n, self.c = n, 0

    def __call__(self, ins, apart=None):
        self.c += 1
        assert self.c <= self.per
        ins.then_inc(self.sig.sem, 1)
        self.engine.wait_ge(self.sig.sem, self.sig.at(self.n * self.per + self.c))
        if apart is not None:
            stand_alone(self.engine, apart)


def over_tiles(engine, turn):
    turn(0, True)
    with engine.Fori(1, TURNS) as i:
        turn(i, False)


def over_double_turns(engine, turn):
    turn(0, True)
    with engine.Fori(1, TURNS // 2) as i:
        turn(i, False)


def slot_turn(n, slot):
    return n // 2 + 1 if isinstance(n, int) else (n + 2 - slot) // 2


def over_blocks(engine, one):
    one(0, 0, True)
    one(1, 1, True)
    with engine.Fori(1, NB // 2) as i:
        one(2 * i, 0, False)
        one(2 * i + 1, 1, False)
    one(NB - 1, 0, False)


def over_blocks_ahead(engine, begin, end):
    begin(0, 0, True)
    begin(1, 1, True)
    end(0, 0, True)
    begin(2, 0, False)
    end(1, 1, True)
    with engine.Fori(1, NB // 2) as i:
        begin(2 * i + 1, 1, False)
        end(2 * i, 0, False)
        begin(2 * i + 2, 0, False)
        end(2 * i + 1, 1, False)
    end(NB - 1, 0, False)


def over_blocks_two_ahead(engine, begin, end):
    for n in range(3):
        begin(n, n % 2, n < 2)
    end(0, 0, True)
    begin(3, 1, False)
    end(1, 1, True)
    with engine.Fori(1, NB // 2 - 1) as i:
        begin(2 * i + 2, 0, False)
        end(2 * i, 0, False)
        begin(2 * i + 3, 1, False)
        end(2 * i + 1, 1, False)
    begin(NB - 1, 0, False)
    end(NB - 3, 0, False)
    end(NB - 2, 1, False)
    end(NB - 1, 0, False)


class Layer:
    def __init__(self, name, heads, cols, w, a, b=None, loops=False, edge_feats=False):
        self.name, self.heads, self.cols, self.w, self.a, self.b = name, heads, cols, w, a, b
        self.loops, self.edge_feats = loops, edge_feats
        self.wcols = 2 * heads if loops else heads


def gnn_kernel(nc, t, out, debug=None, stop=None):
    ctx = ExitStack()
    with ctx:
        def dram(name, shape, dt):
            return nc.dram_tensor(name, shape, dt, kind="Internal").ap()

        def sb(name, shape, dt=F32):
            return ctx.enter_context(nc.sbuf_tensor(name, shape, dt))

        def signal(name):
            return Signal(ctx.enter_context(nc.semaphore(name)))

        edge_ids = dram("edge_ids", [ROWS, 2], I32)
        edge_vals = dram("edge_vals", [ROWS, 4], F32)
        table = {w: dram(f"table{w}", [NB * P, w], F32) for w in (D, 2 * D)}
        sums = [dram(f"sums{k}", [DUMP + P, D], F32) for k in range(ACCS)]
        dst_rows = dram("dst_rows", [1, TP * P], BF16)
        src_rows = dram("src_rows", [1, TP * P], BF16)
        src_ids = dram("src_ids", [1, TP * P], F32)
        feat_rows = dram("feat_rows", [9, TP * P], BF16)
        key_list = dram("key_list", [1, E_PAD], F32)
        block_row = dram("block_row", [1, TP], I32)
        ends = dram("ends", [2, TP + 2], F32)

        x = sb("x", [P, NB, D])
        acc = sb("acc", [P, NB, 2 * D + HW])
        node_rows = acc[:, :, D + HW:2 * D + HW]
        node_parts = acc[:, :, 0:3 * D // 2].bitcast(BF16)
        logits = sb("logits", [P, 8, TP])
        weights = sb("weights", [P, T, HW])
        ones_row = sb("ones_row", [1, P])
        stats = sb("stats", [P, NB, 2])
        rstd = sb("rstd", [P, NB])
        root_t = sb("root_t", [P, NB])
        att = sb("att", [P, NB, 2 * HW])
        src_hot = sb("src_hot", [P, T, NB], U8)
        src_u = sb("src_u", [P, T], U32)
        dst_in = sb("dst_in", [P, TP])
        src_f = sb("src_f", [P, TP])
        edge_w = sb("edge_w", [P, TP])
        keep = sb("keep", [P, T])
        block_of = sb("block_of", [1, TP], I32)
        loop_mask = sb("loop_mask", [P, NB])
        loop_pen = sb("loop_pen", [P, NB])
        ident = sb("ident", [P, P])
        iota_row = sb("iota_row", [P, P])
        iota_col = sb("iota_col", [P, 1])
        left_pen = sb("left_pen", [P, TP])
        right_pen = sb("right_pen", [P, TP])
        left_in = sb("left_in", [P, TP])
        right_in = sb("right_in", [P, TP])
        first = sb("first", [P, TP])
        tile_left_pen = sb("tile_left_pen", [8, TP])
        tile_right_pen = sb("tile_right_pen", [8, TP])

        psum = ctx.enter_context(nc.psum_tensor("psum", [P, 8, 512], F32))

        ds = [signal(f"sw_dma_{i}") for i in range(8)]
        hs = [signal(f"sp_dma_{i}") for i in range(8)]
        hload = signal("load_landed")
        hstore = signal("store_landed")
        hload2 = signal("load2_landed")
        dve_done = signal("dve_done")
        act_done = signal("act_done")
        pe_done = signal("pe_done")
        pool_done = signal("pool_done")
        dve_b = signal("dve_b_done")
        act_b = signal("act_b_done")
        pe_b = signal("pe_b_done")
        flags = [signal(f"flag_{i}") for i in range(16)]
        begun2 = signal("feats_ready")
        passed = signal("waits_passed")
        order_rows = signal("order_rows_loaded")
        order_keyed = signal("order_keys_made")
        order_key = signal("order_keys_stored")
        order_in = signal("order_chunk_landed")
        order_ranked = signal("order_chunk_counted")
        order_step = signal("order_step_done")
        order_staged = signal("order_column_staged")
        order_out = signal("order_column_scattered")
        every = [*flags, *ds, *hs, hload, hstore, hload2, dve_done, act_done, pe_done, pool_done, dve_b, act_b, pe_b]


        V, A, PE, POOL, SP = nc.vector, nc.scalar, nc.tensor, nc.gpsimd, nc.sync

        def tiles_first(ap):
            return ap.rearrange("o (c p i) -> p (o c) i", c=CH, p=P)

        def row(ap, n):
            return ap[:, bass.ds(n, 1), :].rearrange("p o d -> p (o d)")

        def order_phase():
            (loaded, copied, keyed, key_stored, chunk_in, scattered) = (hload, hstore, flags[0], hs[0], order_in, ds[0])
            (counted, flagged, ones_set, staged, ranked) = (flags[1], flags[2], flags[3], order_staged, order_ranked)
            CHUNK = E_PAD // 8
            with ExitStack() as scope:
                def tmp(name, shape, dt=F32):
                    return scope.enter_context(nc.sbuf_tensor(name, shape, dt))

                dst_i = tmp("order_dst", [P, 2, COLS], I32)
                dst_f = tmp("order_dst_f", [P, 2, COLS])
                falls = tmp("order_falls", [P, COLS])
                n_falls = tmp("order_n_falls", [P, 1])
                ones = tmp("order_ones", [P, P])
                flag_f = tmp("order_flag_f", [P, 1])
                flag_i = tmp("order_flag_i", [P, 1], I32)
                key = tmp("order_key", [P, COLS])
                rank = tmp("order_rank", [P, COLS])
                column_i = tmp("order_column_i", [P, COLS], I32)
                column = tmp("order_column", [P, COLS])
                less = tmp("order_less", [P, COLS])
                count = tmp("order_count", [P, 2])
                lane_i = tmp("order_lane_i", [P, 1], I32)
                lane = tmp("order_lane", [P, 1])
                ids = tmp("order_ids", [P, COLS, 2], I32)
                vals = tmp("order_vals", [P, COLS, 4])
                one_rank = tmp("order_one_rank", [P, 1], U32)
                one_ids = tmp("order_one_ids", [P, 2], I32)
                one_vals = tmp("order_one_vals", [P, 4])
                room = acc[:, :, :].rearrange("p n d -> p (n d)")
                chunk, junk = room[:, 0:CHUNK], room[:, CHUNK:2 * CHUNK]

                def flat(ap, rows, per):
                    return ap[0:rows, :].rearrange("(p r) f -> p r f", p=P)

                def unsorted(engine):
                    return engine.If(engine.value_load(flag_i[0:1, 0:1], min_val=0, max_val=1) > 0)

                with nc.Block() as block:
                    @block.sync
                    def _(sp):
                        sp.dma_start(dst_i[:, 0, :], t["dst_list"][0:1, 0:E_PAD].rearrange("o (p c) -> (o p) c", p=P),
                                     ).then_inc(loaded.sem, 16)
                        sp.dma_start(dst_i[:, 1, :], t["dst_list"][0:1, 1:E_PAD + 1].rearrange("o (p c) -> (o p) c", p=P),
                                     ).then_inc(loaded.sem, 16)
                        for to, of in ((edge_ids, t["edge_ids"]), (edge_vals, t["edge_vals"])):
                            sp.dma_start(flat(to, ROWS, 0).rearrange("p r f -> p (r f)"),
                                         flat(of, ROWS, 0).rearrange("p r f -> p (r f)")).then_inc(copied.sem, 16)
                        sp.wait_ge(copied.sem, copied.at(32))
                        sp.wait_ge(flagged.sem, flagged.at(1))
                        with unsorted(sp):
                            sp.dma_start(ids[:, :, :], flat(t["edge_ids"], E_PAD, 0)).then_inc(order_rows.sem, 16)
                            sp.dma_start(vals[:, :, :], flat(t["edge_vals"], E_PAD, 0)).then_inc(order_rows.sem, 16)
                            sp.wait_ge(order_keyed.sem, order_keyed.at(1))
                            sp.dma_start(key_list.rearrange("o (p c) -> (o p) c", p=P), key[:, :]).then_inc(order_key.sem, 16)
                            sp.wait_ge(order_key.sem, order_key.at(16))
                            with sp.Fori(0, E_PAD // CHUNK) as c:
                                sp.wait_ge(ranked.sem, ranked.at(c + 1))
                                sp.dma_start(chunk, key_list[0:1, bass.ds(c * CHUNK, CHUNK)].broadcast_to([P, CHUNK]),
                                             ).then_inc(chunk_in.sem, 16)
                            sp.wait_ge(order_rows.sem, order_rows.at(32))

                    @block.gpsimd
                    def _(pool):
                        step = chain(pool, pool_done)
                        step(POOL.iota(column_i[:, :], [[1, COLS]], base=0, channel_multiplier=0))
                        step(POOL.tensor_copy(column[:, :], column_i[:, :]))
                        step(POOL.iota(lane_i[:, :], [[1, 1]], base=0, channel_multiplier=1))
                        step(POOL.tensor_copy(lane[:, :], lane_i[:, :]))
                        POOL.memset(ones[:, :], 1.0).then_inc(ones_set.sem, 1)
                        pool.wait_ge(flagged.sem, flagged.at(1))
                        with unsorted(pool):
                            with pool.Fori(0, COLS) as j:
                                pool.wait_ge(staged.sem, staged.at(j + 1))
                                stand_alone(pool, passed)
                                pool.indirect_dma_start(
                                    edge_ids, bass.IndirectOffsetOnAxis(ap=one_rank[:, :], axis=0), one_ids[:, :], None,
                                ).then_inc(order_out.sem, 16)
                                pool.indirect_dma_start(
                                    edge_vals, bass.IndirectOffsetOnAxis(ap=one_rank[:, :], axis=0), one_vals[:, :], None,
                                ).then_inc(order_out.sem, 16)
                                pool.wait_ge(order_out.sem, order_out.at(32 * (j + 1)))
                                stand_alone(pool, passed)

                    @block.tensor
                    def _(pe):
                        pe.wait_ge(ones_set.sem, ones_set.at(1))
                        pe.wait_ge(counted.sem, counted.at(1))
                        PE.matmul(psum[:, 0, 0:1], ones[:, :], n_falls[:, :], start=True, stop=True).then_inc(keyed.sem, 1)

                    @block.vector
                    def _(dve):
                        step = chain(dve, dve_done)
                        dve.wait_ge(loaded.sem, loaded.at(32))
                        step(V.tensor_copy(dst_f[:, :, :], dst_i[:, :, :]))
                        step(V.tensor_tensor(falls[:, :], dst_f[:, 0, :], dst_f[:, 1, :], ALU.is_gt))
                        V.reduce_sum(n_falls[:, :], falls[:, :], AX).then_inc(counted.sem, 1)
                        dve.wait_ge(keyed.sem, keyed.at(1))
                        step(V.tensor_scalar_min(flag_f[:, :], psum[:, 0, 0:1], 1.0))
                        V.tensor_copy(flag_i[:, :], flag_f[:, :]).then_inc(flagged.sem, 1)
                        dve_done.phase_ends(step.count[0])
                        dve.wait_ge(flagged.sem, flagged.at(1))
                        with unsorted(dve):
                            V.tensor_scalar(key[:, :], dst_f[:, 0, :], float(P), lane[:, :], ALU.mult, ALU.add,
                                            ).then_inc(order_keyed.sem, 1)
                            V.memset(rank[:, :], 0.0).then_inc(ranked.sem, 1)
                            dve.wait_ge(order_keyed.sem, order_keyed.at(1))
                            with dve.Fori(0, E_PAD // CHUNK) as c:
                                dve.wait_ge(chunk_in.sem, chunk_in.at(16 * (c + 1)))
                                stand_alone(dve, passed)
                                with dve.Fori(0, COLS) as j:
                                    V.tensor_scalar(junk, chunk, key[:, bass.ds(j, 1)], 0.0, ALU.is_lt, ALU.add,
                                                    accum_out=count[:, 0:1]).then_inc(order_step.sem, 1)
                                    dve.wait_ge(order_step.sem, order_step.at(c * (2 * COLS) + j * 2 + 1))
                                    V.tensor_tensor(rank[:, bass.ds(j, 1)], rank[:, bass.ds(j, 1)], count[:, 0:1], ALU.add,
                                                    ).then_inc(order_step.sem, 1)
                                    dve.wait_ge(order_step.sem, order_step.at(c * (2 * COLS) + j * 2 + 2))
                                V.memset(count[:, 0:1], 0.0).then_inc(ranked.sem, 1)
                            dve.wait_ge(order_rows.sem, order_rows.at(32))
                            done = E_PAD // CHUNK * 2 * COLS
                            with dve.Fori(0, COLS) as j:
                                V.tensor_scalar(less[:, :], column[:, :], column[:, bass.ds(j, 1)], None, ALU.is_lt,
                                                ).then_inc(order_step.sem, 1)
                                dve.wait_ge(order_step.sem, order_step.at(done + j * 2 + 1))
                                V.scalar_tensor_tensor(junk[:, 0:COLS], dst_f[:, 0, :], dst_f[:, 0, bass.ds(j, 1)], less[:, :],
                                                       ALU.is_equal, ALU.mult, accum_out=count[:, 1:2]).then_inc(order_step.sem, 1)
                                dve.wait_ge(order_step.sem, order_step.at(done + j * 2 + 2))
                                V.tensor_tensor(one_rank[:, :], rank[:, bass.ds(j, 1)], count[:, 1:2], ALU.add)
                                V.tensor_copy(one_ids[:, :], row(ids, j))
                                V.tensor_copy(one_vals[:, :], row(vals, j)).then_inc(staged.sem, 1)
                                dve.wait_ge(staged.sem, staged.at(j + 1))
                                dve.wait_ge(order_out.sem, order_out.at(32 * (j + 1)))
                                stand_alone(dve, passed)
            for sig, n in ((loaded, 32), (copied, 32), (keyed, 1), (counted, 1), (flagged, 1), (ones_set, 1), (pool_done, 4)):
                sig.phase_ends(n)

        def edge_phase():
            (loaded, gathered, rows_out, rows_in, feats_out) = (hload, ds[0], hs[0], hs[1], hs[2])
            (consts, counted, totalled, placed, tiled, ends_ready, t_ready, feats_split, int_consts) = flags[:9]
            with ExitStack() as scope:
                def tmp(name, shape, dt=F32):
                    return scope.enter_context(nc.sbuf_tensor(name, shape, dt))

                dst_cols = tmp("dst_cols", [P, COLS], I32)
                dst_f = tmp("dst_f", [P, COLS])
                below = tmp("below", [P, COLS])
                cnt = tmp("cnt", [P, NB])
                ones = tmp("ones", [P, P])
                start = tmp("start", [P, NB + 1])
                size = tmp("size", [P, NB])
                size_i = tmp("size_i", [P, NB], I32)
                n_tiles = tmp("n_tiles", [P, NB])
                tile0 = tmp("tile0", [P, NB + 1])
                shift = tmp("shift", [P, NB])
                dshift = tmp("dshift", [P, NB - 1])
                tile_i = tmp("tile_i", [P, CH], I32)
                tile_no = tmp("tile_no", [P, CH])
                past = tmp("past", [P, CH, NB - 1])
                prod = tmp("prod", [P, CH, NB - 1])
                block_t = tmp("block_t", [P, CH])
                block_i = tmp("block_i", [P, CH], I32)
                edge0 = tmp("edge0", [P, CH])
                valid = tmp("valid", [P, CH])
                clamped = tmp("clamped", [P, CH])
                edge0_u = tmp("edge0_u", [P, CH], U32)
                ids_t = tmp("ids_t", [P, CH, 2 * P], I32)
                vals_t = tmp("vals_t", [P, CH, 4 * P])
                iota_i = tmp("iota_i", [P, P], I32)
                dst_g = tmp("dst_g", [P, CH, P])
                dst_l = tmp("dst_l", [P, CH, P])
                inside = tmp("inside", [P, CH, P])
                src_i = tmp("src_i", [P, CH, P], I32)
                src_t = tmp("src_t", [P, CH, P])
                src_lo = tmp("src_lo", [P, CH, P])
                src_hi = tmp("src_hi", [P, CH, P])
                src_hi_e = tmp("src_hi_e", [P, TP])
                w_t = tmp("w_t", [P, CH, P])
                feat_t = tmp("feat_t", [P, 3, CH, P])
                room = acc[:, :, :].rearrange("p n d -> p (n d)")
                feat_b = room[:, 0:9 * TP // 2].bitcast(BF16).rearrange("p (a k c i) -> p a k c i", a=3, k=3, c=CH)
                src_lo_b = tmp("src_lo_b", [P, CH, P], BF16)
                dst_l_b = tmp("dst_l_b", [P, CH, P], BF16)
                same = tmp("same", [P, CH, P])
                prev_last = tmp("prev_last", [P, CH])
                next_first = tmp("next_first", [P, CH])
                none = tmp("none", [1, 2])
                firsts = tmp("firsts", [8, TP + 1])
                lasts = tmp("lasts", [8, TP + 1])
                first_c = tmp("first_c", [P, CH])
                last_c = tmp("last_c", [P, CH])
                prev_block = tmp("prev_block", [P, CH])
                keep_row = tmp("keep_row", [1, TP])
                block_f = tmp("block_f", [1, TP + 1])

                lp3 = left_pen[:, :].rearrange("p (c i) -> p c i", c=CH)
                rp3 = right_pen[:, :].rearrange("p (c i) -> p c i", c=CH)
                li3 = left_in[:, :].rearrange("p (c i) -> p c i", c=CH)
                ri3 = right_in[:, :].rearrange("p (c i) -> p c i", c=CH)
                fi3 = first[:, :].rearrange("p (c i) -> p c i", c=CH)
                turned = [src_t, dst_l, w_t, src_hi]

                with nc.Block() as block:
                    @block.sync
                    def _(sp):
                        sp.dma_start(dst_cols[:, :], t["dst_list"][0:1, 0:E_PAD].rearrange("o (p c) -> (o p) c", p=P)).then_inc(loaded.sem, 16)
                        sp.wait_ge(tiled.sem, tiled.at(1))
                        sp.dma_start(tiles_first(dst_rows), dst_l_b[:, :, :]).then_inc(rows_out.sem, 16)
                        sp.dma_start(tiles_first(src_rows), src_lo_b[:, :, :]).then_inc(rows_out.sem, 16)
                        sp.dma_start(tiles_first(src_ids), src_t[:, :, :]).then_inc(rows_out.sem, 16)
                        sp.dma_start(block_row.rearrange("o (c p) -> p (o c)", p=P), block_i[:, :], allow_slow_non_contiguous=True).then_inc(rows_out.sem, 16)
                        sp.dma_start(ends[0:1, 1:TP + 1].rearrange("o (c p) -> p (o c)", p=P), first_c[:, :], allow_slow_non_contiguous=True).then_inc(rows_out.sem, 16)
                        sp.dma_start(ends[1:2, 1:TP + 1].rearrange("o (c p) -> p (o c)", p=P), last_c[:, :], allow_slow_non_contiguous=True).then_inc(rows_out.sem, 16)
                        sp.dma_start(ends[0:1, TP + 1:TP + 2], none[:, 0:1]).then_inc(rows_out.sem, 16)
                        sp.dma_start(ends[1:2, 0:1], none[:, 1:2]).then_inc(rows_out.sem, 16)
                        sp.wait_ge(rows_out.sem, rows_out.at(16 * 8))
                        sp.dma_start(prev_last[:, :], ends[1:2, 0:TP].rearrange("o (c p) -> p (o c)", p=P),
                                     allow_slow_non_contiguous=True).then_inc(rows_in.sem, 16)
                        sp.dma_start(next_first[:, :], ends[0:1, 2:TP + 2].rearrange("o (c p) -> p (o c)", p=P),
                                     allow_slow_non_contiguous=True).then_inc(rows_in.sem, 16)
                        sp.dma_start(firsts[:, :], ends[0:1, 1:TP + 2].broadcast_to([8, TP + 1])).then_inc(rows_in.sem, 16)
                        sp.dma_start(lasts[:, :], ends[1:2, 0:TP + 1].broadcast_to([8, TP + 1])).then_inc(rows_in.sem, 16)
                        sp.dma_start(block_of[:, :], block_row).then_inc(rows_in.sem, 16)
                        sp.wait_ge(feats_split.sem, feats_split.at(1))
                        for k in range(9):
                            sp.dma_start(tiles_first(feat_rows[k:k + 1, :]), feat_b[:, k // 3, k % 3, :, :]).then_inc(feats_out.sem, 16)
                        sp.wait_ge(rows_in.sem, rows_in.at(16 * 5))
                        sp.wait_ge(feats_out.sem, feats_out.at(16 * 9))

                    @block.gpsimd
                    def _(pool):
                        step = chain(pool, pool_done)
                        step(POOL.iota(tile_i[:, :], [[P, CH]], base=0, channel_multiplier=1))
                        step(POOL.iota(iota_i[:, :], [[1, P]], base=0, channel_multiplier=0))
                        step(POOL.tensor_copy(tile_no[:, :], tile_i[:, :]))
                        step(POOL.tensor_copy(iota_col[:, :], tile_i[:, 0:1]))
                        step(POOL.memset(ones[:, :], 1.0))
                        POOL.tensor_copy(iota_row[:, :], iota_i[:, :]).then_inc(consts.sem, 1)
                        pool.wait_ge(consts.sem, consts.at(1))
                        POOL.tensor_scalar(ident[:, :], iota_row[:, :], iota_col[:, :], None, ALU.is_equal,
                                           ).then_inc(int_consts.sem, 1)
                        pool.wait_ge(placed.sem, placed.at(1))
                        for c in range(CH):
                            pool.indirect_dma_start(
                                ids_t[:, c, :], None, edge_ids,
                                bass.IndirectOffsetOnAxis(ap=edge0_u[:, c:c + 1], axis=0)).then_inc(gathered.sem, 16)
                            pool.indirect_dma_start(
                                vals_t[:, c, :], None, edge_vals,
                                bass.IndirectOffsetOnAxis(ap=edge0_u[:, c:c + 1], axis=0)).then_inc(gathered.sem, 16)
                        pool.wait_ge(gathered.sem, gathered.at(16 * 2 * CH))

                    @block.vector
                    def _(dve):
                        step = chain(dve, dve_done)
                        dve.wait_ge(loaded.sem, loaded.at(16))
                        step(V.tensor_copy(dst_f[:, :], dst_cols[:, :]))
                        for n in range(NB):
                            step(V.tensor_scalar(below[:, :], dst_f[:, :], float((n + 1) * P), 0.0, ALU.is_lt, ALU.add,
                                                 accum_out=cnt[:, n:n + 1]))
                        V.memset(start[:, 0:1], 0.0).then_inc(counted.sem, 1)
                        dve.wait_ge(totalled.sem, totalled.at(1))
                        step(V.tensor_copy(start[:, 1:NB + 1], psum[:, 0, 0:NB]))
                        step(V.tensor_tensor(size[:, :], start[:, 1:NB + 1], start[:, 0:NB], ALU.subtract))
                        step(V.tensor_scalar_add(size_i[:, :], size[:, :], float(P - 1)))
                        step(V.tensor_single_scalar(size_i[:, :], size_i[:, :], P.bit_length() - 1, ALU.arith_shift_right))
                        step(V.tensor_copy(n_tiles[:, :], size_i[:, :]))
                        step(V.memset(tile0[:, 0:1], 0.0))
                        dve.wait_ge(consts.sem, consts.at(1))
                        step(V.tensor_tensor_scan(tile0[:, 1:NB + 1], ones[:, 0:NB], n_tiles[:, :], 0.0, ALU.mult, ALU.add))
                        step(V.scalar_tensor_tensor(shift[:, :], tile0[:, 0:NB], float(-P), start[:, 0:NB], ALU.mult, ALU.add))
                        step(V.tensor_tensor(dshift[:, :], shift[:, 1:NB], shift[:, 0:NB - 1], ALU.subtract))
                        for c in range(CH):
                            step(V.tensor_scalar(past[:, c, :], tile0[:, 1:NB], tile_no[:, c:c + 1], None, ALU.is_le))
                        step(V.reduce_sum(block_t[:, :], past[:, :, :], AX))
                        step(V.tensor_tensor(prod[:, :, :], past[:, :, :],
                                             dshift[:, :].unsqueeze(1).broadcast_to([P, CH, NB - 1]), ALU.mult))
                        step(V.reduce_sum(edge0[:, :], prod[:, :, :], AX))
                        step(V.tensor_tensor(prod[:, :, :], past[:, :, :],
                                             size[:, 1:NB].unsqueeze(1).broadcast_to([P, CH, NB - 1]), ALU.mult))
                        step(V.reduce_sum(valid[:, :], prod[:, :, :], AX))
                        step(V.scalar_tensor_tensor(edge0[:, :], tile_no[:, :], float(P), edge0[:, :], ALU.mult, ALU.add))
                        step(V.scalar_tensor_tensor(valid[:, :], valid[:, :], start[:, 1:2], edge0[:, :], ALU.add, ALU.subtract))
                        step(V.tensor_scalar_min(clamped[:, :], edge0[:, :], float(ROWS - P)))
                        V.tensor_copy(edge0_u[:, :], clamped[:, :]).then_inc(placed.sem, 1)
                        step(V.tensor_copy(block_i[:, :], block_t[:, :]))
                        for c in range(CH):
                            step(V.tensor_scalar(inside[:, c, :], iota_row[:, :], valid[:, c:c + 1], None, ALU.is_lt))
                        dve.wait_ge(gathered.sem, gathered.at(16 * 2 * CH))
                        ids = ids_t[:, :, :].rearrange("p c (i f) -> p c i f", f=2)
                        vals = vals_t[:, :, :].rearrange("p c (i f) -> p c i f", f=4)
                        step(V.tensor_copy(src_i[:, :, :], ids[:, :, :, 0]))
                        step(V.tensor_copy(dst_g[:, :, :], ids[:, :, :, 1]))
                        step(V.tensor_copy(src_t[:, :, :], src_i[:, :, :]))
                        step(V.tensor_single_scalar(src_i[:, :, :], src_i[:, :, :], P - 1, ALU.bitwise_and))
                        step(V.tensor_copy(src_lo[:, :, :], src_i[:, :, :]))
                        step(V.tensor_copy(src_lo_b[:, :, :], src_lo[:, :, :]))
                        step(V.tensor_tensor(src_hi[:, :, :], src_t[:, :, :], src_lo[:, :, :], ALU.subtract))
                        step(V.tensor_scalar(src_hi[:, :, :], src_hi[:, :, :], 1.0 / P, None, ALU.mult))
                        step(V.tensor_scalar(block_t[:, :], block_t[:, :], float(P), None, ALU.mult))
                        for c in range(CH):
                            step(V.tensor_scalar(dst_l[:, c, :], dst_g[:, c, :], block_t[:, c:c + 1], None, ALU.subtract))
                        for d in (dst_g, dst_l):
                            step(V.scalar_tensor_tensor(d[:, :, :], d[:, :, :], 1.0, inside[:, :, :], ALU.add, ALU.mult))
                            step(V.tensor_scalar_add(d[:, :, :], d[:, :, :], -1.0))
                        step(V.tensor_copy(dst_l_b[:, :, :], dst_l[:, :, :]))
                        step(V.tensor_copy(w_t[:, :, :], vals[:, :, :, 0]))
                        step(V.tensor_copy(first_c[:, :], dst_g[:, :, 0]))
                        step(V.tensor_copy(last_c[:, :], dst_g[:, :, P - 1]))
                        V.memset(none[:, :], -5.0).then_inc(tiled.sem, 1)
                        step(V.tensor_tensor(same[:, :, 0:P - 1], dst_g[:, :, 0:P - 1], dst_g[:, :, 1:P], ALU.is_equal))
                        step(V.memset(lp3[:, :, 0:1], -BIG))
                        step(V.memset(rp3[:, :, P - 1:P], -BIG))
                        step(V.tensor_scalar(lp3[:, :, 1:P], same[:, :, 0:P - 1], -1.0, BIG, ALU.add, ALU.mult))
                        step(V.tensor_scalar(rp3[:, :, 0:P - 1], same[:, :, 0:P - 1], -1.0, BIG, ALU.add, ALU.mult))
                        step(V.tensor_scalar(fi3[:, :, 1:P], same[:, :, 0:P - 1], -1.0, 1.0, ALU.mult, ALU.add))
                        for k in range(3):
                            step(V.tensor_copy(feat_t[:, k, :, :], vals[:, :, :, k + 1]))
                        for part in range(3):
                            step(V.tensor_copy(feat_b[:, part, :, :, :], feat_t[:, :, :, :]))
                            if part < 2:
                                step(V.tensor_tensor(feat_t[:, :, :, :], feat_t[:, :, :, :], feat_b[:, part, :, :, :],
                                                     ALU.subtract))
                        V.memset(block_f[:, 0:1], -1.0).then_inc(feats_split.sem, 1)
                        dve.wait_ge(rows_in.sem, rows_in.at(16 * 5))
                        for c in range(CH):
                            step(V.tensor_scalar(li3[:, c, :], dst_g[:, c, :], prev_last[:, c:c + 1], None, ALU.is_equal))
                            step(V.tensor_scalar(ri3[:, c, :], dst_g[:, c, :], next_first[:, c:c + 1], None, ALU.is_equal))
                        step(V.tensor_scalar(fi3[:, :, 0:1], li3[:, :, 0:1], -1.0, 1.0, ALU.mult, ALU.add))
                        step(V.tensor_scalar(left_in[:, :], left_in[:, :], -1.0, BIG, ALU.add, ALU.mult))
                        step(V.tensor_scalar(right_in[:, :], right_in[:, :], -1.0, BIG, ALU.add, ALU.mult))
                        step(V.tensor_tensor(tile_left_pen[:, :], lasts[:, 0:TP], lasts[:, 1:TP + 1], ALU.is_equal))
                        step(V.tensor_tensor(tile_right_pen[:, :], firsts[:, 0:TP], firsts[:, 1:TP + 1], ALU.is_equal))
                        step(V.tensor_scalar(tile_left_pen[:, :], tile_left_pen[:, :], -1.0, BIG, ALU.add, ALU.mult))
                        step(V.tensor_scalar(tile_right_pen[:, :], tile_right_pen[:, :], -1.0, BIG, ALU.add, ALU.mult))
                        step(V.memset(block_f[:, 0:1], -1.0))
                        step(V.tensor_copy(block_f[:, 1:TP + 1], block_of[:, :]))
                        V.tensor_tensor(keep_row[:, :], block_f[:, 0:TP], block_f[:, 1:TP + 1], ALU.is_equal,
                                        ).then_inc(ends_ready.sem, 1)
                        for k, to in enumerate([src_f, dst_in, edge_w, src_hi_e]):
                            dve.wait_ge(t_ready.sem, t_ready.at(k + 1))
                            step(V.tensor_copy(to[:, :], psum[:, 1 + k, :]))
                        step(V.tensor_copy(src_u[:, :], src_f[:, 0:T]))
                        dve.wait_ge(t_ready.sem, t_ready.at(5))
                        step(V.tensor_copy(keep[:, :], psum[:, 5, 0:T]))
                        step(V.tensor_tensor(src_hot[:, :, :],
                                             src_hi_e[:, 0:T].unsqueeze(2).broadcast_to([P, T, NB]),
                                             iota_row[:, 0:NB].unsqueeze(1).broadcast_to([P, T, NB]), ALU.is_equal))
                        dve_done.phase_ends(step.count[0])

                    @block.tensor
                    def _(pe):
                        pe.wait_ge(consts.sem, consts.at(1))
                        pe.wait_ge(counted.sem, counted.at(1))
                        PE.matmul(psum[:, 0, 0:NB], ones[:, :], cnt[:, :], start=True, stop=True).then_inc(totalled.sem, 1)
                        pe.wait_ge(int_consts.sem, int_consts.at(1))
                        pe.wait_ge(tiled.sem, tiled.at(1))
                        for k, array in enumerate(turned):
                            for c in range(CH):
                                last = PE.transpose(psum[:, 1 + k, c * P:(c + 1) * P], array[:, c, :], ident[:, :])
                            last.then_inc(t_ready.sem, 1)
                        pe.wait_ge(ends_ready.sem, ends_ready.at(1))
                        PE.matmul(psum[:, 5, :], ones[0:1, :], keep_row[:, :], start=True, stop=True).then_inc(t_ready.sem, 1)

                    @block.scalar
                    def _(act):
                        act.wait_ge(consts.sem, consts.at(1))
                        act.wait_ge(counted.sem, counted.at(1))
            for sig, n in ((loaded, 16), (gathered, 32 * CH), (rows_out, 16 * 8), (feats_out, 16 * 9), (feats_split, 1), (rows_in, 16 * 5), (consts, 1),
                           (counted, 1), (totalled, 1), (placed, 1), (tiled, 1), (ends_ready, 1), (t_ready, 5),
                           (int_consts, 1), (pool_done, 5)):
                sig.phase_ends(n)


        def refine_root(step):
            step(V.reciprocal(rstd[:, :], rstd[:, :]))
            step(V.tensor_tensor(root_t[:, :], rstd[:, :], rstd[:, :], ALU.mult))
            step(V.scalar_tensor_tensor(root_t[:, :], stats[:, :, 1], EPS, root_t[:, :], ALU.add, ALU.mult))
            step(V.tensor_scalar(root_t[:, :], root_t[:, :], -0.5, 1.5, ALU.mult, ALU.add))
            step(V.tensor_tensor(rstd[:, :], rstd[:, :], root_t[:, :], ALU.mult))

        def row_stats(dve, step, rows, n, bn, mv):
            step(V.bn_stats(bn[:, :], rows), apart=passed)
            step(V.bn_aggr(mv[:, :], bn[:, :]))
            step(V.tensor_copy(row(stats, n), mv[:, :]))

        def group(ap, g):
            return ap[:, bass.ds(g * G, G), :]

        def group_stats(step, rows, g, bn, mv):
            for b in range(G):
                ins = V.bn_stats(bn[:, b, :], row(rows, g * G + b))
            step(ins, apart=passed)
            for b in range(G):
                ins = V.bn_aggr(mv[:, b, :], bn[:, b, :])
            step(ins)
            step(V.tensor_copy(group(stats, g), mv[:, :, :]))

        def scatter_phase():
            (rows_in, hot_ready, index_ready, m_ready, m_copied, out_ready, out_copied, consts, zeroed) = (
                hs[:2], flags[0], flags[1], flags[2], flags[3], flags[4], flags[5], flags[6], hstore)
            with ExitStack() as scope:
                def tmp(name, shape, dt=F32):
                    return scope.enter_context(nc.sbuf_tensor(name, shape, dt))

                ids = tmp("ids_rows", [P, 2, 4 * P])
                equal = tmp("equal", [P, 2, 4 * P])
                hot_w = tmp("hot_w", [P, 2, 4 * P])
                tril = tmp("tril", [P, P])
                junk = tmp("junk", [P, 4, P])
                dup = tmp("dup", [P, 2, 4])
                move = tmp("move", [P, 2, 4])
                index = tmp("index", [P, 4, 4], U32)
                m_sb = tmp("m_sb", [P, 2, 4 * P])
                val = acc[:, :, :].rearrange("p n d -> p (n d)")[:, 0:16 * D].rearrange("p (s v) -> p s v", s=4)
                dump = tmp("dump", [P, 1])
                zero = tmp("zero", [P, (DUMP + P) // P * D // 2])
                SD = 4 * 3

                with nc.Block() as block:
                    @block.sync
                    def _(sp):
                        sp.dma_start(x[:, 0:NB - 1, :], t["x"][0:(NB - 1) * P, :].rearrange("(n p) d -> p n d", p=P),
                                     ).then_inc(hload.sem, 16)
                        sp.wait_ge(consts.sem, consts.at(1))
                        sp.dma_start(x[0:LAST, NB - 1, :], t["x"][(NB - 1) * P:N_NODES, :]).then_inc(hload.sem, 16)
                        for k in range(ACCS):
                            for half in sums[k].rearrange("(h p r) d -> h p (r d)", h=2, p=P):
                                sp.dma_start(half, zero[:, :]).then_inc(zeroed.sem, 16)

                        def turn(i, first):
                            for s in range(4):
                                if not (first and s < 2):
                                    sp.wait_ge(hot_ready.sem, hot_ready.at(4 * i + s - 1))
                                at = (4 * i + s) * (4 * P)
                                sp.dma_start(ids[:, s % 2, :], src_ids[0:1, bass.ds(at, 4 * P)].broadcast_to([P, 4 * P]),
                                             ).then_inc(rows_in[s % 2].sem, 16)
                        over_double_turns(sp, turn)
                        for h in range(2):
                            sp.wait_ge(rows_in[h].sem, rows_in[h].at(16 * TURNS))
                        sp.wait_ge(zeroed.sem, zeroed.at(16 * 2 * ACCS))

                    @block.gpsimd
                    def _(pool):
                        step = chain(pool, pool_done)
                        step(POOL.memset(zero[:, :], 0.0))
                        step(POOL.memset(x[:, NB - 1, :], 0.0))
                        step(POOL.memset(ones_row[:, :], 1.0))
                        step(POOL.memset(tril[:, :], 1.0))
                        whole, part = divmod(N_LOOPS, P)
                        step(POOL.memset(loop_mask[:, :], 0.0))
                        step(POOL.memset(loop_mask[:, 0:whole], 1.0))
                        step(POOL.tensor_scalar(loop_mask[:, whole:whole + 1], iota_col[:, :], float(part), None, ALU.is_lt))
                        step(POOL.tensor_scalar(loop_pen[:, :], loop_mask[:, :], -1.0, BIG, ALU.add, ALU.mult))
                        step(POOL.tensor_scalar(dump[:, :], iota_col[:, :], float(DUMP), None, ALU.add))
                        POOL.tensor_scalar(tril[:, :], iota_row[:, :], iota_col[:, :], None, ALU.is_lt).then_inc(consts.sem, 1)
                        pool.wait_ge(zeroed.sem, zeroed.at(16 * 2 * ACCS))

                        def turn(i, first):
                            for s in range(4):
                                k = 4 * i + s
                                pool.wait_ge(index_ready.sem, index_ready.at(k + 1))
                                pool.wait_ge(out_copied.sem, out_copied.at(k + 1))
                                for j in range(4):
                                    if not (first and s == 0):
                                        pool.wait_ge(ds[j].sem, ds[j].at(16 * k))
                                        stand_alone(pool, passed)
                                    pool.indirect_dma_start(
                                        sums[j], bass.IndirectOffsetOnAxis(ap=index[:, s, j:j + 1], axis=0),
                                        val[:, s, j * D:(j + 1) * D], None, compute_op=ALU.add,
                                    ).then_inc(ds[j].sem, 16)
                        over_double_turns(pool, turn)
                        for j in range(4):
                            pool.wait_ge(ds[j].sem, ds[j].at(16 * 2 * TURNS))

                    @block.vector
                    def _(dve):
                        step = Steps(dve, dve_done, SD)
                        dve.wait_ge(consts.sem, consts.at(1))

                        def turn(i, first):
                            step.turn(i)
                            for s in range(4):
                                k, h = 4 * i + s, s % 2
                                tile = 4 * k
                                dve.wait_ge(rows_in[h].sem, rows_in[h].at(16 * (2 * i + s // 2 + 1)))
                                if not (first and s < 2):
                                    dve.wait_ge(m_ready.sem, m_ready.at(k - 1))
                                for j in range(4):
                                    V.tensor_scalar(equal[:, h, j * P:(j + 1) * P], ids[:, h, j * P:(j + 1) * P],
                                                    src_f[:, bass.ds(tile + j, 1)], None, ALU.is_equal)
                                    ins = V.tensor_scalar(hot_w[:, h, j * P:(j + 1) * P], iota_row[:, :],
                                                          dst_in[:, bass.ds(tile + j, 1)], edge_w[:, bass.ds(tile + j, 1)],
                                                          ALU.is_equal, ALU.mult)
                                ins.then_inc(hot_ready.sem, 1)
                                dve.wait_ge(hot_ready.sem, hot_ready.at(k + 1))
                                for j in range(4):
                                    ins = V.scalar_tensor_tensor(junk[:, j, :], equal[:, h, j * P:(j + 1) * P], 1.0,
                                                                 tril[:, :], ALU.mult, ALU.mult, accum_out=dup[:, h, j:j + 1])
                                step(ins)
                                step(V.tensor_scalar(move[:, h, :], src_f[:, bass.ds(tile, 4)], -1.0, dump[:, :],
                                                     ALU.mult, ALU.add))
                                step(V.scalar_tensor_tensor(dup[:, h, :], dup[:, h, :], 1.0, move[:, h, :], ALU.min, ALU.mult))
                                if not first:
                                    for j in range(4):
                                        dve.wait_ge(ds[j].sem, ds[j].at(16 * (k - 3)))
                                V.tensor_tensor(index[:, s, :], dup[:, h, :], src_f[:, bass.ds(tile, 4)],
                                                ALU.add).then_inc(index_ready.sem, 1)
                        over_double_turns(dve, turn)

                    @block.tensor
                    def _(pe):
                        pe.wait_ge(hload.sem, hload.at(32))

                        def combine(k, h, first):
                            pe.wait_ge(hot_ready.sem, hot_ready.at(k + 1))
                            if not first:
                                pe.wait_ge(m_copied.sem, m_copied.at(k - 1))
                            for j in range(4):
                                cut = slice(j * P, (j + 1) * P)
                                ins = PE.matmul(psum[:, h, cut], hot_w[:, h, cut], equal[:, h, cut], start=True, stop=True)
                            ins.then_inc(m_ready.sem, 1)

                        def weigh(k, h, first, blk):
                            pe.wait_ge(m_copied.sem, m_copied.at(k + 1))
                            if not first:
                                pe.wait_ge(out_copied.sem, out_copied.at(k - 1))
                            for j in range(4):
                                ins = PE.matmul(psum[:, 2 + 2 * h + j // 2, (j % 2) * D:(j % 2 + 1) * D],
                                                m_sb[:, h, j * P:(j + 1) * P],
                                                x[:, bass.ds(blk[j], 1), :].rearrange("p o d -> p (o d)"),
                                                start=True, stop=True)
                            ins.then_inc(out_ready.sem, 1)

                        def turn(i, first, last=False):
                            _, blk = nc.values_load_multi_w_load_instructions(
                                block_of[0:1, bass.ds(i * (2 * U), 2 * U)], engines=[PE_ENGINE], min_val=0, max_val=NB - 1,
                                skip_runtime_bounds_check_because="blocks are counted on the chip, below NB")
                            for s in range(4):
                                if not (last and s == 3):
                                    combine(4 * i + s + 1, (s + 1) % 2, first and s == 0)
                                weigh(4 * i + s, s % 2, first and s < 2, blk[4 * s:4 * s + 4])
                        combine(0, 0, True)
                        turn(0, True)
                        with pe.Fori(1, TURNS // 2 - 1) as i:
                            turn(i, False)
                        turn(TURNS // 2 - 1, False, last=True)

                    @block.scalar
                    def _(act):
                        def combined(k, h, first):
                            act.wait_ge(m_ready.sem, m_ready.at(k + 1))
                            if not first:
                                act.wait_ge(out_ready.sem, out_ready.at(k - 1))
                            A.copy(m_sb[:, h, :], psum[:, h, :]).then_inc(m_copied.sem, 1)

                        def weighed(k, s, first):
                            h = s % 2
                            act.wait_ge(out_ready.sem, out_ready.at(k + 1))
                            if not first:
                                for j in range(4):
                                    act.wait_ge(ds[j].sem, ds[j].at(16 * (k - 3)))
                            A.copy(val[:, s, :], psum[:, 2 + 2 * h:4 + 2 * h, :].rearrange("p b f -> p (b f)"),
                                   ).then_inc(out_copied.sem, 1)

                        def turn(i, first, last=False):
                            for s in range(4):
                                if not (last and s == 3):
                                    combined(4 * i + s + 1, (s + 1) % 2, first and s == 0)
                                weighed(4 * i + s, s, first)
                        combined(0, 0, True)
                        turn(0, True)
                        with act.Fori(1, TURNS // 2 - 1) as i:
                            turn(i, False)
                        turn(TURNS // 2 - 1, False, last=True)
            for sig in (hot_ready, index_ready, m_ready, m_copied, out_ready, out_copied):
                sig.phase_ends(2 * TURNS)
            for sig, n in ((hload, 32), (zeroed, 32 * ACCS), (consts, 1), (pool_done, 9), (dve_done, SD * TURNS // 2),
                           *((d, 32 * TURNS) for d in ds[:4]), *((d, 16 * TURNS) for d in rows_in)):
                sig.phase_ends(n)

        def first_layer_nodes():
            (turned, copied, produced, summed, stat, loaded_w) = flags[:5] + [hload]
            slot_in = hs[:2]
            with ExitStack() as scope:
                def tmp(name, shape, dt=F32):
                    return scope.enter_context(nc.sbuf_tensor(name, shape, dt))

                w_sb = tmp("w0_sb", [P, KC, D])
                b_sb = tmp("b0_sb", [1, D])
                part = tmp("part", [P, 2, ACCS, D])
                sum_t = tmp("sum_t", [P, 2, KC * P])
                bn = tmp("bn", [P, 6])
                mv = tmp("mv", [P, 2])
                SD = 3

                with nc.Block() as block:
                    @block.sync
                    def _(sp):
                        sp.dma_start(w_sb[:, :, :], t["w0"].rearrange("(k p) o -> p k o", p=P)).then_inc(loaded_w.sem, 16)
                        sp.dma_start(b_sb[:, :], t["b0"]).then_inc(loaded_w.sem, 16)

                        def one(n, s, first):
                            if not first:
                                sp.wait_ge(turned.sem, turned.at(n - 1))
                            for k in range(ACCS):
                                sp.dma_start(part[:, s, k, :], sums[k][bass.ds(n * P, P), :]).then_inc(slot_in[s].sem, 16)
                        over_blocks(sp, one)

                    @block.tensor
                    def _(pe):
                        pe.wait_ge(loaded_w.sem, loaded_w.at(32))

                        def turn_over(n, s, first):
                            pe.wait_ge(slot_in[s].sem, slot_in[s].at(16 * ACCS * slot_turn(n, s)))
                            if not first:
                                pe.wait_ge(copied.sem, copied.at(n - 1))
                            for c in range(KC):
                                for k in range(ACCS):
                                    ins = PE.matmul(psum[:, s, c * P:(c + 1) * P], part[:, s, k, c * P:(c + 1) * P],
                                                    ident[:, :], start=k == 0, stop=k == ACCS - 1)
                            ins.then_inc(turned.sem, 1)

                        def product(n, s, first):
                            pe.wait_ge(copied.sem, copied.at(n + 1))
                            if not first:
                                pe.wait_ge(summed.sem, summed.at(n - 1))
                            for c in range(KC):
                                PE.matmul(psum[:, 2 + s, 0:D], sum_t[:, s, c * P:(c + 1) * P], w_sb[:, c, :],
                                          start=c == 0, stop=False)
                            PE.matmul(psum[:, 2 + s, 0:D], ones_row[:, :], b_sb[:, :], start=False, stop=True,
                                      ).then_inc(produced.sem, 1)
                        over_blocks_ahead(pe, turn_over, product)

                    @block.scalar
                    def _(act):
                        def one(n, s, first):
                            act.wait_ge(turned.sem, turned.at(n + 1))
                            if not first:
                                act.wait_ge(produced.sem, produced.at(n - 1))
                            A.copy(sum_t[:, s, :], psum[:, s, 0:KC * P]).then_inc(copied.sem, 1)
                        over_blocks(act, one)

                    @block.vector
                    def _(dve):
                        step = Steps(dve, dve_done, SD)

                        def one(n, s, first):
                            step.turn(n)
                            xn = x[:, bass.ds(n, 1), :].rearrange("p o d -> p (o d)")
                            dve.wait_ge(produced.sem, produced.at(n + 1))
                            V.tensor_tensor(xn, xn, psum[:, 2 + s, 0:D], ALU.add).then_inc(summed.sem, 1)
                            dve.wait_ge(summed.sem, summed.at(n + 1))
                            stand_alone(dve, passed)
                            row_stats(dve, step, xn, n, bn, mv)
                        over_blocks(dve, one)
            for sig in (turned, copied, produced, summed):
                sig.phase_ends(NB)
            for sig, n in ((loaded_w, 32), (dve_done, SD * NB), (slot_in[0], 16 * ACCS * (NB // 2 + 1)),
                           (slot_in[1], 16 * ACCS * (NB // 2))):
                sig.phase_ends(n)


        def project(L, rows_of, affine, es_tab, ed_tab):
            (normed, turned, copied, produced, rows_ready, att_ready, varied, rooted, attended, kept, parted) = flags[:11]
            staged = L.cols > D or L.edge_feats
            stored = hs[:2]
            H, C = L.heads, L.cols
            with ExitStack() as scope:
                def tmp(name, shape, dt=F32):
                    return scope.enter_context(nc.sbuf_tensor(f"{L.name}_{name}", shape, dt))

                w_sb = tmp("w", [P, KC, C])
                a_sb = tmp("a", [P, 2, C])
                prod = tmp("prod", [P, C])
                w_x = tmp("wx", [P, KC, 2 * H])
                g_sb = tmp("g", [P, 2, D]) if affine else None
                y_sb = tmp("y", [P, 2, D])
                x_t = tmp("xt", [P, 2, KC * P])
                wide = tmp("wide", [P, 2, C]) if staged else None
                left = tmp("left", [P, 2, C]) if L.edge_feats else None
                rest = tmp("rest", [P, NB * 2 * H])
                rest2 = tmp("rest2", [P, NB * 2 * H])
                own = tmp("own", [P, NB, 2 * H])
                n_loads = 3 + 2 * affine
                SD = 5

                with nc.Block() as block:
                    @block.sync
                    def _(sp):
                        sp.dma_start(w_sb[:, :, :], t[L.w].rearrange("(k p) o -> p k o", p=P)).then_inc(hload.sem, 16)
                        for k in range(2):
                            sp.dma_start(a_sb[:, k, :], t[L.a[k]].broadcast_to([P, C])).then_inc(hload.sem, 16)
                        if affine:
                            sp.dma_start(g_sb[:, 0, :], t["ln_g"].broadcast_to([P, D])).then_inc(hload.sem, 16)
                            sp.dma_start(g_sb[:, 1, :], t["ln_b"].broadcast_to([P, D])).then_inc(hload.sem, 16)

                        def one(n, s, first):
                            sp.wait_ge(rows_ready.sem, rows_ready.at(n + 1))
                            sp.dma_start(table[C][bass.ds(n * P, P), :], wide[:, s, :] if staged else row(node_rows, n),
                                         ).then_inc(stored[s].sem, 16)
                        over_blocks(sp, one)
                        sp.wait_ge(stored[0].sem, stored[0].at(16 * (NB // 2 + 1)))
                        sp.wait_ge(stored[1].sem, stored[1].at(16 * (NB // 2)))

                    @block.vector
                    def _(dve):
                        step = Steps(dve, dve_done, 4 * KC + 5)
                        step.turn(0)
                        V.tensor_scalar_add(rstd[:, :], stats[:, :, 1], EPS).then_inc(varied.sem, 1)
                        dve.wait_ge(hload.sem, hload.at(16 * n_loads))
                        for k in range(KC):
                            for side in range(2):
                                step(V.tensor_tensor(prod[:, :], w_sb[:, k, :], a_sb[:, side, :], ALU.mult))
                                step(V.reduce_sum(w_x[:, k, side * H:(side + 1) * H],
                                                  prod[:, :].rearrange("p (h d) -> p h d", h=H), AX))
                        V.memset(prod[:, 0:1], 0.0).then_inc(attended.sem, 1)
                        dve.wait_ge(rooted.sem, rooted.at(1))
                        refine_root(step)
                        assert step.c == step.per
                        dve_done.phase_ends(step.per)
                        step = Steps(dve, dve_done, 3 if affine or L.edge_feats else 0)

                        def norm(n, s, first):
                            step.turn(n)
                            y = y_sb[:, s, :]
                            if not first:
                                dve.wait_ge(turned.sem, turned.at(n - 1))
                                if not affine:
                                    dve.wait_ge(kept.sem, kept.at(n - 1))
                            ins = V.tensor_scalar(y, rows_of(n), stats[:, bass.ds(n, 1), 0], rstd[:, bass.ds(n, 1)],
                                                   ALU.subtract, ALU.mult)
                            if affine:
                                step(ins)
                                step(V.tensor_tensor(y, y, g_sb[:, 0, :], ALU.mult))
                                step(V.tensor_tensor(y, y, g_sb[:, 1, :], ALU.add))
                                ins = V.tensor_scalar_max(y, y, 0.0)
                            ins.then_inc(normed.sem, 1)

                        def late(n, s, first):
                            dve.wait_ge(produced.sem, produced.at(n + 1))
                            V.tensor_copy(row(att, n)[:, 0:2 * H], psum[:, 3 + 2 * s, 0:2 * H]).then_inc(att_ready.sem, 1)
                            if L.edge_feats:
                                step.turn(n)
                                dve.wait_ge(rows_ready.sem, rows_ready.at(n + 1))
                                parts = [row(node_parts, n)[:, k * D:(k + 1) * D] for k in range(3)]
                                step(V.tensor_copy(parts[0], wide[:, s, :]))
                                step(V.tensor_tensor(left[:, s, :], wide[:, s, :], parts[0], ALU.subtract))
                                step(V.tensor_copy(parts[1], left[:, s, :]))
                                V.tensor_tensor(parts[2], left[:, s, :], parts[1], ALU.subtract).then_inc(parted.sem, 1)

                        over_blocks_two_ahead(dve, norm, late)
                        dve_done.phase_ends(step.per * NB)
                        dve.wait_ge(att_ready.sem, att_ready.at(NB))
                        step = chain(dve, dve_done)
                        rest_s = rest[:, 0:NB * H]
                        step(V.tensor_copy(rest_s.rearrange("p (n h) -> p n h", h=H), att[:, :, 0:H]))
                        for part in range(3):
                            step(V.tensor_copy(es_tab[:, part, :], rest_s))
                            step(V.tensor_tensor(rest_s, rest_s, es_tab[:, part, :], ALU.subtract))
                        M = L.wcols
                        step(V.tensor_copy(own[:, :, 0:H], att[:, :, H:2 * H]))
                        if L.loops:
                            z = own[:, :, H:2 * H]
                            step(V.tensor_tensor(z, att[:, :, 0:H], att[:, :, H:2 * H], ALU.add))
                            step(V.scalar_tensor_tensor(z, z, 0.2, z, ALU.mult, ALU.max))
                            step(V.tensor_tensor(z, z, loop_mask[:, :].unsqueeze(2).broadcast_to([P, NB, H]), ALU.mult))
                            step(V.tensor_tensor(z, z, loop_pen[:, :].unsqueeze(2).broadcast_to([P, NB, H]), ALU.add))
                        for part in range(3):
                            step(V.tensor_copy(ed_tab[:, :, part, :], own[:, :, 0:M]))
                            step(V.tensor_tensor(own[:, :, 0:M], own[:, :, 0:M], ed_tab[:, :, part, :], ALU.subtract))
                        dve_done.phase_ends(step.count[0])

                    @block.tensor
                    def _(pe):
                        pe.wait_ge(hload.sem, hload.at(16 * n_loads))
                        pe.wait_ge(attended.sem, attended.at(1))

                        def turn_over(n, s, first):
                            pe.wait_ge(normed.sem, normed.at(n + 1))
                            if not first:
                                pe.wait_ge(copied.sem, copied.at(n - 1))
                            for c in range(KC):
                                ins = PE.transpose(psum[:, s, c * P:(c + 1) * P], y_sb[:, s, c * P:(c + 1) * P], ident[:, :])
                            ins.then_inc(turned.sem, 1)

                        def product(n, s, first):
                            pe.wait_ge(copied.sem, copied.at(n + 1))
                            if not first:
                                pe.wait_ge(rows_ready.sem, rows_ready.at(n - 1))
                                pe.wait_ge(att_ready.sem, att_ready.at(n - 1))
                            for c in range(KC):
                                PE.matmul(psum[:, 2 + 2 * s, 0:C], x_t[:, s, c * P:(c + 1) * P], w_sb[:, c, :],
                                          start=c == 0, stop=c == KC - 1)
                            for c in range(KC):
                                ins = PE.matmul(psum[:, 3 + 2 * s, 0:2 * H], x_t[:, s, c * P:(c + 1) * P], w_x[:, c, :],
                                                start=c == 0, stop=c == KC - 1)
                            ins.then_inc(produced.sem, 1)
                        over_blocks_ahead(pe, turn_over, product)

                    if not affine:
                        @block.gpsimd
                        def _(pool):
                            def one(n, s, first):
                                pool.wait_ge(normed.sem, normed.at(n + 1))
                                stand_alone(pool, passed)
                                POOL.tensor_copy(rows_of(n), y_sb[:, s, :]).then_inc(kept.sem, 1)
                            over_blocks(pool, one)

                    @block.scalar
                    def _(act):
                        act.wait_ge(varied.sem, varied.at(1))
                        A.activation(rstd[:, :], rstd[:, :], ACT.Sqrt).then_inc(rooted.sem, 1)

                        def turned_in(n, s, first):
                            act.wait_ge(turned.sem, turned.at(n + 1))
                            if not first:
                                act.wait_ge(produced.sem, produced.at(n - 1))
                            A.copy(x_t[:, s, :], psum[:, s, 0:KC * P]).then_inc(copied.sem, 1)

                        def rows_out(n, s, first):
                            act.wait_ge(produced.sem, produced.at(n + 1))
                            if staged:
                                if L.edge_feats and not first:
                                    act.wait_ge(parted.sem, parted.at(n - 1))
                                if not first:
                                    act.wait_ge(stored[s].sem, stored[s].at(16 * (slot_turn(n, s) - 1)))
                                A.copy(wide[:, s, :], psum[:, 2 + 2 * s, 0:C]).then_inc(rows_ready.sem, 1)
                            else:
                                A.copy(row(node_rows, n), psum[:, 2 + 2 * s, 0:C]).then_inc(rows_ready.sem, 1)
                        over_blocks_ahead(act, turned_in, rows_out)
            for sig in (normed, turned, copied, produced, rows_ready, att_ready):
                sig.phase_ends(NB)
            if not affine:
                kept.phase_ends(NB)
            if L.edge_feats:
                parted.phase_ends(NB)
            for sig, n in ((varied, 1), (rooted, 1), (attended, 1), (hload, 16 * n_loads),
                           (stored[0], 16 * (NB // 2 + 1)), (stored[1], 16 * (NB // 2))):
                sig.phase_ends(n)

        def logit_phase(L, es_tab, ed_tab):
            (hot_s_made, hot_d_made, found, bank_read, selected, summed, es_added, pair_found, rectified, multiplied,
             q_summed, q_added, split, differed, columns_set, folded) = flags[:16]
            folding = pool_done
            hot_made = (hot_s_made, hot_d_made)
            hots_by_act = {"gat_a": (), "gat_b": (), "gat_8": (0,), "gat_e": (0, 1)}[L.name]
            fold = {"gat_8": "es", "gat_e": "q"}.get(L.name)
            rows_in = hs[:2]
            feats_in = hs[2:4]
            H, M, FE = L.heads, L.wcols, L.edge_feats
            with ExitStack() as scope:
                def tmp(name, shape, dt=F32):
                    return scope.enter_context(nc.sbuf_tensor(f"{L.name}_{name}", shape, dt))

                s_rows = tmp("s_rows", [P, 2, 4 * P], BF16)
                d_rows = tmp("d_rows", [P, 2, 4 * P], BF16)
                hot_s = tmp("hot_s", [P, 2, 4 * P], BF16)
                hot_d = tmp("hot_d", [P, 2, 4 * P], BF16)
                hots, rows_sb = (hot_s, hot_d), (s_rows, d_rows)
                sel = tmp("sel", [P, 2, 4, NB * H])
                es = tmp("es", [P, 2, 4, H])
                ed = tmp("ed", [P, 2, 4, H])
                z = tmp("z", [P, 2, 4, H])
                apart = tmp("apart", [P, 2, 2, 4 * P], BF16)
                minus_col = tmp("minus_col", [P, 1])
                one_col = tmp("one_col", [P, 1])
                if FE:
                    feats = tmp("feats", [FEAT_ROWS, 2, 4 * P], BF16)
                    we_sb = tmp("we", [FEAT_ROWS, D])
                    we_part = tmp("we_part", [FEAT_ROWS, D], BF16)
                    we_tab = tmp("we_tab", [FEAT_ROWS, D], BF16)
                    enc = tmp("enc", [P, 2, 4 * D])
                    q = tmp("q", [P, 2, 4, H])
                ED0 = NB * H
                assert ED0 + 3 * M <= BANK // 2

                def looked_up(h):
                    return psum[:, 2 * h:2 * h + 2, :].rearrange("p b (t f) -> p (b t) f", t=2)

                def terms(h):
                    if fold == "q":
                        return enc[:, h, :].rearrange("p (t d) -> p t d", d=D // H)
                    return sel[:, h, :, :].rearrange("p t (n h) -> p t n h", h=H)

                with nc.Block() as block:
                    @block.sync
                    def _(sp):
                        if FE:
                            sp.dma_start(we_sb[:, :], t["we"]).then_inc(hload.sem, 16)
                            sp.wait_ge(begun2.sem, begun2.at(1))

                        def turn(i, first):
                            for h in range(2):
                                k = 2 * i + h
                                at = (i * U + 4 * h) * P
                                if not first:
                                    for made in hot_made:
                                        sp.wait_ge(made.sem, made.at(k - 1))
                                        stand_alone(sp, passed)
                                for rows, to in ((src_rows, s_rows), (dst_rows, d_rows)):
                                    sp.dma_start(to[:, h, :], rows[0:1, bass.ds(at, 4 * P)].broadcast_to([P, 4 * P]),
                                                 ).then_inc(rows_in[h].sem, 16)
                                if FE:
                                    if not first:
                                        sp.wait_ge(pair_found.sem, pair_found.at(2 * k - 2))
                                        stand_alone(sp, passed)
                                    for b in range(3):
                                        sp.dma_start(feats[32 * b:32 * b + 9, h, :], feat_rows[:, bass.ds(at, 4 * P)],
                                                     ).then_inc(feats_in[h].sem, 16)
                        over_tiles(sp, turn)

                    @block.gpsimd
                    def _(pool):
                        if FE:
                            POOL.memset(feats[:, :, :], 1.0).then_inc(begun2.sem, 1)
                        POOL.memset(logits[:, :, T:TP], 0.0)
                        POOL.memset(one_col[:, :], 1.0)
                        POOL.tensor_scalar(minus_col[:, :], iota_col[:, :], -1.0, None, ALU.mult).then_inc(columns_set.sem, 1)
                        if fold:
                            ready, used = (multiplied, q_summed) if fold == "q" else (selected, summed)
                            per = 2 if fold == "q" else 1

                            def turn(i, first):
                                for h in range(2):
                                    k = 2 * i + h
                                    pool.wait_ge(ready.sem, ready.at(per * (k + 1)))
                                    stand_alone(pool, passed)
                                    view = terms(h)
                                    n = view.shape[2]
                                    POOL.tensor_tensor(view[:, :, 0:n // 2], view[:, :, 0:n // 2], view[:, :, n - n // 2:n],
                                                       ALU.add).then_inc(folding.sem, 1)
                                    pool.wait_ge(folding.sem, folding.at(k + 1))
                                    stand_alone(pool, passed)
                                    n = n - n // 2
                                    POOL.tensor_tensor(view[:, :, 0:n // 2], view[:, :, 0:n // 2], view[:, :, n - n // 2:n],
                                                       ALU.add).then_inc(folded.sem, 1)
                            over_tiles(pool, turn)

                    @block.vector
                    def _(dve):
                        if FE:
                            step = chain(dve, dve_done)
                            dve.wait_ge(hload.sem, hload.at(16))
                            for b in range(3):
                                step(V.tensor_copy(we_part[:, :], we_sb[:, :]))
                                step(V.tensor_copy(we_tab[32 * b:32 * b + 32, :], we_part[32 * b:32 * b + 32, :]))
                                step(V.tensor_tensor(we_sb[:, :], we_sb[:, :], we_part[:, :], ALU.subtract))
                            V.memset(q[:, :, :, :], 0.0).then_inc(split.sem, 1)
                            dve_done.phase_ends(step.count[0])

                        def ones_at(i, h, side):
                            if side in hots_by_act:
                                return
                            dve.wait_ge(rows_in[h].sem, rows_in[h].at(32 * (i + 1)))
                            V.tensor_scalar(hots[side][:, h, :], rows_sb[side][:, h, :], iota_col[:, :], None, ALU.is_equal,
                                            ).then_inc(hot_made[side].sem, 1)

                        def sum_es(k, h):
                            n = 7 if fold == "es" else NB
                            waited = folded if fold == "es" else selected
                            dve.wait_ge(waited.sem, waited.at(k + 1))
                            V.reduce_sum(es[:, h, :, :],
                                         sel[:, h, :, :].rearrange("p t (n h) -> p t h n", h=H)[:, :, :, 0:n], AX,
                                         ).then_inc(summed.sem, 1)

                        def sum_q(k, h):
                            dve.wait_ge(folded.sem, folded.at(k + 1))
                            V.reduce_sum(q[:, h, :, :].rearrange("p t h -> p (t h)"), terms(h)[:, :, 0:D // H // 4], AX,
                                         ).then_inc(q_summed.sem, 1)

                        def add_es(k, h):
                            dve.wait_ge(summed.sem, summed.at(k + 1))
                            V.tensor_tensor(z[:, h, :, :], es[:, h, :, :], ed[:, h, :, :], ALU.add).then_inc(es_added.sem, 1)

                        def add_q(k, h):
                            dve.wait_ge(es_added.sem, es_added.at(k + 1))
                            dve.wait_ge(q_summed.sem, q_summed.at(k + 1))
                            V.tensor_tensor(z[:, h, :, :], z[:, h, :, :], q[:, h, :, :], ALU.add).then_inc(q_added.sem, 1)

                        def leaky(k, h, tile):
                            added = q_added if FE else es_added
                            dve.wait_ge(added.sem, added.at(k + 1))
                            V.scalar_tensor_tensor(logits[:, 0:H, bass.ds(tile, 4)].rearrange("p h t -> p t h"),
                                                   z[:, h, :, :], 0.2, z[:, h, :, :], ALU.mult, ALU.max)

                        def turn(i, first, last):
                            for h in range(2):
                                k = 2 * i + h
                                tile = i * U + 4 * h
                                begun = not (first and h == 0)
                                dve.wait_ge(found.sem, found.at(k + 1))
                                V.tensor_tensor(sel[:, h, :, :].rearrange("p t (n h) -> p t n h", h=H),
                                                looked_up(h)[:, :, 0:ED0].rearrange("p t (n h) -> p t n h", h=H),
                                                src_hot[:, bass.ds(tile, 4), :].unsqueeze(3).broadcast_to([P, 4, NB, H]),
                                                ALU.mult).then_inc(selected.sem, 1)
                                parts = looked_up(h)[:, :, ED0:ED0 + 3 * M].rearrange("p t (c m) -> p t m c", c=3)
                                if L.loops:
                                    V.reduce_sum(logits[:, H:2 * H, bass.ds(tile, 4)].rearrange("p h t -> p t h"),
                                                 parts[:, :, H:2 * H, :], AX)
                                V.reduce_sum(ed[:, h, :, :], parts[:, :, 0:H, :], AX).then_inc(bank_read.sem, 1)
                                if begun and fold == "es":
                                    sum_es(k - 1, 1 - h)
                                elif begun:
                                    add_es(k - 1, 1 - h)
                                if FE:
                                    for p in range(2):
                                        cut = slice(2 * p * D, (2 * p + 2) * D)
                                        dve.wait_ge(rectified.sem, rectified.at(2 * k + p + 1))
                                        V.tensor_tensor(enc[:, h, cut], enc[:, h, cut], psum[:, 4 + p, :], ALU.mult,
                                                        ).then_inc(multiplied.sem, 1)
                                        if begun and p == 0:
                                            sum_q(k - 1, 1 - h)
                                    if begun:
                                        add_q(k - 1, 1 - h)
                                if not last:
                                    ones_at(i + 1, h, 0)
                                    ones_at(i + 1, h, 1)
                                if fold != "es":
                                    sum_es(k, h)
                                elif begun:
                                    add_es(k - 1, 1 - h)
                                if begun:
                                    leaky(k - 1, 1 - h, tile - 4)
                        for h in range(2):
                            for side in range(2):
                                ones_at(0, h, side)
                        turn(0, True, False)
                        with dve.Fori(1, TURNS - 1) as i:
                            turn(i, False, False)
                        turn(TURNS - 1, False, True)
                        if fold == "es":
                            sum_es(2 * TURNS - 1, 1)
                        add_es(2 * TURNS - 1, 1)
                        if FE:
                            sum_q(2 * TURNS - 1, 1)
                            add_q(2 * TURNS - 1, 1)
                        leaky(2 * TURNS - 1, 1, T - 4)

                    @block.tensor
                    def _(pe):
                        if FE:
                            pe.wait_ge(split.sem, split.at(1))

                        def turn(i, first):
                            _, blk = nc.values_load_multi_w_load_instructions(
                                block_of[0:1, bass.ds(i * U, U)], engines=[PE_ENGINE], min_val=0, max_val=NB - 1,
                                skip_runtime_bounds_check_because="blocks are counted on the chip, below NB")
                            for h in range(2):
                                k = 2 * i + h
                                for made in hot_made:
                                    pe.wait_ge(made.sem, made.at(k + 1))
                                if not first:
                                    pe.wait_ge(bank_read.sem, bank_read.at(k - 1))
                                for j in range(4):
                                    cut = slice(j * P, (j + 1) * P)
                                    bank = psum[:, 2 * h + j // 2, :]
                                    at = (j % 2) * (BANK // 2)
                                    for part in range(3):
                                        PE.matmul(bank[:, at:at + NB * H], hot_s[:, h, cut], es_tab[:, part, :],
                                                  start=part == 0, stop=part == 2)
                                    at += ED0
                                    ins = PE.matmul(bank[:, at:at + 3 * M], hot_d[:, h, cut],
                                                    ed_tab[:, bass.ds(blk[4 * h + j], 1), :, :].rearrange("p o c m -> p (o c m)"),
                                                    start=True, stop=True)
                                ins.then_inc(found.sem, 1)
                                if not FE:
                                    continue
                                pe.wait_ge(feats_in[h].sem, feats_in[h].at(48 * (i + 1)))
                                for p in range(2):
                                    if not (first and h == 0):
                                        pe.wait_ge(multiplied.sem, multiplied.at(2 * k + p - 1))
                                    for j in (2 * p, 2 * p + 1):
                                        cut, to = slice(j * P, (j + 1) * P), slice((j % 2) * D, (j % 2 + 1) * D)
                                        for part in range(3):
                                            PE.matmul(psum[:, 4 + p, to], hot_d[:, h, cut],
                                                      row(node_parts, blk[4 * h + j])[:, part * D:(part + 1) * D],
                                                      start=part == 0, stop=part == 2)
                                        ins = PE.matmul(psum[:, 6 + p, to], feats[:, h, cut], we_tab[:, :],
                                                        start=True, stop=True)
                                    ins.then_inc(pair_found.sem, 1)
                        over_tiles(pe, turn)

                    if hots_by_act:
                        @block.scalar
                        def _(act):
                            act.wait_ge(columns_set.sem, columns_set.at(1))
                            SIDES = len(hots_by_act)

                            def ones_at(i, h, first):
                                k = 2 * i + h
                                act.wait_ge(rows_in[h].sem, rows_in[h].at(32 * (i + 1)))
                                for side in hots_by_act:
                                    if not first:
                                        act.wait_ge(hot_made[side].sem, hot_made[side].at(k - 1))
                                    A.activation(apart[:, side, h, :], rows_sb[side][:, h, :], ACT.Abs, bias=minus_col[:, :],
                                                 ).then_inc(differed.sem, 1)
                                for n, side in enumerate(hots_by_act):
                                    act.wait_ge(differed.sem, differed.at(k * SIDES + n + 1))
                                    A.activation(hots[side][:, h, :], apart[:, side, h, :], ACT.Relu, bias=one_col[:, :], scale=-1.0,
                                                 ).then_inc(hot_made[side].sem, 1)

                            def turn(i, first, last):
                                for h in range(2):
                                    k = 2 * i + h
                                    if FE:
                                        if not first:
                                            act.wait_ge(q_summed.sem, q_summed.at(k - 1))
                                        for p in range(2):
                                            act.wait_ge(pair_found.sem, pair_found.at(2 * k + p + 1))
                                            A.activation(enc[:, h, 2 * p * D:(2 * p + 2) * D], psum[:, 6 + p, :], ACT.Relu,
                                                         ).then_inc(rectified.sem, 1)
                                    else:
                                        act.wait_ge(found.sem, found.at(k + 1))
                                    if not last:
                                        ones_at(i + 1, h, False)
                            for h in range(2):
                                ones_at(0, h, True)
                            turn(0, True, False)
                            with act.Fori(1, TURNS - 1) as i:
                                turn(i, False, False)
                            turn(TURNS - 1, False, True)
                            differed.phase_ends(SIDES * 2 * TURNS)
            for sig in (*hot_made, found, bank_read, selected, summed, es_added):
                sig.phase_ends(2 * TURNS)
            columns_set.phase_ends(1)
            if fold:
                folding.phase_ends(2 * TURNS)
                folded.phase_ends(2 * TURNS)
            if FE:
                for sig in (pair_found, rectified, multiplied):
                    sig.phase_ends(4 * TURNS)
                for sig in (q_summed, q_added):
                    sig.phase_ends(2 * TURNS)
                for sig in feats_in:
                    sig.phase_ends(48 * TURNS)
                hload.phase_ends(16)
                begun2.phase_ends(1)
                split.phase_ends(1)
            for sig in rows_in:
                sig.phase_ends(32 * TURNS)

        def softmax_phase(L):
            (turned, scanned, all_scanned, gathered, tiles_scanned, spread, spread_in, turned2, shifted, exped, wturned,
             stored, max_done) = flags[:13]
            H, LO = L.heads, L.loops
            with ExitStack() as scope:
                def tmp(name, shape, dt=F32):
                    return scope.enter_context(nc.sbuf_tensor(f"{L.name}_{name}", shape, dt))

                fwd = tmp("fwd", [P, TP])
                bwd = tmp("bwd", [P, TP])
                top = tmp("top", [P, H, TP])
                last_top = tmp("last_top", [P, CH, H])
                first_top = tmp("first_top", [P, CH, H])
                from_left = tmp("from_left", [H, TP + 1])
                from_right = tmp("from_right", [H, TP + 1])
                left_top = tmp("left_top", [P, CH, H])
                right_top = tmp("right_top", [P, CH, H])
                delta = tmp("delta", [P, 2, TP])
                delta_l = tmp("delta_l", [P, 2, TP]) if LO else None

                def turn_edges(pe_ap, bank):
                    for c in range(CH):
                        ins = PE.transpose(psum[:, bank, c * P:(c + 1) * P], pe_ap(c), ident[:, :])
                    return ins

                with nc.Block() as block:
                    @block.gpsimd
                    def _(pool):
                        POOL.memset(acc[:, :, 0:L.cols + HW], 0.0).then_inc(pool_done.sem, 1)

                    @block.tensor
                    def _(pe):
                        for h in range(H):
                            if h >= 2:
                                pe.wait_ge(scanned.sem, scanned.at(h - 1))
                            turn_edges(lambda c: logits[:, h, c * P:(c + 1) * P], h % 2).then_inc(turned.sem, 1)
                        pe.wait_ge(all_scanned.sem, all_scanned.at(1))
                        for k, part in enumerate((last_top, first_top)):
                            for c in range(CH):
                                ins = PE.transpose(psum[0:H, 2 + k, c * P:(c + 1) * P], part[:, c, :], ident[:, :])
                            ins.then_inc(gathered.sem, 1)
                        pe.wait_ge(tiles_scanned.sem, tiles_scanned.at(1))
                        for k, part in enumerate((from_left, from_right)):
                            for c in range(CH):
                                ins = PE.transpose(psum[:, 2 + k, c * H:(c + 1) * H], part[:, c * P + k:(c + 1) * P + k],
                                                   ident[0:H, 0:H])
                        ins.then_inc(spread.sem, 1)

                        def bring(h):
                            if h >= 2:
                                pe.wait_ge(shifted.sem, shifted.at(h - 1))
                            if h == 0:
                                pe.wait_ge(scanned.sem, scanned.at(H))
                            ins = turn_edges(lambda c: logits[:, h, c * P:(c + 1) * P], h % 2)
                            if LO:
                                if h == 0:
                                    pe.wait_ge(spread_in.sem, spread_in.at(1))
                                ins = turn_edges(lambda c: logits[:, H + h, c * P:(c + 1) * P], 2 + h % 2)
                            ins.then_inc(turned2.sem, 1)

                        def take(h):
                            pe.wait_ge(exped.sem, exped.at(h + 1))
                            if h >= 2:
                                pe.wait_ge(stored.sem, stored.at(h - 1))
                            ins = turn_edges(lambda c: delta[:, h % 2, c * P:(c + 1) * P], 4 + h % 2)
                            if LO:
                                ins = turn_edges(lambda c: delta_l[:, h % 2, c * P:(c + 1) * P], 6 + h % 2)
                            ins.then_inc(wturned.sem, 1)
                        bring(0)
                        for h in range(H):
                            if h + 1 < H:
                                bring(h + 1)
                            take(h)

                    @block.vector
                    def _(dve):
                        step = chain(dve, dve_done)
                        for h in range(H):
                            dve.wait_ge(turned.sem, turned.at(h + 1))
                            step(V.tensor_tensor_scan(fwd[:, :], left_pen[:, :], psum[:, h % 2, :], -BIG, ALU.add, ALU.max))
                            V.tensor_tensor_scan(bwd[:, ::-1], right_pen[:, ::-1], psum[:, h % 2, ::-1], -BIG, ALU.add, ALU.max,
                                                 ).then_inc(scanned.sem, 1)
                            dve.wait_ge(scanned.sem, scanned.at(h + 1))
                            step(V.tensor_tensor(top[:, h, :], fwd[:, :], bwd[:, :], ALU.max))
                            step(V.tensor_copy(last_top[:, :, h], fwd[:, P - 1:TP:P]))
                            step(V.tensor_copy(first_top[:, :, h], bwd[:, 0:TP:P]))
                        V.memset(from_left[:, 0:1], -BIG)
                        V.memset(from_right[:, TP:TP + 1], -BIG).then_inc(all_scanned.sem, 1)
                        dve.wait_ge(gathered.sem, gathered.at(2))
                        V.tensor_tensor_scan(from_left[:, 1:TP + 1], tile_left_pen[0:H, :], psum[0:H, 2, :], -BIG,
                                             ALU.add, ALU.max)
                        V.tensor_tensor_scan(from_right[:, TP - 1::-1], tile_right_pen[0:H, ::-1], psum[0:H, 3, ::-1], -BIG,
                                             ALU.add, ALU.max).then_inc(tiles_scanned.sem, 1)
                        dve.wait_ge(spread.sem, spread.at(1))
                        step(V.tensor_copy(left_top[:, :, :].rearrange("p c h -> p (c h)"), psum[:, 2, 0:CH * H]))
                        V.tensor_copy(right_top[:, :, :].rearrange("p c h -> p (c h)"), psum[:, 3, 0:CH * H],
                                      ).then_inc(spread_in.sem, 1)
                        dve.wait_ge(spread_in.sem, spread_in.at(1))
                        for h in range(H):
                            for c in range(CH):
                                cut = slice(c * P, (c + 1) * P)
                                V.scalar_tensor_tensor(top[:, h, cut], left_in[:, cut], left_top[:, c, h:h + 1],
                                                       top[:, h, cut], ALU.add, ALU.max)
                            step(V.memset(fwd[:, 0:1], 0.0))
                            for c in range(CH):
                                cut = slice(c * P, (c + 1) * P)
                                V.scalar_tensor_tensor(top[:, h, cut], right_in[:, cut], right_top[:, c, h:h + 1],
                                                       top[:, h, cut], ALU.add, ALU.max)
                            step(V.memset(fwd[:, 0:1], 0.0))
                            dve.wait_ge(turned2.sem, turned2.at(h + 1))
                            if LO:
                                step(V.tensor_tensor(top[:, h, :], top[:, h, :], psum[:, 2 + h % 2, :], ALU.max))
                            if h >= 2:
                                dve.wait_ge(wturned.sem, wturned.at(h - 1))
                            if LO:
                                V.tensor_tensor(delta_l[:, h % 2, :], psum[:, 2 + h % 2, :], top[:, h, :], ALU.subtract)
                            V.tensor_tensor(delta[:, h % 2, :], psum[:, h % 2, :], top[:, h, :], ALU.subtract,
                                            ).then_inc(shifted.sem, 1)
                            if LO:
                                dve.wait_ge(max_done.sem, max_done.at(h + 1))
                                V.scalar_tensor_tensor(delta_l[:, h % 2, :], delta_l[:, h % 2, :], -1.0, first[:, :],
                                                       ALU.add, ALU.mult).then_inc(exped.sem, 1)
                        dve_done.phase_ends(step.count[0])

                    @block.scalar
                    def _(act):
                        for h in range(H):
                            act.wait_ge(shifted.sem, shifted.at(h + 1))
                            ins = A.activation(delta[:, h % 2, :], delta[:, h % 2, :], ACT.Exp)
                            if LO:
                                A.activation(delta_l[:, h % 2, :], delta_l[:, h % 2, :], ACT.Exp).then_inc(max_done.sem, 1)
                            else:
                                ins.then_inc(exped.sem, 1)
                            act.wait_ge(wturned.sem, wturned.at(h + 1))
                            ins = A.copy(weights[:, :, h], psum[:, 4 + h % 2, 0:T])
                            if LO:
                                ins = A.copy(weights[:, :, H + h], psum[:, 6 + h % 2, 0:T])
                            ins.then_inc(stored.sem, 1)
            for sig in (turned, scanned, turned2, shifted, exped, wturned, stored):
                sig.phase_ends(H)
            if LO:
                max_done.phase_ends(H)
            for sig, n in ((pool_done, 1), (all_scanned, 1), (gathered, 2), (tiles_scanned, 1), (spread, 1), (spread_in, 1)):
                sig.phase_ends(n)

        def gather_phase(L):
            (staged, ready, summed, ran, kept, weighted) = flags[:6]
            H, C, M = L.heads, L.cols, L.wcols
            R = C + M
            with ExitStack() as scope:
                def tmp(name, shape, dt=F32):
                    return scope.enter_context(nc.sbuf_tensor(f"{L.name}_{name}", shape, dt))

                index = tmp("index", [P, 2, 4], U32)
                got = tmp("got", [P, U, R])
                hot = tmp("hot", [P, 4, P])
                running = tmp("running", [P, 4, R])

                def sums_of(s):
                    return psum[:, 2 * s:2 * s + 2, :].rearrange("p b f -> p (b f)")

                with nc.Block() as block:
                    @block.gpsimd
                    def _(pool):
                        def turn(i, first):
                            for h in range(2):
                                pool.wait_ge(staged.sem, staged.at(2 * i + h + 1))
                                stand_alone(pool, passed)
                                for j in range(4):
                                    tile = i * U + 4 * h + j
                                    if not first:
                                        pool.wait_ge(summed.sem, summed.at(tile - U + 1))
                                        stand_alone(pool, passed)
                                    pool.indirect_dma_start(
                                        got[:, 4 * h + j, 0:C], None, table[C],
                                        bass.IndirectOffsetOnAxis(ap=index[:, h, j:j + 1], axis=0),
                                    ).then_inc(ds[4 * h + j].sem, 16)
                        over_tiles(pool, turn)

                    @block.scalar
                    def _(act):
                        for h in range(2):
                            A.copy(index[:, h, :], src_u[:, 4 * h:4 * h + 4]).then_inc(staged.sem, 1)
                        A.copy(got[:, 0:4, C:R], weights[:, 0:4, 0:M]).then_inc(weighted.sem, 1)

                        def turn(i, first, last=False):
                            _, blk = nc.values_load_multi_w_load_instructions(
                                block_of[0:1, bass.ds(i * U, U)], engines=[ACT_ENGINE], min_val=0, max_val=NB - 1,
                                skip_runtime_bounds_check_because="blocks are counted on the chip, below NB")
                            for h in range(2):
                                if not last:
                                    for j in range(4):
                                        act.wait_ge(ds[4 * h + j].sem, ds[4 * h + j].at(16 * (i + 1)))
                                    A.copy(index[:, h, :], src_u[:, bass.ds((i + 1) * U + 4 * h, 4)]).then_inc(staged.sem, 1)
                                if not (last and h == 1):
                                    if not (first and h == 0):
                                        act.wait_ge(summed.sem, summed.at(i * U + 4 * h))
                                    A.copy(got[:, 4 - 4 * h:8 - 4 * h, C:R],
                                           weights[:, bass.ds(i * U + 4 * h + 4, 4), 0:M]).then_inc(weighted.sem, 1)
                                for j in range(4):
                                    act.wait_ge(ran.sem, ran.at(i * U + 4 * h + j + 1))
                                    if not (first and h == 0 and j == 0):
                                        act.wait_ge(kept.sem, kept.at(i * U + 4 * h + j))
                                    A.copy(row(acc, blk[4 * h + j])[:, 0:R], running[:, j, :]).then_inc(kept.sem, 1)
                        turn(0, True)
                        with act.Fori(1, TURNS - 1) as i:
                            turn(i, False)
                        turn(TURNS - 1, False, last=True)

                    @block.vector
                    def _(dve):
                        V.memset(running[:, 3, :], 0.0).then_inc(pool_done.sem, 1)
                        dve.wait_ge(pool_done.sem, pool_done.at(1))

                        def run_on(tile, s, first):
                            dve.wait_ge(summed.sem, summed.at(tile + 1))
                            if not first:
                                dve.wait_ge(ran.sem, ran.at(tile))
                                dve.wait_ge(kept.sem, kept.at(tile - 3))
                            V.scalar_tensor_tensor(running[:, s, :], running[:, (s + 3) % 4, :], keep[:, bass.ds(tile, 1)],
                                                   sums_of(s)[:, 0:R], ALU.mult, ALU.add).then_inc(ran.sem, 1)

                        def turn(i, first):
                            for j in range(U):
                                tile = i * U + j
                                s = j % 4
                                dve.wait_ge(ds[j].sem, ds[j].at(16 * (i + 1)))
                                view = got[:, j, 0:C].rearrange("p (h d) -> p h d", h=H)
                                V.tensor_tensor(view, view, weights[:, bass.ds(tile, 1), 0:H].rearrange(
                                    "p o h -> p (o h)").unsqueeze(2).broadcast_to([P, H, C // H]), ALU.mult)
                                if not (first and j < 4):
                                    dve.wait_ge(summed.sem, summed.at(tile - 3))
                                V.tensor_scalar(hot[:, s, :], iota_row[:, :], dst_in[:, bass.ds(tile, 1)], None,
                                                ALU.is_equal).then_inc(ready.sem, 1)
                                if first and j < 2:
                                    continue
                                if first and j < 6:
                                    if j > 2:
                                        dve.wait_ge(ran.sem, ran.at(tile - 2))
                                    run_on(tile - 2, (s + 2) % 4, True)
                                else:
                                    run_on(tile - 2, (s + 2) % 4, False)
                        over_tiles(dve, turn)
                        run_on(T - 2, 2, False)
                        run_on(T - 1, 3, False)

                    @block.tensor
                    def _(pe):
                        def turn(i, first):
                            for j in range(U):
                                tile = i * U + j
                                s = j % 4
                                if j % 4 == 0:
                                    pe.wait_ge(weighted.sem, weighted.at(2 * i + j // 4 + 1))
                                    stand_alone(pe, passed)
                                pe.wait_ge(ready.sem, ready.at(tile + 1))
                                if not (first and j < 4):
                                    pe.wait_ge(ran.sem, ran.at(tile - 3))
                                for c in range(0, R, BANK):
                                    cut = slice(c, min(c + BANK, R))
                                    ins = PE.matmul(sums_of(s)[:, cut], hot[:, s, :], got[:, j, cut], start=True, stop=True)
                                ins.then_inc(summed.sem, 1)
                        over_tiles(pe, turn)
            for sig in (ready, summed, ran, kept):
                sig.phase_ends(T)
            staged.phase_ends(2 * TURNS)
            weighted.phase_ends(2 * TURNS)
            pool_done.phase_ends(1)
            for sig in ds:
                sig.phase_ends(16 * TURNS)

        def loop_layer_nodes(L, residual):
            (own_ready, own_added) = flags[:2]
            H = L.heads
            with ExitStack() as scope:
                def tmp(name, shape, dt=F32):
                    return scope.enter_context(nc.sbuf_tensor(f"{L.name}_{name}", shape, dt))

                b_sb = tmp("b", [P, D])
                inv = tmp("inv", [P, NB, H])
                own = tmp("own_w", [P, NB, H])
                bn = tmp("bn", [P, G, 6])
                mv = tmp("mv", [P, G, 2])

                def heads(ap, g):
                    return group(ap, g)[:, :, 0:D].rearrange("p g (h d) -> p g h d", h=H)

                def wide(ap, g):
                    return group(ap, g).unsqueeze(3).broadcast_to([P, G, H, D // H])

                with nc.Block() as block:
                    @block.sync
                    def _(sp):
                        sp.dma_start(b_sb[:, :], t[L.b].broadcast_to([P, D])).then_inc(hload.sem, 16)

                    @block.gpsimd
                    def _(pool):
                        pool.wait_ge(hload.sem, hload.at(16))
                        pool.wait_ge(own_ready.sem, own_ready.at(1))
                        with pool.Fori(0, NB // G) as g:
                            POOL.tensor_tensor(heads(node_rows, g), heads(node_rows, g), wide(own, g), ALU.mult,
                                               ).then_inc(pool_done.sem, 1)
                            pool.wait_ge(pool_done.sem, pool_done.at(g + 1))
                            stand_alone(pool, passed)
                            POOL.tensor_tensor(group(node_rows, g), group(node_rows, g),
                                               b_sb[:, :].unsqueeze(1).broadcast_to([P, G, D]), ALU.add,
                                               ).then_inc(own_added.sem, 1)

                    @block.vector
                    def _(dve):
                        step = chain(dve, dve_done)
                        step(V.scalar_tensor_tensor(own[:, :, :], acc[:, :, D + H:D + 2 * H], 1.0,
                                                    loop_mask[:, :].unsqueeze(2).broadcast_to([P, NB, H]), ALU.add, ALU.mult))
                        step(V.tensor_tensor(inv[:, :, :], own[:, :, :], acc[:, :, D:D + H], ALU.add))
                        step(V.tensor_scalar_max(inv[:, :, :], inv[:, :, :], 1e-30))
                        step(V.reciprocal(inv[:, :, :], inv[:, :, :]))
                        V.tensor_tensor(own[:, :, :], own[:, :, :], inv[:, :, :], ALU.mult).then_inc(own_ready.sem, 1)
                        dve_done.phase_ends(4)
                        step = Steps(dve, dve_done, 6 if residual else 5)
                        with dve.Fori(0, NB // G) as g:
                            step.turn(g)
                            step(V.tensor_tensor(heads(acc, g), heads(acc, g), wide(inv, g), ALU.mult))
                            dve.wait_ge(own_added.sem, own_added.at(g + 1))
                            step(V.tensor_tensor(group(node_rows, g), group(node_rows, g), group(acc, g)[:, :, 0:D], ALU.add),
                                 apart=passed)
                            rows = node_rows
                            if residual:
                                rows = x
                                step(V.tensor_tensor(group(x, g), group(x, g), group(node_rows, g), ALU.add), apart=passed)
                            group_stats(step, rows, g, bn, mv)
                        dve_done.phase_ends(step.per * (NB // G))
            for sig, n in ((hload, 16), (own_ready, 1), (own_added, NB // G), (pool_done, NB // G)):
                sig.phase_ends(n)

        def out_project_nodes(L):
            (scaled, turned, copied, produced, exped, taken) = flags[:6]
            H, C, KO = L.heads, L.cols, L.cols // P
            with ExitStack() as scope:
                def tmp(name, shape, dt=F32):
                    return scope.enter_context(nc.sbuf_tensor(f"{L.name}_{name}", shape, dt))

                w_sb = tmp("wo", [P, KO, D])
                b_sb = tmp("bo", [1, D])
                inv = tmp("inv", [P, NB, H])
                m_sb = tmp("m_sb", [P, 2, C])
                m_t = tmp("m_t", [P, 2, C])
                neg = tmp("neg", [P, 2, D])
                bn = tmp("bn", [P, 6])
                mv = tmp("mv", [P, 2])
                with nc.Block() as block:
                    @block.sync
                    def _(sp):
                        sp.dma_start(w_sb[:, :, :], t["wo"].rearrange("(k p) o -> p k o", p=P)).then_inc(hload.sem, 16)
                        sp.dma_start(b_sb[:, :], t["bo"]).then_inc(hload.sem, 16)

                    @block.vector
                    def _(dve):
                        step = chain(dve, dve_done)
                        step(V.tensor_scalar_add(inv[:, :, :], acc[:, :, C:C + H], 1e-16))
                        step(V.reciprocal(inv[:, :, :], inv[:, :, :]))
                        dve_done.phase_ends(2)
                        step = Steps(dve, dve_done, 4)

                        def early(n, s, first):
                            if not first:
                                dve.wait_ge(turned.sem, turned.at(n - 1))
                            V.tensor_tensor(m_sb[:, s, :].rearrange("p (h d) -> p h d", h=H),
                                            row(acc, n)[:, 0:C].rearrange("p (h d) -> p h d", h=H), row(inv, n).unsqueeze(2).broadcast_to([P, H, C // H]), ALU.mult,
                                            ).then_inc(scaled.sem, 1)

                        def clip(n, s, first):
                            xn = row(x, n)
                            z = psum[:, 2 + s, 0:D]
                            dve.wait_ge(produced.sem, produced.at(n + 1))
                            V.tensor_scalar_min(neg[:, s, :], z, 0.0)
                            V.scalar_tensor_tensor(xn, z, 0.0, xn, ALU.max, ALU.add).then_inc(taken.sem, 1)

                        def add_exp(n, s):
                            step.turn(n)
                            xn = row(x, n)
                            dve.wait_ge(exped.sem, exped.at(n + 1))
                            dve.wait_ge(taken.sem, taken.at(n + 1))
                            step(V.scalar_tensor_tensor(xn, neg[:, s, :], -1.0, xn, ALU.add, ALU.add), apart=passed)
                            row_stats(dve, step, xn, n, bn, mv)

                        def late(n, s, first):
                            clip(n, s, first)
                            if not (first and s == 0):
                                add_exp(n - 1, 1 - s)
                        over_blocks_two_ahead(dve, early, late)
                        add_exp(NB - 1, 0)
                        dve_done.phase_ends(step.per * NB)

                    @block.tensor
                    def _(pe):
                        pe.wait_ge(hload.sem, hload.at(32))

                        def turn_over(n, s, first):
                            pe.wait_ge(scaled.sem, scaled.at(n + 1))
                            if not first:
                                pe.wait_ge(copied.sem, copied.at(n - 1))
                            for c in range(KO):
                                ins = PE.transpose(psum[:, s, c * P:(c + 1) * P], m_sb[:, s, c * P:(c + 1) * P], ident[:, :])
                            ins.then_inc(turned.sem, 1)

                        def product(n, s, first):
                            pe.wait_ge(copied.sem, copied.at(n + 1))
                            if not first:
                                pe.wait_ge(taken.sem, taken.at(n - 1))
                            for c in range(KO):
                                PE.matmul(psum[:, 2 + s, 0:D], m_t[:, s, c * P:(c + 1) * P], w_sb[:, c, :], start=c == 0, stop=False)
                            PE.matmul(psum[:, 2 + s, 0:D], ones_row[:, :], b_sb[:, :], start=False, stop=True,
                                      ).then_inc(produced.sem, 1)
                        over_blocks_ahead(pe, turn_over, product)

                    @block.scalar
                    def _(act):
                        def copy_in(n, s, first):
                            act.wait_ge(turned.sem, turned.at(n + 1))
                            if not first:
                                act.wait_ge(produced.sem, produced.at(n - 1))
                            A.copy(m_t[:, s, :], psum[:, s, 0:C]).then_inc(copied.sem, 1)

                        def exp_of(n, s, first):
                            act.wait_ge(taken.sem, taken.at(n + 1))
                            A.activation(neg[:, s, :], neg[:, s, :], ACT.Exp).then_inc(exped.sem, 1)

                        over_blocks_ahead(act, copy_in, exp_of)
            for sig in (scaled, turned, copied, produced, exped, taken):
                sig.phase_ends(NB)
            hload.phase_ends(32)

        def last_layer_nodes(L):
            (stats_in, rooted, normed, biased) = flags[:4]
            H = L.heads
            with ExitStack() as scope:
                def tmp(name, shape, dt=F32):
                    return scope.enter_context(nc.sbuf_tensor(f"{L.name}_{name}", shape, dt))

                b_sb = tmp("b", [P, D])
                inv = tmp("inv", [P, NB, H])
                bn = tmp("bn", [P, G, 6])
                mv = tmp("mv", [P, G, 2])
                with nc.Block() as block:
                    @block.sync
                    def _(sp):
                        sp.dma_start(b_sb[:, :], t[L.b].broadcast_to([P, D])).then_inc(hload.sem, 16)
                        with sp.Fori(0, NB // G - 1) as g:
                            sp.wait_ge(normed.sem, normed.at(g + 1))
                            sp.dma_start(out[bass.ds(g * (G * P), G * P), :].rearrange("(n p) d -> p n d", p=P), group(x, g),
                                         ).then_inc(hstore.sem, 16)
                        sp.wait_ge(normed.sem, normed.at(NB // G))
                        sp.dma_start(out[(NB - G) * P:(NB - 1) * P, :].rearrange("(n p) d -> p n d", p=P), x[:, NB - G:NB - 1, :],
                                     ).then_inc(hstore.sem, 16)
                        sp.dma_start(out[(NB - 1) * P:N_NODES, :], x[0:LAST, NB - 1, :]).then_inc(hstore.sem, 16)
                        sp.wait_ge(hstore.sem, hstore.at(16 * (NB // G + 1)))

                    @block.gpsimd
                    def _(pool):
                        pool.wait_ge(hload.sem, hload.at(16))
                        with pool.Fori(0, NB // G) as g:
                            POOL.tensor_tensor(group(x, g), group(x, g), b_sb[:, :].unsqueeze(1).broadcast_to([P, G, D]), ALU.add,
                                               ).then_inc(biased.sem, 1)

                    @block.vector
                    def _(dve):
                        step = chain(dve, dve_done)
                        step(V.tensor_scalar_max(inv[:, :, :], acc[:, :, D:D + H], 1e-10))
                        step(V.reciprocal(inv[:, :, :], inv[:, :, :]))
                        dve_done.phase_ends(2)
                        step = Steps(dve, dve_done, 5)
                        with dve.Fori(0, NB // G) as g:
                            step.turn(g)
                            sums_g = group(acc, g)[:, :, 0:D].rearrange("p g (h d) -> p g h d", h=H)
                            step(V.tensor_tensor(sums_g, sums_g, group(inv, g).unsqueeze(3).broadcast_to([P, G, H, D // H]),
                                                 ALU.mult))
                            dve.wait_ge(biased.sem, biased.at(g + 1))
                            step(V.tensor_tensor(group(x, g), group(x, g), group(acc, g)[:, :, 0:D], ALU.add), apart=passed)
                            group_stats(step, x, g, bn, mv)
                        dve_done.phase_ends(step.per * (NB // G))
                        V.tensor_scalar_add(rstd[:, :], stats[:, :, 1], EPS).then_inc(stats_in.sem, 1)
                        dve.wait_ge(rooted.sem, rooted.at(1))
                        step = chain(dve, dve_done)
                        refine_root(step)
                        dve_done.phase_ends(5)
                        with dve.Fori(0, NB // G) as g:
                            for b in range(G):
                                n = g * G + b
                                ins = V.tensor_scalar(row(x, n), row(x, n), stats[:, bass.ds(n, 1), 0], rstd[:, bass.ds(n, 1)],
                                                      ALU.subtract, ALU.mult)
                            ins.then_inc(normed.sem, 1)

                    @block.scalar
                    def _(act):
                        act.wait_ge(stats_in.sem, stats_in.at(1))
                        A.activation(rstd[:, :], rstd[:, :], ACT.Sqrt).then_inc(rooted.sem, 1)
            for sig, n in ((hload, 16), (hstore, 16 * (NB // G + 1)), (stats_in, 1), (rooted, 1), (normed, NB // G),
                           (biased, NB // G)):
                sig.phase_ends(n)

        def attention_layer(L, rows_of, affine):
            with ExitStack() as scope:
                es_tab = scope.enter_context(nc.sbuf_tensor(f"{L.name}_es_tab", [P, 3, NB * L.heads], BF16))
                ed_tab = scope.enter_context(nc.sbuf_tensor(f"{L.name}_ed_tab", [P, NB, 3, L.wcols], BF16))
                project(L, rows_of, affine, es_tab, ed_tab)
                logit_phase(L, es_tab, ed_tab)
                softmax_phase(L)
                gather_phase(L)

        gat_a = Layer("gat_a", 4, D, loops=True, w="w1", a=("a1s", "a1d"), b="b1")
        gat_b = Layer("gat_b", 1, D, loops=True, w="w2", a=("a2s", "a2d"), b="b2")
        gat_8 = Layer("gat_8", 8, 2 * D, w="w3", a=("a3s", "a3d"))
        gat_e = Layer("gat_e", 8, D, edge_feats=True, w="w4", a=("a4s", "a4d"), b="b4")

        order_phase()
        edge_phase()
        scatter_phase()
        first_layer_nodes()
        if stop == 0:
            return debug(nc, dict(locals()), out)
        attention_layer(gat_a, lambda n: row(x, n), False)
        loop_layer_nodes(gat_a, residual=False)
        if stop == 1:
            return debug(nc, dict(locals()), out)
        attention_layer(gat_b, lambda n: row(node_rows, n), True)
        loop_layer_nodes(gat_b, residual=True)
        if stop == 2:
            return debug(nc, dict(locals()), out)
        attention_layer(gat_8, lambda n: row(x, n), False)
        out_project_nodes(gat_8)
        if stop == 3:
            return debug(nc, dict(locals()), out)
        attention_layer(gat_e, lambda n: row(x, n), False)
        last_layer_nodes(gat_e)


_OUT = "out_dram"


def _layout(i):
    def a(n):
        return np.asarray(i[n])

    def row(n):
        return np.ascontiguousarray(a(n).reshape(1, -1))

    pad = ROWS - N_EDGES
    ids = np.stack([np.pad(a("src"), (0, pad)), np.pad(a("dst"), (0, pad), constant_values=NO_NODE)], axis=1)
    vals = np.concatenate([np.pad(a("edge_weight"), (0, pad))[:, None], np.pad(a("edge_attr_3"), ((0, pad), (0, 0)))], axis=1)
    H3 = a("L2_gnn_a").shape[1] // 2
    chunk = np.concatenate([a("L3_gnn_edge_W").T] * 3 + [row("L3_gnn_edge_b"), np.zeros((FEAT_ROWS // 3 - 10, D), np.float32)])
    we = np.ascontiguousarray(np.concatenate([chunk] * 3))
    return {
        "x": a("x"),
        "edge_ids": np.ascontiguousarray(ids),
        "edge_vals": np.ascontiguousarray(vals),
        "dst_list": np.pad(a("dst"), (0, pad), constant_values=NO_NODE).reshape(1, ROWS),
        "w0": np.ascontiguousarray(a("L0_gnn_W").T), "b0": row("L0_gnn_b"),
        "w1": a("L1_gnn_W1"), "a1s": row("L1_gnn_a1_src"), "a1d": row("L1_gnn_a1_dst"), "b1": row("L1_gnn_b1"),
        "ln_g": row("L1_gnn_ln_g"), "ln_b": row("L1_gnn_ln_b"),
        "w2": a("L1_gnn_W2"), "a2s": row("L1_gnn_a2_src"), "a2d": row("L1_gnn_a2_dst"), "b2": row("L1_gnn_b2"),
        "w3": np.ascontiguousarray(a("L2_gnn_W").transpose(1, 0, 2).reshape(D, -1)),
        "a3s": np.ascontiguousarray(a("L2_gnn_a")[:, :H3].reshape(1, -1)),
        "a3d": np.ascontiguousarray(a("L2_gnn_a")[:, H3:].reshape(1, -1)),
        "wo": a("L2_gnn_Wo"), "bo": row("L2_gnn_bo"),
        "w4": np.ascontiguousarray(a("L3_gnn_W").T), "a4s": row("L3_gnn_a_src"), "a4d": row("L3_gnn_a_dst"),
        "we": we, "b4": row("L3_gnn_bias"),
    }


def kernel(**inputs):
    import concourse.bacc as bacc
    from concourse.bass_utils import run_bass_kernel_spmd

    nc = bacc.Bacc("TRN2", target_bir_lowering=False, num_devices=1)
    arrays = _layout(inputs)
    given = {n: nc.dram_tensor(f"in_{n}", a.shape, mybir.dt.from_np(a.dtype), kind="ExternalInput").ap()
             for n, a in arrays.items()}
    out = nc.dram_tensor(_OUT, (N_NODES, D), F32, kind="ExternalOutput").ap()
    gnn_kernel(nc, given, out)
    r = run_bass_kernel_spmd(nc, [{f"in_{n}": a for n, a in arrays.items()}], core_ids=[0])
    return r.results[0][_OUT]
```

```python
from contextlib import ExitStack

import concourse.bass as bass
import numpy as np
from concourse import mybir

F32 = mybir.dt.float32
BF16 = mybir.dt.bfloat16
I32 = mybir.dt.int32
U32 = mybir.dt.uint32
U8 = mybir.dt.uint8
ALU = mybir.AluOpType
ACT = mybir.ActivationFunctionType
AX = mybir.AxisListType.X
DVE_ENGINE = mybir.EngineType.DVE
PE_ENGINE = mybir.EngineType.PE
ACT_ENGINE = mybir.EngineType.Activation

P = 128
N_NODES = 3125
D = 256
KC = D // P
NB = -(-N_NODES // P)
FEAT_ROWS = 96
LAST = N_NODES - (NB - 1) * P
N_LOOPS = 625
N_EDGES = 50000
COLS = -(-N_EDGES // P)
E_PAD = COLS * P
ROWS = E_PAD + P
U = 8
T = -(-(N_EDGES // P + NB) // U) * U
TURNS = T // U
assert TURNS % 2 == 0
CH = 4
TP = CH * P
NO_NODE = NB * P
G = 5
assert NB % G == 0
BANK = 512
BIG = 1e30
EPS = 1e-5
HW = 8
ACCS = 4
DUMP = NB * P
assert T <= TP and ROWS >= N_EDGES + P


class Signal:

    def __init__(self, sem):
        self.sem = sem
        self.base = 0

    def at(self, count):
        return count + self.base

    def phase_ends(self, counted):
        self.base += counted


def chain(engine, sig):
    count = [0]

    def step(ins):
        count[0] += 1
        ins.then_inc(sig.sem, 1)
        engine.wait_ge(sig.sem, sig.at(count[0]))
        return count[0]

    step.count = count
    return step


def stand_alone(engine, passed):
    engine.sem_inc(passed.sem, 1)


def folded_size(n, times):
    for _ in range(times):
        n -= n // 2
    return n


class Steps:

    def __init__(self, engine, sig, per):
        self.engine, self.sig, self.per = engine, sig, per

    def turn(self, n):
        self.n, self.c = n, 0

    def __call__(self, ins, apart=None):
        self.c += 1
        assert self.c <= self.per
        ins.then_inc(self.sig.sem, 1)
        self.engine.wait_ge(self.sig.sem, self.sig.at(self.n * self.per + self.c))
        if apart is not None:
            stand_alone(self.engine, apart)


def over_tiles(engine, turn):
    turn(0, True)
    with engine.Fori(1, TURNS) as i:
        turn(i, False)


def over_double_turns(engine, turn):
    turn(0, True)
    with engine.Fori(1, TURNS // 2) as i:
        turn(i, False)


def slot_turn(n, slot):
    return n // 2 + 1 if isinstance(n, int) else (n + 2 - slot) // 2


def over_blocks(engine, one):
    one(0, 0, True)
    one(1, 1, True)
    with engine.Fori(1, NB // 2) as i:
        one(2 * i, 0, False)
        one(2 * i + 1, 1, False)
    one(NB - 1, 0, False)


def over_blocks_ahead(engine, begin, end):
    begin(0, 0, True)
    begin(1, 1, True)
    end(0, 0, True)
    begin(2, 0, False)
    end(1, 1, True)
    with engine.Fori(1, NB // 2) as i:
        begin(2 * i + 1, 1, False)
        end(2 * i, 0, False)
        begin(2 * i + 2, 0, False)
        end(2 * i + 1, 1, False)
    end(NB - 1, 0, False)


def over_blocks_two_ahead(engine, begin, end):
    for n in range(3):
        begin(n, n % 2, n < 2)
    end(0, 0, True)
    begin(3, 1, False)
    end(1, 1, True)
    with engine.Fori(1, NB // 2 - 1) as i:
        begin(2 * i + 2, 0, False)
        end(2 * i, 0, False)
        begin(2 * i + 3, 1, False)
        end(2 * i + 1, 1, False)
    begin(NB - 1, 0, False)
    end(NB - 3, 0, False)
    end(NB - 2, 1, False)
    end(NB - 1, 0, False)


class Layer:
    def __init__(self, name, heads, cols, w, a, b=None, loops=False, edge_feats=False):
        self.name, self.heads, self.cols, self.w, self.a, self.b = name, heads, cols, w, a, b
        self.loops, self.edge_feats = loops, edge_feats
        self.wcols = 2 * heads if loops else heads


def gnn_kernel(nc, t, out):
    ctx = ExitStack()
    with ctx:
        def dram(name, shape, dt):
            return nc.dram_tensor(name, shape, dt, kind="Internal").ap()

        def sb(name, shape, dt=F32):
            return ctx.enter_context(nc.sbuf_tensor(name, shape, dt))

        def signal(name):
            return Signal(ctx.enter_context(nc.semaphore(name)))

        edge_ids = dram("edge_ids", [ROWS, 2], I32)
        edge_vals = dram("edge_vals", [ROWS, 4], F32)
        table = {w: dram(f"table{w}", [NB * P, w], F32) for w in (D, 2 * D)}
        sums = [dram(f"sums{k}", [DUMP + P, D], F32) for k in range(ACCS)]
        dst_rows = dram("dst_rows", [1, TP * P], BF16)
        src_rows = dram("src_rows", [1, TP * P], BF16)
        src_ids = dram("src_ids", [1, TP * P], F32)
        feat_rows = dram("feat_rows", [9, TP * P], BF16)
        key_list = dram("key_list", [1, E_PAD], F32)
        block_row = dram("block_row", [1, TP], I32)
        ends = dram("ends", [2, TP + 2], F32)

        x = sb("x", [P, NB, D])
        acc = sb("acc", [P, NB, 2 * D + HW])
        node_rows = acc[:, :, D + HW:2 * D + HW]
        node_parts = acc[:, :, 0:3 * D // 2].bitcast(BF16)
        logits = sb("logits", [P, 8, TP])
        weights = sb("weights", [P, T, HW])
        ones_row = sb("ones_row", [1, P])
        stats = sb("stats", [P, NB, 2])
        rstd = sb("rstd", [P, NB])
        root_t = sb("root_t", [P, NB])
        att = sb("att", [P, NB, 2 * HW])
        src_hot = sb("src_hot", [P, T, NB], U8)
        src_u = sb("src_u", [P, T], U32)
        dst_in = sb("dst_in", [P, TP])
        src_f = sb("src_f", [P, TP])
        edge_w = sb("edge_w", [P, TP])
        keep = sb("keep", [P, T])
        block_of = sb("block_of", [1, TP], I32)
        loop_mask = sb("loop_mask", [P, NB])
        loop_pen = sb("loop_pen", [P, NB])
        ident = sb("ident", [P, P])
        iota_row = sb("iota_row", [P, P])
        iota_col = sb("iota_col", [P, 1])
        left_pen = sb("left_pen", [P, TP])
        right_pen = sb("right_pen", [P, TP])
        left_in = sb("left_in", [P, TP])
        right_in = sb("right_in", [P, TP])
        first = sb("first", [P, TP])
        tile_left_pen = sb("tile_left_pen", [8, TP])
        tile_right_pen = sb("tile_right_pen", [8, TP])

        psum = ctx.enter_context(nc.psum_tensor("psum", [P, 8, 512], F32))

        ds = [signal(f"sw_dma_{i}") for i in range(8)]
        hs = [signal(f"sp_dma_{i}") for i in range(8)]
        hload = signal("load_landed")
        hstore = signal("store_landed")
        dve_done = signal("dve_done")
        pool_done = signal("pool_done")
        named = {}

        def signals(phase, names):
            for name in names.split():
                if (phase, name) not in named:
                    named[phase, name] = signal(f"{phase}_{name}")
            return [named[phase, name] for name in names.split()]

        passed = signal("waits_passed")
        order_rows = signal("order_rows_loaded")
        order_keyed = signal("order_keys_made")
        order_key = signal("order_keys_stored")
        order_in = signal("order_chunk_landed")
        order_ranked = signal("order_chunk_counted")
        order_step = signal("order_step_done")
        order_staged = signal("order_column_staged")
        order_out = signal("order_column_scattered")


        V, A, PE, POOL, SP = nc.vector, nc.scalar, nc.tensor, nc.gpsimd, nc.sync

        def tiles_first(ap):
            return ap.rearrange("o (c p i) -> p (o c) i", c=CH, p=P)

        def row(ap, n):
            return ap[:, bass.ds(n, 1), :].rearrange("p o d -> p (o d)")

        def order_phase():
            (loaded, copied, chunk_in, staged, ranked) = (hload, hstore, order_in, order_staged, order_ranked)
            (keyed, counted, flagged, ones_set) = signals("order", "summed counted flagged ones_set")
            CHUNK = E_PAD // 8
            with ExitStack() as scope:
                def tmp(name, shape, dt=F32):
                    return scope.enter_context(nc.sbuf_tensor(name, shape, dt))

                dst_i = tmp("order_dst", [P, 2, COLS], I32)
                dst_f = tmp("order_dst_f", [P, 2, COLS])
                falls = tmp("order_falls", [P, COLS])
                n_falls = tmp("order_n_falls", [P, 1])
                ones = tmp("order_ones", [P, P])
                flag_f = tmp("order_flag_f", [P, 1])
                flag_i = tmp("order_flag_i", [P, 1], I32)
                key = tmp("order_key", [P, COLS])
                rank = tmp("order_rank", [P, COLS])
                column_i = tmp("order_column_i", [P, COLS], I32)
                column = tmp("order_column", [P, COLS])
                less = tmp("order_less", [P, COLS])
                count = tmp("order_count", [P, 2])
                lane_i = tmp("order_lane_i", [P, 1], I32)
                lane = tmp("order_lane", [P, 1])
                ids = tmp("order_ids", [P, COLS, 2], I32)
                vals = tmp("order_vals", [P, COLS, 4])
                one_rank = tmp("order_one_rank", [P, 1], U32)
                one_ids = tmp("order_one_ids", [P, 2], I32)
                one_vals = tmp("order_one_vals", [P, 4])
                room = acc[:, :, :].rearrange("p n d -> p (n d)")
                chunk, junk = room[:, 0:CHUNK], room[:, CHUNK:2 * CHUNK]

                def flat(ap, rows):
                    return ap[0:rows, :].rearrange("(p r) f -> p r f", p=P)

                def unsorted(engine):
                    return engine.If(engine.value_load(flag_i[0:1, 0:1], min_val=0, max_val=1) > 0)

                with nc.Block() as block:
                    @block.sync
                    def _(sp):
                        sp.dma_start(dst_i[:, 0, :], t["dst_list"][0:1, 0:E_PAD].rearrange("o (p c) -> (o p) c", p=P),
                                     ).then_inc(loaded.sem, 16)
                        sp.dma_start(dst_i[:, 1, :], t["dst_list"][0:1, 1:E_PAD + 1].rearrange("o (p c) -> (o p) c", p=P),
                                     ).then_inc(loaded.sem, 16)
                        for to, of in ((edge_ids, t["edge_ids"]), (edge_vals, t["edge_vals"])):
                            sp.dma_start(flat(to, ROWS).rearrange("p r f -> p (r f)"),
                                         flat(of, ROWS).rearrange("p r f -> p (r f)")).then_inc(copied.sem, 16)
                        sp.wait_ge(copied.sem, copied.at(32))
                        sp.wait_ge(flagged.sem, flagged.at(1))
                        with unsorted(sp):
                            sp.dma_start(ids[:, :, :], flat(t["edge_ids"], E_PAD)).then_inc(order_rows.sem, 16)
                            sp.dma_start(vals[:, :, :], flat(t["edge_vals"], E_PAD)).then_inc(order_rows.sem, 16)
                            sp.wait_ge(order_keyed.sem, order_keyed.at(1))
                            sp.dma_start(key_list.rearrange("o (p c) -> (o p) c", p=P), key[:, :]).then_inc(order_key.sem, 16)
                            sp.wait_ge(order_key.sem, order_key.at(16))
                            with sp.Fori(0, E_PAD // CHUNK) as c:
                                sp.wait_ge(ranked.sem, ranked.at(c + 1))
                                sp.dma_start(chunk, key_list[0:1, bass.ds(c * CHUNK, CHUNK)].broadcast_to([P, CHUNK]),
                                             ).then_inc(chunk_in.sem, 16)
                            sp.wait_ge(order_rows.sem, order_rows.at(32))

                    @block.gpsimd
                    def _(pool):
                        step = chain(pool, pool_done)
                        step(POOL.iota(column_i[:, :], [[1, COLS]], base=0, channel_multiplier=0))
                        step(POOL.tensor_copy(column[:, :], column_i[:, :]))
                        step(POOL.iota(lane_i[:, :], [[1, 1]], base=0, channel_multiplier=1))
                        step(POOL.tensor_copy(lane[:, :], lane_i[:, :]))
                        POOL.memset(ones[:, :], 1.0).then_inc(ones_set.sem, 1)
                        pool.wait_ge(flagged.sem, flagged.at(1))
                        with unsorted(pool):
                            with pool.Fori(0, COLS) as j:
                                pool.wait_ge(staged.sem, staged.at(j + 1))
                                stand_alone(pool, passed)
                                pool.indirect_dma_start(
                                    edge_ids, bass.IndirectOffsetOnAxis(ap=one_rank[:, :], axis=0), one_ids[:, :], None,
                                ).then_inc(order_out.sem, 16)
                                pool.indirect_dma_start(
                                    edge_vals, bass.IndirectOffsetOnAxis(ap=one_rank[:, :], axis=0), one_vals[:, :], None,
                                ).then_inc(order_out.sem, 16)
                                pool.wait_ge(order_out.sem, order_out.at(32 * (j + 1)))
                                stand_alone(pool, passed)

                    @block.tensor
                    def _(pe):
                        pe.wait_ge(ones_set.sem, ones_set.at(1))
                        pe.wait_ge(counted.sem, counted.at(1))
                        PE.matmul(psum[:, 0, 0:1], ones[:, :], n_falls[:, :], start=True, stop=True).then_inc(keyed.sem, 1)

                    @block.vector
                    def _(dve):
                        step = chain(dve, dve_done)
                        dve.wait_ge(loaded.sem, loaded.at(32))
                        step(V.tensor_copy(dst_f[:, :, :], dst_i[:, :, :]))
                        step(V.tensor_tensor(falls[:, :], dst_f[:, 0, :], dst_f[:, 1, :], ALU.is_gt))
                        V.reduce_sum(n_falls[:, :], falls[:, :], AX).then_inc(counted.sem, 1)
                        dve.wait_ge(keyed.sem, keyed.at(1))
                        step(V.tensor_scalar_min(flag_f[:, :], psum[:, 0, 0:1], 1.0))
                        V.tensor_copy(flag_i[:, :], flag_f[:, :]).then_inc(flagged.sem, 1)
                        dve_done.phase_ends(step.count[0])
                        dve.wait_ge(flagged.sem, flagged.at(1))
                        with unsorted(dve):
                            V.tensor_scalar(key[:, :], dst_f[:, 0, :], float(P), lane[:, :], ALU.mult, ALU.add,
                                            ).then_inc(order_keyed.sem, 1)
                            V.memset(rank[:, :], 0.0).then_inc(ranked.sem, 1)
                            dve.wait_ge(order_keyed.sem, order_keyed.at(1))
                            with dve.Fori(0, E_PAD // CHUNK) as c:
                                dve.wait_ge(chunk_in.sem, chunk_in.at(16 * (c + 1)))
                                stand_alone(dve, passed)
                                with dve.Fori(0, COLS) as j:
                                    V.tensor_scalar(junk, chunk, key[:, bass.ds(j, 1)], 0.0, ALU.is_lt, ALU.add,
                                                    accum_out=count[:, 0:1]).then_inc(order_step.sem, 1)
                                    dve.wait_ge(order_step.sem, order_step.at(c * (2 * COLS) + j * 2 + 1))
                                    V.tensor_tensor(rank[:, bass.ds(j, 1)], rank[:, bass.ds(j, 1)], count[:, 0:1], ALU.add,
                                                    ).then_inc(order_step.sem, 1)
                                    dve.wait_ge(order_step.sem, order_step.at(c * (2 * COLS) + j * 2 + 2))
                                V.memset(count[:, 0:1], 0.0).then_inc(ranked.sem, 1)
                            dve.wait_ge(order_rows.sem, order_rows.at(32))
                            done = E_PAD // CHUNK * 2 * COLS
                            with dve.Fori(0, COLS) as j:
                                V.tensor_scalar(less[:, :], column[:, :], column[:, bass.ds(j, 1)], None, ALU.is_lt,
                                                ).then_inc(order_step.sem, 1)
                                dve.wait_ge(order_step.sem, order_step.at(done + j * 2 + 1))
                                V.scalar_tensor_tensor(junk[:, 0:COLS], dst_f[:, 0, :], dst_f[:, 0, bass.ds(j, 1)], less[:, :],
                                                       ALU.is_equal, ALU.mult, accum_out=count[:, 1:2]).then_inc(order_step.sem, 1)
                                dve.wait_ge(order_step.sem, order_step.at(done + j * 2 + 2))
                                V.tensor_tensor(one_rank[:, :], rank[:, bass.ds(j, 1)], count[:, 1:2], ALU.add)
                                V.tensor_copy(one_ids[:, :], row(ids, j))
                                V.tensor_copy(one_vals[:, :], row(vals, j)).then_inc(staged.sem, 1)
                                dve.wait_ge(staged.sem, staged.at(j + 1))
                                dve.wait_ge(order_out.sem, order_out.at(32 * (j + 1)))
                                stand_alone(dve, passed)
            for sig, n in ((loaded, 32), (copied, 32), (keyed, 1), (counted, 1), (flagged, 1), (ones_set, 1), (pool_done, 4)):
                sig.phase_ends(n)

        def edge_phase():
            (loaded, gathered, rows_out, rows_in, feats_out) = (hload, ds[0], hs[0], hs[1], hs[2])
            (consts, counted, totalled, placed, tiled, ends_ready, t_ready, feats_split, ident_set) = signals(
                "edge", "consts_set counted totalled placed tiled ends_ready turned feats_split ident_set")
            with ExitStack() as scope:
                def tmp(name, shape, dt=F32):
                    return scope.enter_context(nc.sbuf_tensor(name, shape, dt))

                dst_cols = tmp("dst_cols", [P, COLS], I32)
                dst_f = tmp("dst_f", [P, COLS])
                below = tmp("below", [P, COLS])
                cnt = tmp("cnt", [P, NB])
                ones = tmp("ones", [P, P])
                start = tmp("start", [P, NB + 1])
                size = tmp("size", [P, NB])
                size_i = tmp("size_i", [P, NB], I32)
                n_tiles = tmp("n_tiles", [P, NB])
                tile0 = tmp("tile0", [P, NB + 1])
                shift = tmp("shift", [P, NB])
                dshift = tmp("dshift", [P, NB - 1])
                tile_i = tmp("tile_i", [P, CH], I32)
                tile_no = tmp("tile_no", [P, CH])
                past = tmp("past", [P, CH, NB - 1])
                prod = tmp("prod", [P, CH, NB - 1])
                block_t = tmp("block_t", [P, CH])
                block_i = tmp("block_i", [P, CH], I32)
                edge0 = tmp("edge0", [P, CH])
                valid = tmp("valid", [P, CH])
                clamped = tmp("clamped", [P, CH])
                edge0_u = tmp("edge0_u", [P, CH], U32)
                ids_t = tmp("ids_t", [P, CH, 2 * P], I32)
                vals_t = tmp("vals_t", [P, CH, 4 * P])
                iota_i = tmp("iota_i", [P, P], I32)
                dst_g = tmp("dst_g", [P, CH, P])
                dst_l = tmp("dst_l", [P, CH, P])
                inside = tmp("inside", [P, CH, P])
                src_i = tmp("src_i", [P, CH, P], I32)
                src_t = tmp("src_t", [P, CH, P])
                src_lo = tmp("src_lo", [P, CH, P])
                src_hi = tmp("src_hi", [P, CH, P])
                src_hi_e = tmp("src_hi_e", [P, TP])
                w_t = tmp("w_t", [P, CH, P])
                feat_t = tmp("feat_t", [P, 3, CH, P])
                room = acc[:, :, :].rearrange("p n d -> p (n d)")
                feat_b = room[:, 0:9 * TP // 2].bitcast(BF16).rearrange("p (a k c i) -> p a k c i", a=3, k=3, c=CH)
                src_lo_b = tmp("src_lo_b", [P, CH, P], BF16)
                dst_l_b = tmp("dst_l_b", [P, CH, P], BF16)
                same = tmp("same", [P, CH, P])
                prev_last = tmp("prev_last", [P, CH])
                next_first = tmp("next_first", [P, CH])
                none = tmp("none", [1, 2])
                firsts = tmp("firsts", [8, TP + 1])
                lasts = tmp("lasts", [8, TP + 1])
                first_c = tmp("first_c", [P, CH])
                last_c = tmp("last_c", [P, CH])
                prev_block = tmp("prev_block", [P, CH])
                keep_row = tmp("keep_row", [1, TP])
                block_f = tmp("block_f", [1, TP + 1])

                lp3 = left_pen[:, :].rearrange("p (c i) -> p c i", c=CH)
                rp3 = right_pen[:, :].rearrange("p (c i) -> p c i", c=CH)
                li3 = left_in[:, :].rearrange("p (c i) -> p c i", c=CH)
                ri3 = right_in[:, :].rearrange("p (c i) -> p c i", c=CH)
                fi3 = first[:, :].rearrange("p (c i) -> p c i", c=CH)
                turned = [src_t, dst_l, w_t, src_hi]

                with nc.Block() as block:
                    @block.sync
                    def _(sp):
                        sp.dma_start(dst_cols[:, :], t["dst_list"][0:1, 0:E_PAD].rearrange("o (p c) -> (o p) c", p=P),
                                     ).then_inc(loaded.sem, 16)
                        sp.wait_ge(tiled.sem, tiled.at(1))
                        sp.dma_start(tiles_first(dst_rows), dst_l_b[:, :, :]).then_inc(rows_out.sem, 16)
                        sp.dma_start(tiles_first(src_rows), src_lo_b[:, :, :]).then_inc(rows_out.sem, 16)
                        sp.dma_start(tiles_first(src_ids), src_t[:, :, :]).then_inc(rows_out.sem, 16)
                        sp.dma_start(block_row.rearrange("o (c p) -> p (o c)", p=P), block_i[:, :],
                                     allow_slow_non_contiguous=True).then_inc(rows_out.sem, 16)
                        sp.dma_start(ends[0:1, 1:TP + 1].rearrange("o (c p) -> p (o c)", p=P), first_c[:, :],
                                     allow_slow_non_contiguous=True).then_inc(rows_out.sem, 16)
                        sp.dma_start(ends[1:2, 1:TP + 1].rearrange("o (c p) -> p (o c)", p=P), last_c[:, :],
                                     allow_slow_non_contiguous=True).then_inc(rows_out.sem, 16)
                        sp.dma_start(ends[0:1, TP + 1:TP + 2], none[:, 0:1]).then_inc(rows_out.sem, 16)
                        sp.dma_start(ends[1:2, 0:1], none[:, 1:2]).then_inc(rows_out.sem, 16)
                        sp.wait_ge(rows_out.sem, rows_out.at(16 * 8))
                        sp.dma_start(prev_last[:, :], ends[1:2, 0:TP].rearrange("o (c p) -> p (o c)", p=P),
                                     allow_slow_non_contiguous=True).then_inc(rows_in.sem, 16)
                        sp.dma_start(next_first[:, :], ends[0:1, 2:TP + 2].rearrange("o (c p) -> p (o c)", p=P),
                                     allow_slow_non_contiguous=True).then_inc(rows_in.sem, 16)
                        sp.dma_start(firsts[:, :], ends[0:1, 1:TP + 2].broadcast_to([8, TP + 1])).then_inc(rows_in.sem, 16)
                        sp.dma_start(lasts[:, :], ends[1:2, 0:TP + 1].broadcast_to([8, TP + 1])).then_inc(rows_in.sem, 16)
                        sp.dma_start(block_of[:, :], block_row).then_inc(rows_in.sem, 16)
                        sp.wait_ge(feats_split.sem, feats_split.at(1))
                        for k in range(9):
                            sp.dma_start(tiles_first(feat_rows[k:k + 1, :]), feat_b[:, k // 3, k % 3, :, :],
                                         ).then_inc(feats_out.sem, 16)
                        sp.wait_ge(rows_in.sem, rows_in.at(16 * 5))
                        sp.wait_ge(feats_out.sem, feats_out.at(16 * 9))

                    @block.gpsimd
                    def _(pool):
                        step = chain(pool, pool_done)
                        step(POOL.iota(tile_i[:, :], [[P, CH]], base=0, channel_multiplier=1))
                        step(POOL.iota(iota_i[:, :], [[1, P]], base=0, channel_multiplier=0))
                        step(POOL.tensor_copy(tile_no[:, :], tile_i[:, :]))
                        step(POOL.tensor_copy(iota_col[:, :], tile_i[:, 0:1]))
                        step(POOL.memset(ones[:, :], 1.0))
                        POOL.tensor_copy(iota_row[:, :], iota_i[:, :]).then_inc(consts.sem, 1)
                        pool.wait_ge(consts.sem, consts.at(1))
                        POOL.tensor_scalar(ident[:, :], iota_row[:, :], iota_col[:, :], None, ALU.is_equal,
                                           ).then_inc(ident_set.sem, 1)
                        pool.wait_ge(placed.sem, placed.at(1))
                        for c in range(CH):
                            pool.indirect_dma_start(
                                ids_t[:, c, :], None, edge_ids,
                                bass.IndirectOffsetOnAxis(ap=edge0_u[:, c:c + 1], axis=0)).then_inc(gathered.sem, 16)
                            pool.indirect_dma_start(
                                vals_t[:, c, :], None, edge_vals,
                                bass.IndirectOffsetOnAxis(ap=edge0_u[:, c:c + 1], axis=0)).then_inc(gathered.sem, 16)
                        pool.wait_ge(gathered.sem, gathered.at(16 * 2 * CH))

                    @block.vector
                    def _(dve):
                        step = chain(dve, dve_done)
                        dve.wait_ge(loaded.sem, loaded.at(16))
                        step(V.tensor_copy(dst_f[:, :], dst_cols[:, :]))
                        for n in range(NB):
                            step(V.tensor_scalar(below[:, :], dst_f[:, :], float((n + 1) * P), 0.0, ALU.is_lt, ALU.add,
                                                 accum_out=cnt[:, n:n + 1]))
                        V.memset(start[:, 0:1], 0.0).then_inc(counted.sem, 1)
                        dve.wait_ge(totalled.sem, totalled.at(1))
                        step(V.tensor_copy(start[:, 1:NB + 1], psum[:, 0, 0:NB]))
                        step(V.tensor_tensor(size[:, :], start[:, 1:NB + 1], start[:, 0:NB], ALU.subtract))
                        step(V.tensor_scalar_add(size_i[:, :], size[:, :], float(P - 1)))
                        step(V.tensor_single_scalar(size_i[:, :], size_i[:, :], P.bit_length() - 1, ALU.arith_shift_right))
                        step(V.tensor_copy(n_tiles[:, :], size_i[:, :]))
                        step(V.memset(tile0[:, 0:1], 0.0))
                        dve.wait_ge(consts.sem, consts.at(1))
                        step(V.tensor_tensor_scan(tile0[:, 1:NB + 1], ones[:, 0:NB], n_tiles[:, :], 0.0, ALU.mult, ALU.add))
                        step(V.scalar_tensor_tensor(shift[:, :], tile0[:, 0:NB], float(-P), start[:, 0:NB], ALU.mult, ALU.add))
                        step(V.tensor_tensor(dshift[:, :], shift[:, 1:NB], shift[:, 0:NB - 1], ALU.subtract))
                        for c in range(CH):
                            step(V.tensor_scalar(past[:, c, :], tile0[:, 1:NB], tile_no[:, c:c + 1], None, ALU.is_le))
                        step(V.reduce_sum(block_t[:, :], past[:, :, :], AX))
                        step(V.tensor_tensor(prod[:, :, :], past[:, :, :],
                                             dshift[:, :].unsqueeze(1).broadcast_to([P, CH, NB - 1]), ALU.mult))
                        step(V.reduce_sum(edge0[:, :], prod[:, :, :], AX))
                        step(V.tensor_tensor(prod[:, :, :], past[:, :, :],
                                             size[:, 1:NB].unsqueeze(1).broadcast_to([P, CH, NB - 1]), ALU.mult))
                        step(V.reduce_sum(valid[:, :], prod[:, :, :], AX))
                        step(V.scalar_tensor_tensor(edge0[:, :], tile_no[:, :], float(P), edge0[:, :], ALU.mult, ALU.add))
                        step(V.scalar_tensor_tensor(valid[:, :], valid[:, :], start[:, 1:2], edge0[:, :], ALU.add, ALU.subtract))
                        step(V.tensor_scalar_min(clamped[:, :], edge0[:, :], float(ROWS - P)))
                        V.tensor_copy(edge0_u[:, :], clamped[:, :]).then_inc(placed.sem, 1)
                        step(V.tensor_copy(block_i[:, :], block_t[:, :]))
                        for c in range(CH):
                            step(V.tensor_scalar(inside[:, c, :], iota_row[:, :], valid[:, c:c + 1], None, ALU.is_lt))
                        dve.wait_ge(gathered.sem, gathered.at(16 * 2 * CH))
                        ids = ids_t[:, :, :].rearrange("p c (i f) -> p c i f", f=2)
                        vals = vals_t[:, :, :].rearrange("p c (i f) -> p c i f", f=4)
                        step(V.tensor_copy(src_i[:, :, :], ids[:, :, :, 0]))
                        step(V.tensor_copy(dst_g[:, :, :], ids[:, :, :, 1]))
                        step(V.tensor_copy(src_t[:, :, :], src_i[:, :, :]))
                        step(V.tensor_single_scalar(src_i[:, :, :], src_i[:, :, :], P - 1, ALU.bitwise_and))
                        step(V.tensor_copy(src_lo[:, :, :], src_i[:, :, :]))
                        step(V.tensor_copy(src_lo_b[:, :, :], src_lo[:, :, :]))
                        step(V.tensor_tensor(src_hi[:, :, :], src_t[:, :, :], src_lo[:, :, :], ALU.subtract))
                        step(V.tensor_scalar(src_hi[:, :, :], src_hi[:, :, :], 1.0 / P, None, ALU.mult))
                        step(V.tensor_scalar(block_t[:, :], block_t[:, :], float(P), None, ALU.mult))
                        for c in range(CH):
                            step(V.tensor_scalar(dst_l[:, c, :], dst_g[:, c, :], block_t[:, c:c + 1], None, ALU.subtract))
                        for d in (dst_g, dst_l):
                            step(V.scalar_tensor_tensor(d[:, :, :], d[:, :, :], 1.0, inside[:, :, :], ALU.add, ALU.mult))
                            step(V.tensor_scalar_add(d[:, :, :], d[:, :, :], -1.0))
                        step(V.tensor_copy(dst_l_b[:, :, :], dst_l[:, :, :]))
                        step(V.tensor_copy(w_t[:, :, :], vals[:, :, :, 0]))
                        step(V.tensor_copy(first_c[:, :], dst_g[:, :, 0]))
                        step(V.tensor_copy(last_c[:, :], dst_g[:, :, P - 1]))
                        V.memset(none[:, :], -5.0).then_inc(tiled.sem, 1)
                        step(V.tensor_tensor(same[:, :, 0:P - 1], dst_g[:, :, 0:P - 1], dst_g[:, :, 1:P], ALU.is_equal))
                        step(V.memset(lp3[:, :, 0:1], -BIG))
                        step(V.memset(rp3[:, :, P - 1:P], -BIG))
                        step(V.tensor_scalar(lp3[:, :, 1:P], same[:, :, 0:P - 1], -1.0, BIG, ALU.add, ALU.mult))
                        step(V.tensor_scalar(rp3[:, :, 0:P - 1], same[:, :, 0:P - 1], -1.0, BIG, ALU.add, ALU.mult))
                        step(V.tensor_scalar(fi3[:, :, 1:P], same[:, :, 0:P - 1], -1.0, 1.0, ALU.mult, ALU.add))
                        for k in range(3):
                            step(V.tensor_copy(feat_t[:, k, :, :], vals[:, :, :, k + 1]))
                        for part in range(3):
                            step(V.tensor_copy(feat_b[:, part, :, :, :], feat_t[:, :, :, :]))
                            if part < 2:
                                step(V.tensor_tensor(feat_t[:, :, :, :], feat_t[:, :, :, :], feat_b[:, part, :, :, :],
                                                     ALU.subtract))
                        V.memset(block_f[:, 0:1], -1.0).then_inc(feats_split.sem, 1)
                        dve.wait_ge(rows_in.sem, rows_in.at(16 * 5))
                        for c in range(CH):
                            step(V.tensor_scalar(li3[:, c, :], dst_g[:, c, :], prev_last[:, c:c + 1], None, ALU.is_equal))
                            step(V.tensor_scalar(ri3[:, c, :], dst_g[:, c, :], next_first[:, c:c + 1], None, ALU.is_equal))
                        step(V.tensor_scalar(fi3[:, :, 0:1], li3[:, :, 0:1], -1.0, 1.0, ALU.mult, ALU.add))
                        step(V.tensor_scalar(left_in[:, :], left_in[:, :], -1.0, BIG, ALU.add, ALU.mult))
                        step(V.tensor_scalar(right_in[:, :], right_in[:, :], -1.0, BIG, ALU.add, ALU.mult))
                        step(V.tensor_tensor(tile_left_pen[:, :], lasts[:, 0:TP], lasts[:, 1:TP + 1], ALU.is_equal))
                        step(V.tensor_tensor(tile_right_pen[:, :], firsts[:, 0:TP], firsts[:, 1:TP + 1], ALU.is_equal))
                        step(V.tensor_scalar(tile_left_pen[:, :], tile_left_pen[:, :], -1.0, BIG, ALU.add, ALU.mult))
                        step(V.tensor_scalar(tile_right_pen[:, :], tile_right_pen[:, :], -1.0, BIG, ALU.add, ALU.mult))
                        step(V.memset(block_f[:, 0:1], -1.0))
                        step(V.tensor_copy(block_f[:, 1:TP + 1], block_of[:, :]))
                        V.tensor_tensor(keep_row[:, :], block_f[:, 0:TP], block_f[:, 1:TP + 1], ALU.is_equal,
                                        ).then_inc(ends_ready.sem, 1)
                        for k, to in enumerate([src_f, dst_in, edge_w, src_hi_e]):
                            dve.wait_ge(t_ready.sem, t_ready.at(k + 1))
                            step(V.tensor_copy(to[:, :], psum[:, 1 + k, :]))
                        step(V.tensor_copy(src_u[:, :], src_f[:, 0:T]))
                        dve.wait_ge(t_ready.sem, t_ready.at(5))
                        step(V.tensor_copy(keep[:, :], psum[:, 5, 0:T]))
                        step(V.tensor_tensor(src_hot[:, :, :],
                                             src_hi_e[:, 0:T].unsqueeze(2).broadcast_to([P, T, NB]),
                                             iota_row[:, 0:NB].unsqueeze(1).broadcast_to([P, T, NB]), ALU.is_equal))
                        dve_done.phase_ends(step.count[0])

                    @block.tensor
                    def _(pe):
                        pe.wait_ge(consts.sem, consts.at(1))
                        pe.wait_ge(counted.sem, counted.at(1))
                        PE.matmul(psum[:, 0, 0:NB], ones[:, :], cnt[:, :], start=True, stop=True).then_inc(totalled.sem, 1)
                        pe.wait_ge(ident_set.sem, ident_set.at(1))
                        pe.wait_ge(tiled.sem, tiled.at(1))
                        for k, array in enumerate(turned):
                            for c in range(CH):
                                last = PE.transpose(psum[:, 1 + k, c * P:(c + 1) * P], array[:, c, :], ident[:, :])
                            last.then_inc(t_ready.sem, 1)
                        pe.wait_ge(ends_ready.sem, ends_ready.at(1))
                        PE.matmul(psum[:, 5, :], ones[0:1, :], keep_row[:, :], start=True, stop=True).then_inc(t_ready.sem, 1)
            for sig, n in ((loaded, 16), (gathered, 32 * CH), (rows_out, 16 * 8), (feats_out, 16 * 9), (feats_split, 1), (rows_in, 16 * 5), (consts, 1),
                           (counted, 1), (totalled, 1), (placed, 1), (tiled, 1), (ends_ready, 1), (t_ready, 5),
                           (ident_set, 1), (pool_done, 5)):
                sig.phase_ends(n)


        def refine_root(step):
            step(V.reciprocal(rstd[:, :], rstd[:, :]))
            step(V.tensor_tensor(root_t[:, :], rstd[:, :], rstd[:, :], ALU.mult))
            step(V.scalar_tensor_tensor(root_t[:, :], stats[:, :, 1], EPS, root_t[:, :], ALU.add, ALU.mult))
            step(V.tensor_scalar(root_t[:, :], root_t[:, :], -0.5, 1.5, ALU.mult, ALU.add))
            step(V.tensor_tensor(rstd[:, :], rstd[:, :], root_t[:, :], ALU.mult))

        def row_stats(dve, step, rows, n, bn, mv):
            step(V.bn_stats(bn[:, :], rows), apart=passed)
            step(V.bn_aggr(mv[:, :], bn[:, :]))
            step(V.tensor_copy(row(stats, n), mv[:, :]))

        def group(ap, g):
            return ap[:, bass.ds(g * G, G), :]

        def group_stats(step, rows, g, bn, mv):
            for b in range(G):
                ins = V.bn_stats(bn[:, b, :], row(rows, g * G + b))
            step(ins, apart=passed)
            for b in range(G):
                ins = V.bn_aggr(mv[:, b, :], bn[:, b, :])
            step(ins)
            step(V.tensor_copy(group(stats, g), mv[:, :, :]))

        def scatter_phase():
            (hot_ready, index_ready, m_ready, m_copied, out_ready, out_copied, consts) = signals(
                "scatter", "hot_made index_made combined combined_copied weighed weighed_copied consts_set")
            (rows_in, zeroed) = (hs[:2], hstore)
            with ExitStack() as scope:
                def tmp(name, shape, dt=F32):
                    return scope.enter_context(nc.sbuf_tensor(name, shape, dt))

                ids = tmp("ids_rows", [P, 2, 4 * P])
                equal = tmp("equal", [P, 2, 4 * P])
                hot_w = tmp("hot_w", [P, 2, 4 * P])
                tril = tmp("tril", [P, P])
                junk = tmp("junk", [P, 4, P])
                dup = tmp("dup", [P, 2, 4])
                move = tmp("move", [P, 2, 4])
                index = tmp("index", [P, 4, 4], U32)
                m_sb = tmp("m_sb", [P, 2, 4 * P])
                val = acc[:, :, :].rearrange("p n d -> p (n d)")[:, 0:16 * D].rearrange("p (s v) -> p s v", s=4)
                dump = tmp("dump", [P, 1])
                zero = tmp("zero", [P, (DUMP + P) // P * D // 2])
                SD = 4 * 3

                with nc.Block() as block:
                    @block.sync
                    def _(sp):
                        sp.dma_start(x[:, 0:NB - 1, :], t["x"][0:(NB - 1) * P, :].rearrange("(n p) d -> p n d", p=P),
                                     ).then_inc(hload.sem, 16)
                        sp.wait_ge(consts.sem, consts.at(1))
                        sp.dma_start(x[0:LAST, NB - 1, :], t["x"][(NB - 1) * P:N_NODES, :]).then_inc(hload.sem, 16)
                        for k in range(ACCS):
                            for half in sums[k].rearrange("(h p r) d -> h p (r d)", h=2, p=P):
                                sp.dma_start(half, zero[:, :]).then_inc(zeroed.sem, 16)

                        def turn(i, first):
                            for s in range(4):
                                if not (first and s < 2):
                                    sp.wait_ge(hot_ready.sem, hot_ready.at(4 * i + s - 1))
                                at = (4 * i + s) * (4 * P)
                                sp.dma_start(ids[:, s % 2, :], src_ids[0:1, bass.ds(at, 4 * P)].broadcast_to([P, 4 * P]),
                                             ).then_inc(rows_in[s % 2].sem, 16)
                        over_double_turns(sp, turn)
                        for h in range(2):
                            sp.wait_ge(rows_in[h].sem, rows_in[h].at(16 * TURNS))
                        sp.wait_ge(zeroed.sem, zeroed.at(16 * 2 * ACCS))

                    @block.gpsimd
                    def _(pool):
                        step = chain(pool, pool_done)
                        step(POOL.memset(zero[:, :], 0.0))
                        step(POOL.memset(x[:, NB - 1, :], 0.0))
                        step(POOL.memset(ones_row[:, :], 1.0))
                        step(POOL.memset(tril[:, :], 1.0))
                        whole, part = divmod(N_LOOPS, P)
                        step(POOL.memset(loop_mask[:, :], 0.0))
                        step(POOL.memset(loop_mask[:, 0:whole], 1.0))
                        step(POOL.tensor_scalar(loop_mask[:, whole:whole + 1], iota_col[:, :], float(part), None, ALU.is_lt))
                        step(POOL.tensor_scalar(loop_pen[:, :], loop_mask[:, :], -1.0, BIG, ALU.add, ALU.mult))
                        step(POOL.tensor_scalar(dump[:, :], iota_col[:, :], float(DUMP), None, ALU.add))
                        POOL.tensor_scalar(tril[:, :], iota_row[:, :], iota_col[:, :], None, ALU.is_lt).then_inc(consts.sem, 1)
                        pool.wait_ge(zeroed.sem, zeroed.at(16 * 2 * ACCS))

                        def turn(i, first):
                            for s in range(4):
                                k = 4 * i + s
                                pool.wait_ge(index_ready.sem, index_ready.at(k + 1))
                                pool.wait_ge(out_copied.sem, out_copied.at(k + 1))
                                for j in range(4):
                                    if not (first and s == 0):
                                        pool.wait_ge(ds[j].sem, ds[j].at(16 * k))
                                        stand_alone(pool, passed)
                                    pool.indirect_dma_start(
                                        sums[j], bass.IndirectOffsetOnAxis(ap=index[:, s, j:j + 1], axis=0),
                                        val[:, s, j * D:(j + 1) * D], None, compute_op=ALU.add,
                                    ).then_inc(ds[j].sem, 16)
                        over_double_turns(pool, turn)
                        for j in range(4):
                            pool.wait_ge(ds[j].sem, ds[j].at(16 * 2 * TURNS))

                    @block.vector
                    def _(dve):
                        step = Steps(dve, dve_done, SD)
                        dve.wait_ge(consts.sem, consts.at(1))

                        def turn(i, first):
                            step.turn(i)
                            for s in range(4):
                                k, h = 4 * i + s, s % 2
                                tile = 4 * k
                                dve.wait_ge(rows_in[h].sem, rows_in[h].at(16 * (2 * i + s // 2 + 1)))
                                if not (first and s < 2):
                                    dve.wait_ge(m_ready.sem, m_ready.at(k - 1))
                                for j in range(4):
                                    V.tensor_scalar(equal[:, h, j * P:(j + 1) * P], ids[:, h, j * P:(j + 1) * P],
                                                    src_f[:, bass.ds(tile + j, 1)], None, ALU.is_equal)
                                    ins = V.tensor_scalar(hot_w[:, h, j * P:(j + 1) * P], iota_row[:, :],
                                                          dst_in[:, bass.ds(tile + j, 1)], edge_w[:, bass.ds(tile + j, 1)],
                                                          ALU.is_equal, ALU.mult)
                                ins.then_inc(hot_ready.sem, 1)
                                dve.wait_ge(hot_ready.sem, hot_ready.at(k + 1))
                                for j in range(4):
                                    ins = V.scalar_tensor_tensor(junk[:, j, :], equal[:, h, j * P:(j + 1) * P], 1.0,
                                                                 tril[:, :], ALU.mult, ALU.mult, accum_out=dup[:, h, j:j + 1])
                                step(ins)
                                step(V.tensor_scalar(move[:, h, :], src_f[:, bass.ds(tile, 4)], -1.0, dump[:, :],
                                                     ALU.mult, ALU.add))
                                step(V.scalar_tensor_tensor(dup[:, h, :], dup[:, h, :], 1.0, move[:, h, :], ALU.min, ALU.mult))
                                if not first:
                                    for j in range(4):
                                        dve.wait_ge(ds[j].sem, ds[j].at(16 * (k - 3)))
                                V.tensor_tensor(index[:, s, :], dup[:, h, :], src_f[:, bass.ds(tile, 4)],
                                                ALU.add).then_inc(index_ready.sem, 1)
                        over_double_turns(dve, turn)

                    @block.tensor
                    def _(pe):
                        pe.wait_ge(hload.sem, hload.at(32))

                        def combine(k, h, first):
                            pe.wait_ge(hot_ready.sem, hot_ready.at(k + 1))
                            if not first:
                                pe.wait_ge(m_copied.sem, m_copied.at(k - 1))
                            for j in range(4):
                                cut = slice(j * P, (j + 1) * P)
                                ins = PE.matmul(psum[:, h, cut], hot_w[:, h, cut], equal[:, h, cut], start=True, stop=True)
                            ins.then_inc(m_ready.sem, 1)

                        def weigh(k, h, first, blk):
                            pe.wait_ge(m_copied.sem, m_copied.at(k + 1))
                            if not first:
                                pe.wait_ge(out_copied.sem, out_copied.at(k - 1))
                            for j in range(4):
                                ins = PE.matmul(psum[:, 2 + 2 * h + j // 2, (j % 2) * D:(j % 2 + 1) * D],
                                                m_sb[:, h, j * P:(j + 1) * P],
                                                x[:, bass.ds(blk[j], 1), :].rearrange("p o d -> p (o d)"),
                                                start=True, stop=True)
                            ins.then_inc(out_ready.sem, 1)

                        def turn(i, first, last=False):
                            _, blk = nc.values_load_multi_w_load_instructions(
                                block_of[0:1, bass.ds(i * (2 * U), 2 * U)], engines=[PE_ENGINE], min_val=0, max_val=NB - 1,
                                skip_runtime_bounds_check_because="blocks are counted on the chip, below NB")
                            for s in range(4):
                                if not (last and s == 3):
                                    combine(4 * i + s + 1, (s + 1) % 2, first and s == 0)
                                weigh(4 * i + s, s % 2, first and s < 2, blk[4 * s:4 * s + 4])
                        combine(0, 0, True)
                        turn(0, True)
                        with pe.Fori(1, TURNS // 2 - 1) as i:
                            turn(i, False)
                        turn(TURNS // 2 - 1, False, last=True)

                    @block.scalar
                    def _(act):
                        def combined(k, h, first):
                            act.wait_ge(m_ready.sem, m_ready.at(k + 1))
                            if not first:
                                act.wait_ge(out_ready.sem, out_ready.at(k - 1))
                            A.copy(m_sb[:, h, :], psum[:, h, :]).then_inc(m_copied.sem, 1)

                        def weighed(k, s, first):
                            h = s % 2
                            act.wait_ge(out_ready.sem, out_ready.at(k + 1))
                            if not first:
                                for j in range(4):
                                    act.wait_ge(ds[j].sem, ds[j].at(16 * (k - 3)))
                            A.copy(val[:, s, :], psum[:, 2 + 2 * h:4 + 2 * h, :].rearrange("p b f -> p (b f)"),
                                   ).then_inc(out_copied.sem, 1)

                        def turn(i, first, last=False):
                            for s in range(4):
                                if not (last and s == 3):
                                    combined(4 * i + s + 1, (s + 1) % 2, first and s == 0)
                                weighed(4 * i + s, s, first)
                        combined(0, 0, True)
                        turn(0, True)
                        with act.Fori(1, TURNS // 2 - 1) as i:
                            turn(i, False)
                        turn(TURNS // 2 - 1, False, last=True)
            for sig in (hot_ready, index_ready, m_ready, m_copied, out_ready, out_copied):
                sig.phase_ends(2 * TURNS)
            for sig, n in ((hload, 32), (zeroed, 32 * ACCS), (consts, 1), (pool_done, 9), (dve_done, SD * TURNS // 2),
                           *((d, 32 * TURNS) for d in ds[:4]), *((d, 16 * TURNS) for d in rows_in)):
                sig.phase_ends(n)

        def first_layer_nodes():
            (turned, copied, produced, summed) = signals("first", "turned copied produced summed")
            loaded_w = hload
            slot_in = hs[:2]
            with ExitStack() as scope:
                def tmp(name, shape, dt=F32):
                    return scope.enter_context(nc.sbuf_tensor(name, shape, dt))

                w_sb = tmp("w0_sb", [P, KC, D])
                b_sb = tmp("b0_sb", [1, D])
                part = tmp("part", [P, 2, ACCS, D])
                sum_t = tmp("sum_t", [P, 2, KC * P])
                bn = tmp("bn", [P, 6])
                mv = tmp("mv", [P, 2])
                SD = 3

                with nc.Block() as block:
                    @block.sync
                    def _(sp):
                        sp.dma_start(w_sb[:, :, :], t["w0"].rearrange("(k p) o -> p k o", p=P)).then_inc(loaded_w.sem, 16)
                        sp.dma_start(b_sb[:, :], t["b0"]).then_inc(loaded_w.sem, 16)

                        def one(n, s, first):
                            if not first:
                                sp.wait_ge(turned.sem, turned.at(n - 1))
                            for k in range(ACCS):
                                sp.dma_start(part[:, s, k, :], sums[k][bass.ds(n * P, P), :]).then_inc(slot_in[s].sem, 16)
                        over_blocks(sp, one)

                    @block.tensor
                    def _(pe):
                        pe.wait_ge(loaded_w.sem, loaded_w.at(32))

                        def turn_over(n, s, first):
                            pe.wait_ge(slot_in[s].sem, slot_in[s].at(16 * ACCS * slot_turn(n, s)))
                            if not first:
                                pe.wait_ge(copied.sem, copied.at(n - 1))
                            for c in range(KC):
                                for k in range(ACCS):
                                    ins = PE.matmul(psum[:, s, c * P:(c + 1) * P], part[:, s, k, c * P:(c + 1) * P],
                                                    ident[:, :], start=k == 0, stop=k == ACCS - 1)
                            ins.then_inc(turned.sem, 1)

                        def product(n, s, first):
                            pe.wait_ge(copied.sem, copied.at(n + 1))
                            if not first:
                                pe.wait_ge(summed.sem, summed.at(n - 1))
                            for c in range(KC):
                                PE.matmul(psum[:, 2 + s, 0:D], sum_t[:, s, c * P:(c + 1) * P], w_sb[:, c, :],
                                          start=c == 0, stop=False)
                            PE.matmul(psum[:, 2 + s, 0:D], ones_row[:, :], b_sb[:, :], start=False, stop=True,
                                      ).then_inc(produced.sem, 1)
                        over_blocks_ahead(pe, turn_over, product)

                    @block.scalar
                    def _(act):
                        def one(n, s, first):
                            act.wait_ge(turned.sem, turned.at(n + 1))
                            if not first:
                                act.wait_ge(produced.sem, produced.at(n - 1))
                            A.copy(sum_t[:, s, :], psum[:, s, 0:KC * P]).then_inc(copied.sem, 1)
                        over_blocks(act, one)

                    @block.vector
                    def _(dve):
                        step = Steps(dve, dve_done, SD)

                        def one(n, s, first):
                            step.turn(n)
                            xn = x[:, bass.ds(n, 1), :].rearrange("p o d -> p (o d)")
                            dve.wait_ge(produced.sem, produced.at(n + 1))
                            V.tensor_tensor(xn, xn, psum[:, 2 + s, 0:D], ALU.add).then_inc(summed.sem, 1)
                            dve.wait_ge(summed.sem, summed.at(n + 1))
                            stand_alone(dve, passed)
                            row_stats(dve, step, xn, n, bn, mv)
                        over_blocks(dve, one)
            for sig in (turned, copied, produced, summed):
                sig.phase_ends(NB)
            for sig, n in ((loaded_w, 32), (dve_done, SD * NB), (slot_in[0], 16 * ACCS * (NB // 2 + 1)),
                           (slot_in[1], 16 * ACCS * (NB // 2))):
                sig.phase_ends(n)


        def project(L, rows_of, affine, es_tab, ed_tab):
            (normed, turned, copied, produced, rows_ready, att_ready, varied, rooted, attended, kept, parted) = signals(
                "project", "normed turned copied produced rows_ready att_ready varied rooted attended kept parted")
            staged = L.cols > D or L.edge_feats
            stored = hs[:2]
            H, C = L.heads, L.cols
            with ExitStack() as scope:
                def tmp(name, shape, dt=F32):
                    return scope.enter_context(nc.sbuf_tensor(f"{L.name}_{name}", shape, dt))

                w_sb = tmp("w", [P, KC, C])
                a_sb = tmp("a", [P, 2, C])
                prod = tmp("prod", [P, KC, C])
                w_x = tmp("wx", [P, KC, 2 * H])
                g_sb = tmp("g", [P, 2, D]) if affine else None
                y_sb = tmp("y", [P, 2, D])
                x_t = tmp("xt", [P, 2, KC * P])
                wide = tmp("wide", [P, 2, C]) if staged else None
                left = tmp("left", [P, 2, C]) if L.edge_feats else None
                rest = tmp("rest", [P, NB * H])
                own = tmp("own", [P, NB, 2 * H])
                n_loads = 3 + 2 * affine

                with nc.Block() as block:
                    @block.sync
                    def _(sp):
                        sp.dma_start(w_sb[:, :, :], t[L.w].rearrange("(k p) o -> p k o", p=P)).then_inc(hload.sem, 16)
                        for k in range(2):
                            sp.dma_start(a_sb[:, k, :], t[L.a[k]].broadcast_to([P, C])).then_inc(hload.sem, 16)
                        if affine:
                            sp.dma_start(g_sb[:, 0, :], t["ln_g"].broadcast_to([P, D])).then_inc(hload.sem, 16)
                            sp.dma_start(g_sb[:, 1, :], t["ln_b"].broadcast_to([P, D])).then_inc(hload.sem, 16)

                        def one(n, s, first):
                            sp.wait_ge(rows_ready.sem, rows_ready.at(n + 1))
                            sp.dma_start(table[C][bass.ds(n * P, P), :], wide[:, s, :] if staged else row(node_rows, n),
                                         ).then_inc(stored[s].sem, 16)
                        over_blocks(sp, one)
                        sp.wait_ge(stored[0].sem, stored[0].at(16 * (NB // 2 + 1)))
                        sp.wait_ge(stored[1].sem, stored[1].at(16 * (NB // 2)))

                    @block.vector
                    def _(dve):
                        step = Steps(dve, dve_done, 4 + 5)
                        step.turn(0)
                        V.tensor_scalar_add(rstd[:, :], stats[:, :, 1], EPS).then_inc(varied.sem, 1)
                        dve.wait_ge(rooted.sem, rooted.at(1))
                        refine_root(step)
                        dve.wait_ge(hload.sem, hload.at(16 * n_loads))
                        for side in range(2):
                            for k in range(KC):
                                ins = V.tensor_tensor(prod[:, k, :], w_sb[:, k, :], a_sb[:, side, :], ALU.mult)
                            step(ins)
                            for k in range(KC):
                                ins = V.reduce_sum(w_x[:, k, side * H:(side + 1) * H],
                                                   prod[:, k, :].rearrange("p (h d) -> p h d", h=H), AX)
                            step(ins)
                        V.memset(prod[:, 0, 0:1], 0.0).then_inc(attended.sem, 1)
                        assert step.c == step.per
                        dve_done.phase_ends(step.per)
                        step = Steps(dve, dve_done, 3 if affine else 2 if L.edge_feats else 0)

                        def norm(n, s, first):
                            step.turn(n)
                            y = y_sb[:, s, :]
                            if not first:
                                dve.wait_ge(turned.sem, turned.at(n - 1))
                                if not affine:
                                    dve.wait_ge(kept.sem, kept.at(n - 1))
                            ins = V.tensor_scalar(y, rows_of(n), stats[:, bass.ds(n, 1), 0], rstd[:, bass.ds(n, 1)],
                                                   ALU.subtract, ALU.mult)
                            if affine:
                                step(ins)
                                step(V.tensor_tensor(y, y, g_sb[:, 0, :], ALU.mult))
                                step(V.tensor_tensor(y, y, g_sb[:, 1, :], ALU.add))
                                ins = V.tensor_scalar_max(y, y, 0.0)
                            ins.then_inc(normed.sem, 1)

                        def late(n, s, first):
                            dve.wait_ge(produced.sem, produced.at(n + 1))
                            V.tensor_copy(row(att, n)[:, 0:2 * H], psum[:, 3 + 2 * s, 0:2 * H]).then_inc(att_ready.sem, 1)
                            if L.edge_feats:
                                step.turn(n)
                                dve.wait_ge(rows_ready.sem, rows_ready.at(n + 1))
                                parts = [row(node_parts, n)[:, k * D:(k + 1) * D] for k in range(3)]
                                step(V.tensor_tensor(left[:, s, :], wide[:, s, :], parts[0], ALU.subtract))
                                step(V.tensor_copy(parts[1], left[:, s, :]))
                                V.tensor_tensor(parts[2], left[:, s, :], parts[1], ALU.subtract).then_inc(parted.sem, 1)

                        over_blocks_two_ahead(dve, norm, late)
                        dve_done.phase_ends(step.per * NB)
                        dve.wait_ge(att_ready.sem, att_ready.at(NB))
                        step = chain(dve, dve_done)
                        M = L.wcols
                        V.tensor_copy(rest[:, :].rearrange("p (n h) -> p n h", h=H), att[:, :, 0:H])
                        step(V.tensor_copy(own[:, :, 0:H], att[:, :, H:2 * H]))
                        if L.loops:
                            z = own[:, :, H:2 * H]
                            step(V.tensor_tensor(z, att[:, :, 0:H], att[:, :, H:2 * H], ALU.add))
                            step(V.scalar_tensor_tensor(z, z, 0.2, z, ALU.mult, ALU.max))
                            step(V.tensor_tensor(z, z, loop_mask[:, :].unsqueeze(2).broadcast_to([P, NB, H]), ALU.mult))
                            step(V.tensor_tensor(z, z, loop_pen[:, :].unsqueeze(2).broadcast_to([P, NB, H]), ALU.add))
                        for part in range(3):
                            V.tensor_copy(es_tab[:, part, :], rest[:, :])
                            step(V.tensor_copy(ed_tab[:, :, part, :], own[:, :, 0:M]))
                            if part < 2:
                                V.tensor_tensor(rest[:, :], rest[:, :], es_tab[:, part, :], ALU.subtract)
                                step(V.tensor_tensor(own[:, :, 0:M], own[:, :, 0:M], ed_tab[:, :, part, :], ALU.subtract))
                        dve_done.phase_ends(step.count[0])

                    @block.tensor
                    def _(pe):
                        pe.wait_ge(hload.sem, hload.at(16 * n_loads))
                        pe.wait_ge(attended.sem, attended.at(1))

                        def turn_over(n, s, first):
                            pe.wait_ge(normed.sem, normed.at(n + 1))
                            if not first:
                                pe.wait_ge(copied.sem, copied.at(n - 1))
                            for c in range(KC):
                                ins = PE.transpose(psum[:, s, c * P:(c + 1) * P], y_sb[:, s, c * P:(c + 1) * P], ident[:, :])
                            ins.then_inc(turned.sem, 1)

                        def product(n, s, first):
                            pe.wait_ge(copied.sem, copied.at(n + 1))
                            if not first:
                                pe.wait_ge(rows_ready.sem, rows_ready.at(n - 1))
                                pe.wait_ge(att_ready.sem, att_ready.at(n - 1))
                            for c in range(KC):
                                PE.matmul(psum[:, 2 + 2 * s, 0:C], x_t[:, s, c * P:(c + 1) * P], w_sb[:, c, :],
                                          start=c == 0, stop=c == KC - 1)
                            for c in range(KC):
                                ins = PE.matmul(psum[:, 3 + 2 * s, 0:2 * H], x_t[:, s, c * P:(c + 1) * P], w_x[:, c, :],
                                                start=c == 0, stop=c == KC - 1)
                            ins.then_inc(produced.sem, 1)
                        over_blocks_ahead(pe, turn_over, product)

                    if not affine:
                        @block.gpsimd
                        def _(pool):
                            def one(n, s, first):
                                pool.wait_ge(normed.sem, normed.at(n + 1))
                                stand_alone(pool, passed)
                                POOL.tensor_copy(rows_of(n), y_sb[:, s, :]).then_inc(kept.sem, 1)
                            over_blocks(pool, one)

                    @block.scalar
                    def _(act):
                        act.wait_ge(varied.sem, varied.at(1))
                        A.activation(rstd[:, :], rstd[:, :], ACT.Sqrt).then_inc(rooted.sem, 1)

                        def turned_in(n, s, first):
                            act.wait_ge(turned.sem, turned.at(n + 1))
                            if not first:
                                act.wait_ge(produced.sem, produced.at(n - 1))
                            A.copy(x_t[:, s, :], psum[:, s, 0:KC * P]).then_inc(copied.sem, 1)

                        def rows_out(n, s, first):
                            act.wait_ge(produced.sem, produced.at(n + 1))
                            if staged:
                                if L.edge_feats and not first:
                                    act.wait_ge(parted.sem, parted.at(n - 1))
                                if not first:
                                    act.wait_ge(stored[s].sem, stored[s].at(16 * (slot_turn(n, s) - 1)))
                                if L.edge_feats:
                                    A.copy(row(node_parts, n)[:, 0:D], psum[:, 2 + 2 * s, 0:C])
                                A.copy(wide[:, s, :], psum[:, 2 + 2 * s, 0:C]).then_inc(rows_ready.sem, 1)
                            else:
                                A.copy(row(node_rows, n), psum[:, 2 + 2 * s, 0:C]).then_inc(rows_ready.sem, 1)
                        over_blocks_ahead(act, turned_in, rows_out)
            for sig in (normed, turned, copied, produced, rows_ready, att_ready):
                sig.phase_ends(NB)
            if not affine:
                kept.phase_ends(NB)
            if L.edge_feats:
                parted.phase_ends(NB)
            for sig, n in ((varied, 1), (rooted, 1), (attended, 1), (hload, 16 * n_loads),
                           (stored[0], 16 * (NB // 2 + 1)), (stored[1], 16 * (NB // 2))):
                sig.phase_ends(n)

        def logit_phase(L, es_tab, ed_tab):
            (hot_s_made, hot_d_made, found, bank_read, selected, summed, es_added, pair_found, rectified, multiplied,
             q_summed, q_added, split, differed, columns_set, es_folded, q_folded, feats_set) = signals(
                "logit", "hot_s_made hot_d_made found bank_read selected es_summed es_added pair_found rectified "
                "multiplied q_summed q_added we_split differed columns_set es_folded q_folded feats_set")
            folding = pool_done
            hot_made = (hot_s_made, hot_d_made)
            H, M, FE = L.heads, L.wcols, L.edge_feats
            hots_by_act = (0, 1) if FE else (0,)
            es_folds = 2 if H == 8 and not FE else 0
            q_folds = 2 if FE else 0
            rows_in = hs[:4]
            feats_in = hs[4:8]
            with ExitStack() as scope:
                def tmp(name, shape, dt=F32):
                    return scope.enter_context(nc.sbuf_tensor(f"{L.name}_{name}", shape, dt))

                s_rows = tmp("s_rows", [P, 4, 4 * P], BF16)
                d_rows = tmp("d_rows", [P, 4, 4 * P], BF16)
                hot_s = tmp("hot_s", [P, 2, 4 * P], BF16)
                hot_d = tmp("hot_d", [P, 2, 4 * P], BF16)
                hots, rows_sb = (hot_s, hot_d), (s_rows, d_rows)
                sel = tmp("sel", [P, 2, 4, NB * H])
                es = tmp("es", [P, 2, 4, H])
                ed = tmp("ed", [P, 2, 4, H])
                z = tmp("z", [P, 2, 4, H])
                apart = tmp("apart", [P, 2, 2, 4 * P], BF16)
                minus_col = tmp("minus_col", [P, 1])
                one_col = tmp("one_col", [P, 1])
                if FE:
                    feats = tmp("feats", [FEAT_ROWS, 4, 4 * P], BF16)
                    we_sb = tmp("we", [FEAT_ROWS, D])
                    we_part = tmp("we_part", [FEAT_ROWS, D], BF16)
                    we_tab = tmp("we_tab", [FEAT_ROWS, D], BF16)
                    enc = tmp("enc", [P, 2, 4 * D])
                    q = tmp("q", [P, 2, 4, H])
                ED0 = NB * H
                assert ED0 + 3 * M <= BANK // 2

                def looked_up(h):
                    return psum[:, 2 * h:2 * h + 2, :].rearrange("p b (t f) -> p (b t) f", t=2)

                def products(h):
                    return sel[:, h, :, :].rearrange("p t (n h) -> p t n h", h=H)

                def terms(h):
                    return enc[:, h, :].rearrange("p (t d) -> p t d", d=D // H)

                with nc.Block() as block:
                    @block.sync
                    def _(sp):
                        if FE:
                            sp.dma_start(we_sb[:, :], t["we"]).then_inc(hload.sem, 16)
                            sp.wait_ge(feats_set.sem, feats_set.at(1))

                        def turn(i, first):
                            for s in range(4):
                                k = 4 * i + s
                                at = k * (4 * P)
                                if not first:
                                    for made in hot_made:
                                        sp.wait_ge(made.sem, made.at(k - 3))
                                        stand_alone(sp, passed)
                                for rows, to in ((src_rows, s_rows), (dst_rows, d_rows)):
                                    sp.dma_start(to[:, s, :], rows[0:1, bass.ds(at, 4 * P)].broadcast_to([P, 4 * P]),
                                                 ).then_inc(rows_in[s].sem, 16)
                                if FE:
                                    if not first:
                                        sp.wait_ge(pair_found.sem, pair_found.at(2 * k - 6))
                                        stand_alone(sp, passed)
                                    for b in range(3):
                                        sp.dma_start(feats[32 * b:32 * b + 9, s, :], feat_rows[:, bass.ds(at, 4 * P)],
                                                     ).then_inc(feats_in[s].sem, 16)
                        over_double_turns(sp, turn)

                    @block.gpsimd
                    def _(pool):
                        if FE:
                            POOL.memset(feats[:, :, :], 1.0).then_inc(feats_set.sem, 1)
                        POOL.memset(logits[:, :, T:TP], 0.0)
                        POOL.memset(one_col[:, :], 1.0)
                        POOL.tensor_scalar(minus_col[:, :], iota_col[:, :], -1.0, None, ALU.mult).then_inc(columns_set.sem, 1)
                        def fold(view, times, k, done, folded):
                            n = view.shape[2]
                            for step in range(times):
                                ins = POOL.tensor_tensor(view[:, :, 0:n // 2], view[:, :, 0:n // 2], view[:, :, n - n // 2:n],
                                                         ALU.add)
                                n -= n // 2
                                if step < times - 1:
                                    ins.then_inc(folding.sem, 1)
                                    pool.wait_ge(folding.sem, folding.at(k * STEPS + done + step + 1))
                                    stand_alone(pool, passed)
                            ins.then_inc(folded.sem, 1)

                        def turn(i, first):
                            for h in range(2):
                                k = 2 * i + h
                                if es_folds:
                                    pool.wait_ge(selected.sem, selected.at(k + 1))
                                    stand_alone(pool, passed)
                                    fold(products(h), es_folds, k, 0, es_folded)
                                if q_folds:
                                    pool.wait_ge(multiplied.sem, multiplied.at(2 * k + 2))
                                    stand_alone(pool, passed)
                                    fold(terms(h), q_folds, k, max(0, es_folds - 1), q_folded)
                        STEPS = max(0, es_folds - 1) + max(0, q_folds - 1)
                        if es_folds or q_folds:
                            over_tiles(pool, turn)
                            folding.phase_ends(2 * TURNS * STEPS)

                    @block.vector
                    def _(dve):
                        if FE:
                            step = chain(dve, dve_done)
                            dve.wait_ge(hload.sem, hload.at(16))
                            for b in range(3):
                                step(V.tensor_copy(we_part[:, :], we_sb[:, :]))
                                step(V.tensor_copy(we_tab[32 * b:32 * b + 32, :], we_part[32 * b:32 * b + 32, :]))
                                step(V.tensor_tensor(we_sb[:, :], we_sb[:, :], we_part[:, :], ALU.subtract))
                            V.memset(q[:, :, :, :], 0.0).then_inc(split.sem, 1)
                            dve_done.phase_ends(step.count[0])

                        def ones_at(i, s, side):
                            if side in hots_by_act:
                                return
                            i, s = i + s // 4, s % 4
                            dve.wait_ge(rows_in[s].sem, rows_in[s].at(32 * (i + 1)))
                            V.tensor_scalar(hots[side][:, s % 2, :], rows_sb[side][:, s, :], iota_col[:, :], None, ALU.is_equal,
                                            ).then_inc(hot_made[side].sem, 1)

                        def sum_es(k, h):
                            ready = es_folded if es_folds else selected
                            dve.wait_ge(ready.sem, ready.at(k + 1))
                            n = folded_size(NB, es_folds)
                            V.reduce_sum(es[:, h, :, :],
                                         sel[:, h, :, :].rearrange("p t (n h) -> p t h n", h=H)[:, :, :, 0:n], AX,
                                         ).then_inc(summed.sem, 1)

                        def sum_q(k, h):
                            dve.wait_ge(q_folded.sem, q_folded.at(k + 1))
                            V.reduce_sum(q[:, h, :, :].rearrange("p t h -> p (t h)"),
                                         terms(h)[:, :, 0:folded_size(D // H, q_folds)], AX,
                                         ).then_inc(q_summed.sem, 1)

                        def add_es(k, h):
                            dve.wait_ge(summed.sem, summed.at(k + 1))
                            V.tensor_tensor(z[:, h, :, :], es[:, h, :, :], ed[:, h, :, :], ALU.add).then_inc(es_added.sem, 1)

                        def add_q(k, h):
                            dve.wait_ge(es_added.sem, es_added.at(k + 1))
                            dve.wait_ge(q_summed.sem, q_summed.at(k + 1))
                            V.tensor_tensor(z[:, h, :, :], z[:, h, :, :], q[:, h, :, :], ALU.add).then_inc(q_added.sem, 1)

                        def leaky(k, h, tile):
                            added = q_added if FE else es_added
                            dve.wait_ge(added.sem, added.at(k + 1))
                            V.scalar_tensor_tensor(logits[:, 0:H, bass.ds(tile, 4)].rearrange("p h t -> p t h"),
                                                   z[:, h, :, :], 0.2, z[:, h, :, :], ALU.mult, ALU.max)

                        def turn(i, first, last):
                            for s in range(4):
                                k, h = 4 * i + s, s % 2
                                tile = 4 * k
                                begun = not (first and s == 0)
                                dve.wait_ge(found.sem, found.at(k + 1))
                                V.tensor_tensor(sel[:, h, :, :].rearrange("p t (n h) -> p t n h", h=H),
                                                looked_up(h)[:, :, 0:ED0].rearrange("p t (n h) -> p t n h", h=H),
                                                src_hot[:, bass.ds(tile, 4), :].unsqueeze(3).broadcast_to([P, 4, NB, H]),
                                                ALU.mult).then_inc(selected.sem, 1)
                                parts = looked_up(h)[:, :, ED0:ED0 + 3 * M].rearrange("p t (c m) -> p t m c", c=3)
                                if L.loops:
                                    V.reduce_sum(logits[:, H:2 * H, bass.ds(tile, 4)].rearrange("p h t -> p t h"),
                                                 parts[:, :, H:2 * H, :], AX)
                                V.reduce_sum(ed[:, h, :, :], parts[:, :, 0:H, :], AX).then_inc(bank_read.sem, 1)
                                if begun and es_folds:
                                    sum_es(k - 1, 1 - h)
                                elif begun:
                                    add_es(k - 1, 1 - h)
                                if FE:
                                    for p in range(2):
                                        cut = slice(2 * p * D, (2 * p + 2) * D)
                                        dve.wait_ge(rectified.sem, rectified.at(2 * k + p + 1))
                                        V.tensor_tensor(enc[:, h, cut], enc[:, h, cut], psum[:, 4 + p, :], ALU.mult,
                                                        ).then_inc(multiplied.sem, 1)
                                        if begun and p == 0:
                                            sum_q(k - 1, 1 - h)
                                            if es_folds:
                                                add_es(k - 1, 1 - h)
                                    if begun:
                                        add_q(k - 1, 1 - h)
                                if not (last and s >= 2):
                                    ones_at(i, s + 2, 0)
                                    ones_at(i, s + 2, 1)
                                if not es_folds:
                                    sum_es(k, h)
                                elif begun and not FE:
                                    add_es(k - 1, 1 - h)
                                if begun:
                                    leaky(k - 1, 1 - h, tile - 4)
                        for h in range(2):
                            for side in range(2):
                                ones_at(0, h, side)
                        turn(0, True, False)
                        with dve.Fori(1, TURNS // 2 - 1) as i:
                            turn(i, False, False)
                        turn(TURNS // 2 - 1, False, True)
                        if es_folds:
                            sum_es(2 * TURNS - 1, 1)
                        add_es(2 * TURNS - 1, 1)
                        if FE:
                            sum_q(2 * TURNS - 1, 1)
                            add_q(2 * TURNS - 1, 1)
                        leaky(2 * TURNS - 1, 1, T - 4)

                    @block.tensor
                    def _(pe):
                        if FE:
                            pe.wait_ge(split.sem, split.at(1))

                        def turn(i, first):
                            _, blk = nc.values_load_multi_w_load_instructions(
                                block_of[0:1, bass.ds(i * (2 * U), 2 * U)], engines=[PE_ENGINE], min_val=0, max_val=NB - 1,
                                skip_runtime_bounds_check_because="blocks are counted on the chip, below NB")
                            for s in range(4):
                                k, h = 4 * i + s, s % 2
                                for made in hot_made:
                                    pe.wait_ge(made.sem, made.at(k + 1))
                                if not (first and s < 2):
                                    pe.wait_ge(bank_read.sem, bank_read.at(k - 1))
                                for j in range(4):
                                    cut = slice(j * P, (j + 1) * P)
                                    bank = psum[:, 2 * h + j // 2, :]
                                    at = (j % 2) * (BANK // 2)
                                    for part in range(3):
                                        PE.matmul(bank[:, at:at + NB * H], hot_s[:, h, cut], es_tab[:, part, :],
                                                  start=part == 0, stop=part == 2)
                                    at += ED0
                                    ins = PE.matmul(bank[:, at:at + 3 * M], hot_d[:, h, cut],
                                                    ed_tab[:, bass.ds(blk[4 * s + j], 1), :, :].rearrange("p o c m -> p (o c m)"),
                                                    start=True, stop=True)
                                ins.then_inc(found.sem, 1)
                                if not FE:
                                    continue
                                pe.wait_ge(feats_in[s].sem, feats_in[s].at(48 * (i + 1)))
                                for p in range(2):
                                    if not (first and s == 0):
                                        pe.wait_ge(multiplied.sem, multiplied.at(2 * k + p - 1))
                                    for j in (2 * p, 2 * p + 1):
                                        cut, to = slice(j * P, (j + 1) * P), slice((j % 2) * D, (j % 2 + 1) * D)
                                        for part in range(3):
                                            PE.matmul(psum[:, 4 + p, to], hot_d[:, h, cut],
                                                      row(node_parts, blk[4 * s + j])[:, part * D:(part + 1) * D],
                                                      start=part == 0, stop=part == 2)
                                        ins = PE.matmul(psum[:, 6 + p, to], feats[:, s, cut], we_tab[:, :],
                                                        start=True, stop=True)
                                    ins.then_inc(pair_found.sem, 1)
                        over_double_turns(pe, turn)

                    if hots_by_act:
                        @block.scalar
                        def _(act):
                            act.wait_ge(columns_set.sem, columns_set.at(1))
                            SIDES = len(hots_by_act)

                            def ones_at(i, s, first):
                                i, s = i + s // 4, s % 4
                                k, h = 4 * i + s, s % 2
                                act.wait_ge(rows_in[s].sem, rows_in[s].at(32 * (i + 1)))
                                for side in hots_by_act:
                                    if not first:
                                        act.wait_ge(hot_made[side].sem, hot_made[side].at(k - 1))
                                    A.activation(apart[:, side, h, :], rows_sb[side][:, s, :], ACT.Abs, bias=minus_col[:, :],
                                                 ).then_inc(differed.sem, 1)
                                for n, side in enumerate(hots_by_act):
                                    act.wait_ge(differed.sem, differed.at(k * SIDES + n + 1))
                                    A.activation(hots[side][:, h, :], apart[:, side, h, :], ACT.Relu, bias=one_col[:, :], scale=-1.0,
                                                 ).then_inc(hot_made[side].sem, 1)

                            def turn(i, first, last):
                                for s in range(4):
                                    k, h = 4 * i + s, s % 2
                                    if FE:
                                        if not (first and s < 2):
                                            act.wait_ge(q_summed.sem, q_summed.at(k - 1))
                                        for p in range(2):
                                            act.wait_ge(pair_found.sem, pair_found.at(2 * k + p + 1))
                                            A.activation(enc[:, h, 2 * p * D:(2 * p + 2) * D], psum[:, 6 + p, :], ACT.Relu,
                                                         ).then_inc(rectified.sem, 1)
                                    else:
                                        act.wait_ge(found.sem, found.at(k + 1))
                                    if not (last and s >= 2):
                                        ones_at(i, s + 2, False)
                            for h in range(2):
                                ones_at(0, h, True)
                            turn(0, True, False)
                            with act.Fori(1, TURNS // 2 - 1) as i:
                                turn(i, False, False)
                            turn(TURNS // 2 - 1, False, True)
                            differed.phase_ends(SIDES * 2 * TURNS)
            for sig in (*hot_made, found, bank_read, selected, summed, es_added):
                sig.phase_ends(2 * TURNS)
            columns_set.phase_ends(1)
            if es_folds:
                es_folded.phase_ends(2 * TURNS)
            if q_folds:
                q_folded.phase_ends(2 * TURNS)
            if FE:
                for sig in (pair_found, rectified, multiplied):
                    sig.phase_ends(4 * TURNS)
                for sig in (q_summed, q_added):
                    sig.phase_ends(2 * TURNS)
                for sig in feats_in:
                    sig.phase_ends(48 * TURNS // 2)
                hload.phase_ends(16)
                feats_set.phase_ends(1)
                split.phase_ends(1)
            for sig in rows_in:
                sig.phase_ends(32 * TURNS // 2)

        def softmax_phase(L):
            (turned, scanned, all_scanned, gathered, tiles_scanned, spread, spread_in, turned2, shifted, exped, wturned,
             stored, loops_exped) = signals(
                "softmax", "turned scanned all_scanned gathered tiles_scanned spread spread_in turned_again shifted exped "
                "turned_back stored loops_exped")
            H, LO = L.heads, L.loops
            with ExitStack() as scope:
                def tmp(name, shape, dt=F32):
                    return scope.enter_context(nc.sbuf_tensor(f"{L.name}_{name}", shape, dt))

                fwd = tmp("fwd", [P, TP])
                bwd = tmp("bwd", [P, TP])
                top = tmp("top", [P, H, TP])
                last_top = tmp("last_top", [P, CH, H])
                first_top = tmp("first_top", [P, CH, H])
                from_left = tmp("from_left", [H, TP + 1])
                from_right = tmp("from_right", [H, TP + 1])
                left_top = tmp("left_top", [P, CH, H])
                right_top = tmp("right_top", [P, CH, H])
                delta = tmp("delta", [P, 2, TP])
                delta_l = tmp("delta_l", [P, 2, TP]) if LO else None

                def turn_edges(pe_ap, bank):
                    for c in range(CH):
                        ins = PE.transpose(psum[:, bank, c * P:(c + 1) * P], pe_ap(c), ident[:, :])
                    return ins

                with nc.Block() as block:
                    @block.gpsimd
                    def _(pool):
                        POOL.memset(acc[:, :, 0:L.cols + HW], 0.0).then_inc(pool_done.sem, 1)

                    @block.tensor
                    def _(pe):
                        for h in range(H):
                            if h >= 2:
                                pe.wait_ge(scanned.sem, scanned.at(h - 1))
                            turn_edges(lambda c: logits[:, h, c * P:(c + 1) * P], h % 2).then_inc(turned.sem, 1)
                        pe.wait_ge(all_scanned.sem, all_scanned.at(1))
                        for k, part in enumerate((last_top, first_top)):
                            for c in range(CH):
                                ins = PE.transpose(psum[0:H, 2 + k, c * P:(c + 1) * P], part[:, c, :], ident[:, :])
                            ins.then_inc(gathered.sem, 1)
                        pe.wait_ge(tiles_scanned.sem, tiles_scanned.at(1))
                        for k, part in enumerate((from_left, from_right)):
                            for c in range(CH):
                                ins = PE.transpose(psum[:, 2 + k, c * H:(c + 1) * H], part[:, c * P + k:(c + 1) * P + k],
                                                   ident[0:H, 0:H])
                        ins.then_inc(spread.sem, 1)

                        def bring(h):
                            if h >= 2:
                                pe.wait_ge(shifted.sem, shifted.at(h - 1))
                            if h == 0:
                                pe.wait_ge(scanned.sem, scanned.at(H))
                            ins = turn_edges(lambda c: logits[:, h, c * P:(c + 1) * P], h % 2)
                            if LO:
                                if h == 0:
                                    pe.wait_ge(spread_in.sem, spread_in.at(1))
                                ins = turn_edges(lambda c: logits[:, H + h, c * P:(c + 1) * P], 2 + h % 2)
                            ins.then_inc(turned2.sem, 1)

                        def take(h):
                            pe.wait_ge(exped.sem, exped.at(h + 1))
                            if h >= 2:
                                pe.wait_ge(stored.sem, stored.at(h - 1))
                            ins = turn_edges(lambda c: delta[:, h % 2, c * P:(c + 1) * P], 4 + h % 2)
                            if LO:
                                ins = turn_edges(lambda c: delta_l[:, h % 2, c * P:(c + 1) * P], 6 + h % 2)
                            ins.then_inc(wturned.sem, 1)
                        bring(0)
                        for h in range(H):
                            if h + 1 < H:
                                bring(h + 1)
                            take(h)

                    @block.vector
                    def _(dve):
                        step = chain(dve, dve_done)
                        for h in range(H):
                            dve.wait_ge(turned.sem, turned.at(h + 1))
                            step(V.tensor_tensor_scan(fwd[:, :], left_pen[:, :], psum[:, h % 2, :], -BIG, ALU.add, ALU.max))
                            V.tensor_tensor_scan(bwd[:, ::-1], right_pen[:, ::-1], psum[:, h % 2, ::-1], -BIG, ALU.add, ALU.max,
                                                 ).then_inc(scanned.sem, 1)
                            dve.wait_ge(scanned.sem, scanned.at(h + 1))
                            step(V.tensor_tensor(top[:, h, :], fwd[:, :], bwd[:, :], ALU.max))
                            step(V.tensor_copy(last_top[:, :, h], fwd[:, P - 1:TP:P]))
                            step(V.tensor_copy(first_top[:, :, h], bwd[:, 0:TP:P]))
                        V.memset(from_left[:, 0:1], -BIG)
                        V.memset(from_right[:, TP:TP + 1], -BIG).then_inc(all_scanned.sem, 1)
                        dve.wait_ge(gathered.sem, gathered.at(2))
                        V.tensor_tensor_scan(from_left[:, 1:TP + 1], tile_left_pen[0:H, :], psum[0:H, 2, :], -BIG,
                                             ALU.add, ALU.max)
                        V.tensor_tensor_scan(from_right[:, TP - 1::-1], tile_right_pen[0:H, ::-1], psum[0:H, 3, ::-1], -BIG,
                                             ALU.add, ALU.max).then_inc(tiles_scanned.sem, 1)
                        dve.wait_ge(spread.sem, spread.at(1))
                        step(V.tensor_copy(left_top[:, :, :].rearrange("p c h -> p (c h)"), psum[:, 2, 0:CH * H]))
                        V.tensor_copy(right_top[:, :, :].rearrange("p c h -> p (c h)"), psum[:, 3, 0:CH * H],
                                      ).then_inc(spread_in.sem, 1)
                        dve.wait_ge(spread_in.sem, spread_in.at(1))
                        for h in range(H):
                            for c in range(CH):
                                cut = slice(c * P, (c + 1) * P)
                                ins = V.scalar_tensor_tensor(top[:, h, cut], left_in[:, cut], left_top[:, c, h:h + 1],
                                                             top[:, h, cut], ALU.add, ALU.max)
                            step(ins)
                            for c in range(CH):
                                cut = slice(c * P, (c + 1) * P)
                                ins = V.scalar_tensor_tensor(top[:, h, cut], right_in[:, cut], right_top[:, c, h:h + 1],
                                                             top[:, h, cut], ALU.add, ALU.max)
                            step(ins)
                            dve.wait_ge(turned2.sem, turned2.at(h + 1))
                            if LO:
                                step(V.tensor_tensor(top[:, h, :], top[:, h, :], psum[:, 2 + h % 2, :], ALU.max))
                            if h >= 2:
                                dve.wait_ge(wturned.sem, wturned.at(h - 1))
                            if LO:
                                V.tensor_tensor(delta_l[:, h % 2, :], psum[:, 2 + h % 2, :], top[:, h, :], ALU.subtract)
                            V.tensor_tensor(delta[:, h % 2, :], psum[:, h % 2, :], top[:, h, :], ALU.subtract,
                                            ).then_inc(shifted.sem, 1)
                            if LO:
                                dve.wait_ge(loops_exped.sem, loops_exped.at(h + 1))
                                V.scalar_tensor_tensor(delta_l[:, h % 2, :], delta_l[:, h % 2, :], -1.0, first[:, :],
                                                       ALU.add, ALU.mult).then_inc(exped.sem, 1)
                        dve_done.phase_ends(step.count[0])

                    @block.scalar
                    def _(act):
                        for h in range(H):
                            act.wait_ge(shifted.sem, shifted.at(h + 1))
                            ins = A.activation(delta[:, h % 2, :], delta[:, h % 2, :], ACT.Exp)
                            if LO:
                                A.activation(delta_l[:, h % 2, :], delta_l[:, h % 2, :], ACT.Exp).then_inc(loops_exped.sem, 1)
                            else:
                                ins.then_inc(exped.sem, 1)
                            act.wait_ge(wturned.sem, wturned.at(h + 1))
                            ins = A.copy(weights[:, :, h], psum[:, 4 + h % 2, 0:T])
                            if LO:
                                ins = A.copy(weights[:, :, H + h], psum[:, 6 + h % 2, 0:T])
                            ins.then_inc(stored.sem, 1)
            for sig in (turned, scanned, turned2, shifted, exped, wturned, stored):
                sig.phase_ends(H)
            if LO:
                loops_exped.phase_ends(H)
            for sig, n in ((pool_done, 1), (all_scanned, 1), (gathered, 2), (tiles_scanned, 1), (spread, 1), (spread_in, 1)):
                sig.phase_ends(n)

        def gather_phase(L):
            (staged, ready, summed, ran, kept, weighted, minus_set, differed, hot_made) = signals(
                "gather", "index_staged ready summed ran_on kept weighted minus_set differed hot_made")
            H, C, M = L.heads, L.cols, L.wcols
            R = C + M
            share = C > D
            with ExitStack() as scope:
                def tmp(name, shape, dt=F32):
                    return scope.enter_context(nc.sbuf_tensor(f"{L.name}_{name}", shape, dt))

                index = tmp("index", [P, 2, 4], U32)
                got = tmp("got", [P, U, R])
                hot = tmp("hot", [P, 4, P])
                running = tmp("running", [P, 4, R])
                if share:
                    minus_dst = tmp("minus_dst", [P, T])
                    one_col = tmp("gather_one_col", [P, 1])
                    apart = tmp("gather_apart", [P, 4, P])

                def sums_of(s):
                    return psum[:, 2 * s:2 * s + 2, :].rearrange("p b f -> p (b f)")

                with nc.Block() as block:
                    @block.gpsimd
                    def _(pool):
                        def turn(i, first):
                            for h in range(2):
                                pool.wait_ge(staged.sem, staged.at(2 * i + h + 1))
                                stand_alone(pool, passed)
                                for j in range(4):
                                    tile = i * U + 4 * h + j
                                    if not first:
                                        pool.wait_ge(summed.sem, summed.at(tile - U + 1))
                                        stand_alone(pool, passed)
                                    pool.indirect_dma_start(
                                        got[:, 4 * h + j, 0:C], None, table[C],
                                        bass.IndirectOffsetOnAxis(ap=index[:, h, j:j + 1], axis=0),
                                    ).then_inc(ds[4 * h + j].sem, 16)
                        over_tiles(pool, turn)

                    @block.scalar
                    def _(act):
                        for h in range(2):
                            A.copy(index[:, h, :], src_u[:, 4 * h:4 * h + 4]).then_inc(staged.sem, 1)
                        A.copy(got[:, 0:4, C:R], weights[:, 0:4, 0:M]).then_inc(weighted.sem, 1)

                        def differ(tile, s):
                            if not (isinstance(tile, int) and tile < 4):
                                act.wait_ge(hot_made.sem, hot_made.at(tile - 3))
                            A.activation(apart[:, s, :], iota_row[:, :], ACT.Abs, bias=minus_dst[:, bass.ds(tile, 1)],
                                         ).then_inc(differed.sem, 1)

                        def make_hot(tile, s):
                            if not (isinstance(tile, int) and tile < 4):
                                act.wait_ge(summed.sem, summed.at(tile - 3))
                            act.wait_ge(differed.sem, differed.at(tile + 1))
                            A.activation(hot[:, s, :], apart[:, s, :], ACT.Relu, bias=one_col[:, :], scale=-1.0,
                                         ).then_inc(hot_made.sem, 1)

                        if share:
                            act.wait_ge(minus_set.sem, minus_set.at(1))
                            for tile in range(3):
                                differ(tile, tile)
                            for tile in range(2):
                                make_hot(tile, tile)

                        def turn(i, first, last=False):
                            _, blk = nc.values_load_multi_w_load_instructions(
                                block_of[0:1, bass.ds(i * U, U)], engines=[ACT_ENGINE], min_val=0, max_val=NB - 1,
                                skip_runtime_bounds_check_because="blocks are counted on the chip, below NB")
                            for h in range(2):
                                if not last:
                                    for j in range(4):
                                        act.wait_ge(ds[4 * h + j].sem, ds[4 * h + j].at(16 * (i + 1)))
                                    A.copy(index[:, h, :], src_u[:, bass.ds((i + 1) * U + 4 * h, 4)]).then_inc(staged.sem, 1)
                                if not (last and h == 1):
                                    if not (first and h == 0):
                                        act.wait_ge(summed.sem, summed.at(i * U + 4 * h))
                                    A.copy(got[:, 4 - 4 * h:8 - 4 * h, C:R],
                                           weights[:, bass.ds(i * U + 4 * h + 4, 4), 0:M]).then_inc(weighted.sem, 1)
                                for j in range(4):
                                    ahead = 4 * h + j + 2
                                    if share and not (last and ahead >= U):
                                        make_hot(i * U + ahead, ahead % 4)
                                    act.wait_ge(ran.sem, ran.at(i * U + 4 * h + j + 1))
                                    if not (first and h == 0 and j == 0):
                                        act.wait_ge(kept.sem, kept.at(i * U + 4 * h + j))
                                    A.copy(row(acc, blk[4 * h + j])[:, 0:R], running[:, j, :]).then_inc(kept.sem, 1)
                                    if share and not (last and ahead + 1 >= U):
                                        differ(i * U + ahead + 1, (ahead + 1) % 4)
                        turn(0, True)
                        with act.Fori(1, TURNS - 1) as i:
                            turn(i, False)
                        turn(TURNS - 1, False, last=True)

                    @block.vector
                    def _(dve):
                        if share:
                            V.memset(one_col[:, :], 1.0)
                            V.tensor_scalar(minus_dst[:, :], dst_in[:, 0:T], -1.0, None, ALU.mult).then_inc(minus_set.sem, 1)
                        V.memset(running[:, 3, :], 0.0).then_inc(pool_done.sem, 1)
                        dve.wait_ge(pool_done.sem, pool_done.at(1))

                        def run_on(tile, s, first):
                            dve.wait_ge(summed.sem, summed.at(tile + 1))
                            if not first:
                                dve.wait_ge(ran.sem, ran.at(tile))
                                dve.wait_ge(kept.sem, kept.at(tile - 3))
                            V.scalar_tensor_tensor(running[:, s, :], running[:, (s + 3) % 4, :], keep[:, bass.ds(tile, 1)],
                                                   sums_of(s)[:, 0:R], ALU.mult, ALU.add).then_inc(ran.sem, 1)

                        def turn(i, first):
                            for j in range(U):
                                tile = i * U + j
                                s = j % 4
                                dve.wait_ge(ds[j].sem, ds[j].at(16 * (i + 1)))
                                view = got[:, j, 0:C].rearrange("p (h d) -> p h d", h=H)
                                ins = V.tensor_tensor(view, view, weights[:, bass.ds(tile, 1), 0:H].rearrange(
                                    "p o h -> p (o h)").unsqueeze(2).broadcast_to([P, H, C // H]), ALU.mult)
                                if not share:
                                    if not (first and j < 4):
                                        dve.wait_ge(summed.sem, summed.at(tile - 3))
                                    ins = V.tensor_scalar(hot[:, s, :], iota_row[:, :], dst_in[:, bass.ds(tile, 1)], None,
                                                          ALU.is_equal)
                                ins.then_inc(ready.sem, 1)
                                if first and j < 2:
                                    continue
                                if first and j < 6:
                                    if j > 2:
                                        dve.wait_ge(ran.sem, ran.at(tile - 2))
                                    run_on(tile - 2, (s + 2) % 4, True)
                                else:
                                    run_on(tile - 2, (s + 2) % 4, False)
                        over_tiles(dve, turn)
                        run_on(T - 2, 2, False)
                        run_on(T - 1, 3, False)

                    @block.tensor
                    def _(pe):
                        def turn(i, first):
                            for j in range(U):
                                tile = i * U + j
                                s = j % 4
                                if j % 4 == 0:
                                    pe.wait_ge(weighted.sem, weighted.at(2 * i + j // 4 + 1))
                                    stand_alone(pe, passed)
                                pe.wait_ge(ready.sem, ready.at(tile + 1))
                                if share:
                                    pe.wait_ge(hot_made.sem, hot_made.at(tile + 1))
                                if not (first and j < 4):
                                    pe.wait_ge(ran.sem, ran.at(tile - 3))
                                for c in range(0, R, BANK):
                                    cut = slice(c, min(c + BANK, R))
                                    ins = PE.matmul(sums_of(s)[:, cut], hot[:, s, :], got[:, j, cut], start=True, stop=True)
                                ins.then_inc(summed.sem, 1)
                        over_tiles(pe, turn)
            for sig in (ready, summed, ran, kept):
                sig.phase_ends(T)
            staged.phase_ends(2 * TURNS)
            weighted.phase_ends(2 * TURNS)
            if share:
                minus_set.phase_ends(1)
                for sig in (differed, hot_made):
                    sig.phase_ends(T)
            pool_done.phase_ends(1)
            for sig in ds:
                sig.phase_ends(16 * TURNS)

        def loop_layer_nodes(L, residual):
            (own_ready, own_added) = signals("loops", "own_ready own_added")
            H = L.heads
            with ExitStack() as scope:
                def tmp(name, shape, dt=F32):
                    return scope.enter_context(nc.sbuf_tensor(f"{L.name}_{name}", shape, dt))

                b_sb = tmp("b", [P, D])
                inv = tmp("inv", [P, NB, H])
                own = tmp("own_w", [P, NB, H])
                bn = tmp("bn", [P, G, 6])
                mv = tmp("mv", [P, G, 2])

                def heads(ap, g):
                    return group(ap, g)[:, :, 0:D].rearrange("p g (h d) -> p g h d", h=H)

                def wide(ap, g):
                    return group(ap, g).unsqueeze(3).broadcast_to([P, G, H, D // H])

                with nc.Block() as block:
                    @block.sync
                    def _(sp):
                        sp.dma_start(b_sb[:, :], t[L.b].broadcast_to([P, D])).then_inc(hload.sem, 16)

                    @block.gpsimd
                    def _(pool):
                        pool.wait_ge(hload.sem, hload.at(16))
                        pool.wait_ge(own_ready.sem, own_ready.at(1))
                        with pool.Fori(0, NB // G) as g:
                            POOL.tensor_tensor(heads(node_rows, g), heads(node_rows, g), wide(own, g), ALU.mult,
                                               ).then_inc(pool_done.sem, 1)
                            pool.wait_ge(pool_done.sem, pool_done.at(g + 1))
                            stand_alone(pool, passed)
                            POOL.tensor_tensor(group(node_rows, g), group(node_rows, g),
                                               b_sb[:, :].unsqueeze(1).broadcast_to([P, G, D]), ALU.add,
                                               ).then_inc(own_added.sem, 1)

                    @block.vector
                    def _(dve):
                        step = chain(dve, dve_done)
                        step(V.scalar_tensor_tensor(own[:, :, :], acc[:, :, D + H:D + 2 * H], 1.0,
                                                    loop_mask[:, :].unsqueeze(2).broadcast_to([P, NB, H]), ALU.add, ALU.mult))
                        step(V.tensor_tensor(inv[:, :, :], own[:, :, :], acc[:, :, D:D + H], ALU.add))
                        step(V.tensor_scalar_max(inv[:, :, :], inv[:, :, :], 1e-30))
                        step(V.reciprocal(inv[:, :, :], inv[:, :, :]))
                        V.tensor_tensor(own[:, :, :], own[:, :, :], inv[:, :, :], ALU.mult).then_inc(own_ready.sem, 1)
                        dve_done.phase_ends(4)
                        step = Steps(dve, dve_done, 6 if residual else 5)
                        with dve.Fori(0, NB // G) as g:
                            step.turn(g)
                            step(V.tensor_tensor(heads(acc, g), heads(acc, g), wide(inv, g), ALU.mult))
                            dve.wait_ge(own_added.sem, own_added.at(g + 1))
                            step(V.tensor_tensor(group(node_rows, g), group(node_rows, g), group(acc, g)[:, :, 0:D], ALU.add),
                                 apart=passed)
                            rows = node_rows
                            if residual:
                                rows = x
                                step(V.tensor_tensor(group(x, g), group(x, g), group(node_rows, g), ALU.add), apart=passed)
                            group_stats(step, rows, g, bn, mv)
                        dve_done.phase_ends(step.per * (NB // G))
            for sig, n in ((hload, 16), (own_ready, 1), (own_added, NB // G), (pool_done, NB // G)):
                sig.phase_ends(n)

        def out_project_nodes(L):
            (scaled, turned, copied, produced, exped, taken) = signals(
                "out", "scaled turned copied produced exped taken")
            H, C, KO = L.heads, L.cols, L.cols // P
            with ExitStack() as scope:
                def tmp(name, shape, dt=F32):
                    return scope.enter_context(nc.sbuf_tensor(f"{L.name}_{name}", shape, dt))

                w_sb = tmp("wo", [P, KO, D])
                b_sb = tmp("bo", [1, D])
                inv = tmp("inv", [P, NB, H])
                m_sb = tmp("m_sb", [P, 2, C])
                m_t = tmp("m_t", [P, 2, C])
                neg = tmp("neg", [P, 2, D])
                bn = tmp("bn", [P, 6])
                mv = tmp("mv", [P, 2])
                with nc.Block() as block:
                    @block.sync
                    def _(sp):
                        sp.dma_start(w_sb[:, :, :], t["wo"].rearrange("(k p) o -> p k o", p=P)).then_inc(hload.sem, 16)
                        sp.dma_start(b_sb[:, :], t["bo"]).then_inc(hload.sem, 16)

                    @block.vector
                    def _(dve):
                        step = chain(dve, dve_done)
                        step(V.tensor_scalar_add(inv[:, :, :], acc[:, :, C:C + H], 1e-16))
                        step(V.reciprocal(inv[:, :, :], inv[:, :, :]))
                        dve_done.phase_ends(2)
                        step = Steps(dve, dve_done, 4)

                        def early(n, s, first):
                            if not first:
                                dve.wait_ge(turned.sem, turned.at(n - 1))
                            V.tensor_tensor(m_sb[:, s, :].rearrange("p (h d) -> p h d", h=H),
                                            row(acc, n)[:, 0:C].rearrange("p (h d) -> p h d", h=H),
                                            row(inv, n).unsqueeze(2).broadcast_to([P, H, C // H]), ALU.mult,
                                            ).then_inc(scaled.sem, 1)

                        def clip(n, s, first):
                            xn = row(x, n)
                            z = psum[:, 2 + s, 0:D]
                            dve.wait_ge(produced.sem, produced.at(n + 1))
                            V.tensor_scalar_min(neg[:, s, :], z, 0.0)
                            V.scalar_tensor_tensor(xn, z, 0.0, xn, ALU.max, ALU.add).then_inc(taken.sem, 1)

                        def add_exp(n, s):
                            step.turn(n)
                            xn = row(x, n)
                            dve.wait_ge(exped.sem, exped.at(n + 1))
                            dve.wait_ge(taken.sem, taken.at(n + 1))
                            step(V.scalar_tensor_tensor(xn, neg[:, s, :], -1.0, xn, ALU.add, ALU.add), apart=passed)
                            row_stats(dve, step, xn, n, bn, mv)

                        def late(n, s, first):
                            clip(n, s, first)
                            if not (first and s == 0):
                                add_exp(n - 1, 1 - s)
                        over_blocks_two_ahead(dve, early, late)
                        add_exp(NB - 1, 0)
                        dve_done.phase_ends(step.per * NB)

                    @block.tensor
                    def _(pe):
                        pe.wait_ge(hload.sem, hload.at(32))

                        def turn_over(n, s, first):
                            pe.wait_ge(scaled.sem, scaled.at(n + 1))
                            if not first:
                                pe.wait_ge(copied.sem, copied.at(n - 1))
                            for c in range(KO):
                                ins = PE.transpose(psum[:, s, c * P:(c + 1) * P], m_sb[:, s, c * P:(c + 1) * P], ident[:, :])
                            ins.then_inc(turned.sem, 1)

                        def product(n, s, first):
                            pe.wait_ge(copied.sem, copied.at(n + 1))
                            if not first:
                                pe.wait_ge(taken.sem, taken.at(n - 1))
                            for c in range(KO):
                                PE.matmul(psum[:, 2 + s, 0:D], m_t[:, s, c * P:(c + 1) * P], w_sb[:, c, :], start=c == 0, stop=False)
                            PE.matmul(psum[:, 2 + s, 0:D], ones_row[:, :], b_sb[:, :], start=False, stop=True,
                                      ).then_inc(produced.sem, 1)
                        over_blocks_ahead(pe, turn_over, product)

                    @block.scalar
                    def _(act):
                        def copy_in(n, s, first):
                            act.wait_ge(turned.sem, turned.at(n + 1))
                            if not first:
                                act.wait_ge(produced.sem, produced.at(n - 1))
                            A.copy(m_t[:, s, :], psum[:, s, 0:C]).then_inc(copied.sem, 1)

                        def exp_of(n, s, first):
                            act.wait_ge(taken.sem, taken.at(n + 1))
                            A.activation(neg[:, s, :], neg[:, s, :], ACT.Exp).then_inc(exped.sem, 1)

                        over_blocks_ahead(act, copy_in, exp_of)
            for sig in (scaled, turned, copied, produced, exped, taken):
                sig.phase_ends(NB)
            hload.phase_ends(32)

        def last_layer_nodes(L):
            (stats_in, rooted, normed, biased) = signals("last", "varied rooted normed biased")
            H = L.heads
            with ExitStack() as scope:
                def tmp(name, shape, dt=F32):
                    return scope.enter_context(nc.sbuf_tensor(f"{L.name}_{name}", shape, dt))

                b_sb = tmp("b", [P, D])
                inv = tmp("inv", [P, NB, H])
                bn = tmp("bn", [P, G, 6])
                mv = tmp("mv", [P, G, 2])
                with nc.Block() as block:
                    @block.sync
                    def _(sp):
                        sp.dma_start(b_sb[:, :], t[L.b].broadcast_to([P, D])).then_inc(hload.sem, 16)
                        with sp.Fori(0, NB // G - 1) as g:
                            sp.wait_ge(normed.sem, normed.at(g + 1))
                            sp.dma_start(out[bass.ds(g * (G * P), G * P), :].rearrange("(n p) d -> p n d", p=P), group(x, g),
                                         ).then_inc(hstore.sem, 16)
                        sp.wait_ge(normed.sem, normed.at(NB // G))
                        sp.dma_start(out[(NB - G) * P:(NB - 1) * P, :].rearrange("(n p) d -> p n d", p=P), x[:, NB - G:NB - 1, :],
                                     ).then_inc(hstore.sem, 16)
                        sp.dma_start(out[(NB - 1) * P:N_NODES, :], x[0:LAST, NB - 1, :]).then_inc(hstore.sem, 16)
                        sp.wait_ge(hstore.sem, hstore.at(16 * (NB // G + 1)))

                    @block.gpsimd
                    def _(pool):
                        pool.wait_ge(hload.sem, hload.at(16))
                        with pool.Fori(0, NB // G) as g:
                            POOL.tensor_tensor(group(x, g), group(x, g), b_sb[:, :].unsqueeze(1).broadcast_to([P, G, D]), ALU.add,
                                               ).then_inc(biased.sem, 1)

                    @block.vector
                    def _(dve):
                        step = chain(dve, dve_done)
                        step(V.tensor_scalar_max(inv[:, :, :], acc[:, :, D:D + H], 1e-10))
                        step(V.reciprocal(inv[:, :, :], inv[:, :, :]))
                        dve_done.phase_ends(2)
                        step = Steps(dve, dve_done, 5)
                        with dve.Fori(0, NB // G) as g:
                            step.turn(g)
                            sums_g = group(acc, g)[:, :, 0:D].rearrange("p g (h d) -> p g h d", h=H)
                            step(V.tensor_tensor(sums_g, sums_g, group(inv, g).unsqueeze(3).broadcast_to([P, G, H, D // H]),
                                                 ALU.mult))
                            dve.wait_ge(biased.sem, biased.at(g + 1))
                            step(V.tensor_tensor(group(x, g), group(x, g), group(acc, g)[:, :, 0:D], ALU.add), apart=passed)
                            group_stats(step, x, g, bn, mv)
                        dve_done.phase_ends(step.per * (NB // G))
                        V.tensor_scalar_add(rstd[:, :], stats[:, :, 1], EPS).then_inc(stats_in.sem, 1)
                        dve.wait_ge(rooted.sem, rooted.at(1))
                        step = chain(dve, dve_done)
                        refine_root(step)
                        dve_done.phase_ends(5)
                        with dve.Fori(0, NB // G) as g:
                            for b in range(G):
                                n = g * G + b
                                ins = V.tensor_scalar(row(x, n), row(x, n), stats[:, bass.ds(n, 1), 0], rstd[:, bass.ds(n, 1)],
                                                      ALU.subtract, ALU.mult)
                            ins.then_inc(normed.sem, 1)

                    @block.scalar
                    def _(act):
                        act.wait_ge(stats_in.sem, stats_in.at(1))
                        A.activation(rstd[:, :], rstd[:, :], ACT.Sqrt).then_inc(rooted.sem, 1)
            for sig, n in ((hload, 16), (hstore, 16 * (NB // G + 1)), (stats_in, 1), (rooted, 1), (normed, NB // G),
                           (biased, NB // G)):
                sig.phase_ends(n)

        def attention_layer(L, rows_of, affine):
            with ExitStack() as scope:
                es_tab = scope.enter_context(nc.sbuf_tensor(f"{L.name}_es_tab", [P, 3, NB * L.heads], BF16))
                ed_tab = scope.enter_context(nc.sbuf_tensor(f"{L.name}_ed_tab", [P, NB, 3, L.wcols], BF16))
                project(L, rows_of, affine, es_tab, ed_tab)
                logit_phase(L, es_tab, ed_tab)
                softmax_phase(L)
                gather_phase(L)

        gat_a = Layer("gat_a", 4, D, loops=True, w="w1", a=("a1s", "a1d"), b="b1")
        gat_b = Layer("gat_b", 1, D, loops=True, w="w2", a=("a2s", "a2d"), b="b2")
        gat_8 = Layer("gat_8", 8, 2 * D, w="w3", a=("a3s", "a3d"))
        gat_e = Layer("gat_e", 8, D, edge_feats=True, w="w4", a=("a4s", "a4d"), b="b4")

        order_phase()
        edge_phase()
        scatter_phase()
        first_layer_nodes()
        attention_layer(gat_a, lambda n: row(x, n), False)
        loop_layer_nodes(gat_a, residual=False)
        attention_layer(gat_b, lambda n: row(node_rows, n), True)
        loop_layer_nodes(gat_b, residual=True)
        attention_layer(gat_8, lambda n: row(x, n), False)
        out_project_nodes(gat_8)
        attention_layer(gat_e, lambda n: row(x, n), False)
        last_layer_nodes(gat_e)


_OUT = "out_dram"


def _layout(i):
    def a(n):
        return np.asarray(i[n])

    def row(n):
        return np.ascontiguousarray(a(n).reshape(1, -1))

    pad = ROWS - N_EDGES
    ids = np.stack([np.pad(a("src"), (0, pad)), np.pad(a("dst"), (0, pad), constant_values=NO_NODE)], axis=1)
    vals = np.concatenate([np.pad(a("edge_weight"), (0, pad))[:, None], np.pad(a("edge_attr_3"), ((0, pad), (0, 0)))], axis=1)
    H3 = a("L2_gnn_a").shape[1] // 2
    chunk = np.concatenate([a("L3_gnn_edge_W").T] * 3 + [row("L3_gnn_edge_b"), np.zeros((FEAT_ROWS // 3 - 10, D), np.float32)])
    we = np.ascontiguousarray(np.concatenate([chunk] * 3))
    return {
        "x": a("x"),
        "edge_ids": np.ascontiguousarray(ids),
        "edge_vals": np.ascontiguousarray(vals),
        "dst_list": np.pad(a("dst"), (0, pad), constant_values=NO_NODE).reshape(1, ROWS),
        "w0": np.ascontiguousarray(a("L0_gnn_W").T), "b0": row("L0_gnn_b"),
        "w1": a("L1_gnn_W1"), "a1s": row("L1_gnn_a1_src"), "a1d": row("L1_gnn_a1_dst"), "b1": row("L1_gnn_b1"),
        "ln_g": row("L1_gnn_ln_g"), "ln_b": row("L1_gnn_ln_b"),
        "w2": a("L1_gnn_W2"), "a2s": row("L1_gnn_a2_src"), "a2d": row("L1_gnn_a2_dst"), "b2": row("L1_gnn_b2"),
        "w3": np.ascontiguousarray(a("L2_gnn_W").transpose(1, 0, 2).reshape(D, -1)),
        "a3s": np.ascontiguousarray(a("L2_gnn_a")[:, :H3].reshape(1, -1)),
        "a3d": np.ascontiguousarray(a("L2_gnn_a")[:, H3:].reshape(1, -1)),
        "wo": a("L2_gnn_Wo"), "bo": row("L2_gnn_bo"),
        "w4": np.ascontiguousarray(a("L3_gnn_W").T), "a4s": row("L3_gnn_a_src"), "a4d": row("L3_gnn_a_dst"),
        "we": we, "b4": row("L3_gnn_bias"),
    }


def kernel(**inputs):
    import concourse.bacc as bacc
    from concourse.bass_utils import run_bass_kernel_spmd

    nc = bacc.Bacc("TRN2", target_bir_lowering=False, num_devices=1)
    arrays = _layout(inputs)
    given = {n: nc.dram_tensor(f"in_{n}", a.shape, mybir.dt.from_np(a.dtype), kind="ExternalInput").ap()
             for n, a in arrays.items()}
    out = nc.dram_tensor(_OUT, (N_NODES, D), F32, kind="ExternalOutput").ap()
    gnn_kernel(nc, given, out)
    r = run_bass_kernel_spmd(nc, [{f"in_{n}": a for n, a in arrays.items()}], core_ids=[0])
    return r.results[0][_OUT]
```
